# Optimizing a Trainium2 kernel written in Bass

```python
import numpy as np
import jax
import jax.numpy as jnp

def _softmax(x, axis=-1):
    return jax.nn.softmax(x, axis=axis)

def _gelu(x):
    return jax.nn.gelu(x, approximate=True)

def _silu(x):
    return jax.nn.silu(x)

def _sigmoid(x):
    return jax.nn.sigmoid(x)

def _layernorm(x, axis=-1, eps=1e-05):
    m = jnp.mean(x, axis=axis, keepdims=True)
    v = jnp.var(x, axis=axis, keepdims=True)
    return (x - m) / jnp.sqrt(v + eps)

def _scatter_add(tgt, idx, src, axis=0):
    return tgt.at[idx].add(src)

def _segment_sum(src, seg, n):
    return jax.ops.segment_sum(src, seg, n)
kernel_name = 'mk_xattn_seq_d2_seqx_r8_196708'

def setup_inputs(seed: int=0):
    np.random.seed(seed)
    _w = jnp.asarray

    def _rec_inputs():
        import jax
        import jax.numpy as jnp
        _rk = jax.random.key(seed)
        x = -0.0003929 + 0.9999 * jax.random.normal(jax.random.fold_in(_rk, 1), (8, 128, 256), jnp.float32)
        _lenS = 128 - jax.random.randint(jax.random.fold_in(_rk, 7), (8,), 0, max(1, 128 // 4) + 1, jnp.int32)
        _lenS2 = 128 - jax.random.randint(jax.random.fold_in(_rk, 8), (8,), 0, max(1, 128 // 4) + 1, jnp.int32)
        _ctx_2048P = jax.random.normal(jax.random.fold_in(_rk, 11), (8, 16, 256), jnp.float32)
        _ctx_2048c = jax.random.dirichlet(jax.random.fold_in(_rk, 511), 0.3 * jnp.ones((16,), jnp.float32), (8, 128))
        _ctx_2048t = jnp.einsum('bsk,bkd->bsd', _ctx_2048c, _ctx_2048P)
        _ctx_2048t = _ctx_2048t * jax.lax.rsqrt(jnp.mean(jnp.square(_ctx_2048t)) + 1e-12) * 0.953939
        ctx_2048 = 2.81802e-05 + 1.00001 * (_ctx_2048t + 0.3 * jax.random.normal(jax.random.fold_in(_rk, 611), (8, 128, 256), jnp.float32))
        return (x, ctx_2048)
    x, ctx_2048 = _rec_inputs()

    def _L0_xattn_setup():
        import jax, jax.numpy as jnp
        import numpy as np
        B, C1, C2, N = (8, 128, 128, 256)
        D = C2 // 8
        key = jax.random.key(seed)
        ks = jax.random.split(key, 8)
        s1 = 1.0 / np.sqrt(C1)
        s2 = 1.0 / np.sqrt(C2)
        return {'x1': jax.random.normal(ks[0], (B, C1, N), jnp.float32), 'x2': jax.random.normal(ks[1], (B, C2, N), jnp.float32), 'Wq': jax.random.uniform(ks[2], (D, C1), jnp.float32, -s1, s1), 'bq': jax.random.uniform(ks[3], (D,), jnp.float32, -s1, s1), 'Wk': jax.random.uniform(ks[4], (D, C2), jnp.float32, -s2, s2), 'bk': jax.random.uniform(ks[5], (D,), jnp.float32, -s2, s2), 'Wv': jax.random.uniform(ks[6], (C1, C2), jnp.float32, -s2, s2), 'bv': jax.random.uniform(ks[7], (C1,), jnp.float32, -s2, s2)}
    _L0_xattn_all = _L0_xattn_setup()
    _L0_xattn_in = {k: v for k, v in _L0_xattn_all.items() if k in ('Wq', 'bq', 'Wk', 'bk', 'Wv', 'bv')}
    del _L0_xattn_all

    def _L1_xattn_setup():
        import jax, jax.numpy as jnp
        import numpy as np
        B, L, E, H = (4, 64, 256, 32)
        S = E // H
        EXTRA_MAA, EXTRA_DECAY = (32, 64)
        EPS = 1e-05

        def _ln(x, w, b):
            m = jnp.mean(x, axis=-1, keepdims=True)
            v = jnp.mean((x - m) ** 2, axis=-1, keepdims=True)
            return (x - m) * jax.lax.rsqrt(v + EPS) * w + b

        def _token_shift(xn, prev_row):
            first = (prev_row - xn[:, 0])[:, None]
            rest = xn[:, :-1] - xn[:, 1:]
            return jnp.concatenate([first, rest], axis=1)
        key = jax.random.key(seed)
        ks = jax.random.split(key, 24)
        rn = lambda k, shp, s=1.0: jax.random.normal(k, shp, dtype=jnp.float32) * s
        return dict(x=rn(ks[0], (B, L, E)), state=rn(ks[1], (B, 2 + S, E), 0.1), ln1_w=jnp.ones((E,), jnp.float32), ln1_b=jnp.zeros((E,), jnp.float32), ln2_w=jnp.ones((E,), jnp.float32), ln2_b=jnp.zeros((E,), jnp.float32), maa_x=rn(ks[2], (E,), 0.02), maa_w1=rn(ks[3], (E, 5 * EXTRA_MAA), 0.02), maa_w2=rn(ks[4], (5, EXTRA_MAA, E), 0.02), maa_stack=rn(ks[5], (5, E), 0.02), time_decay=rn(ks[6], (E,), 0.5), decay_w1=rn(ks[7], (E, EXTRA_DECAY), 0.02), decay_w2=rn(ks[8], (EXTRA_DECAY, E), 0.02), faaaa=rn(ks[9], (H, S), 0.1), Wr=rn(ks[10], (E, E), 0.02), Wk=rn(ks[11], (E, E), 0.02), Wv=rn(ks[12], (E, E), 0.02), Wg=rn(ks[13], (E, E), 0.02), Wo=rn(ks[14], (E, E), 0.02), gn_w=jnp.ones((E,), jnp.float32), gn_b=jnp.zeros((E,), jnp.float32), ffn_maa_k=rn(ks[15], (E,), 0.02), ffn_maa_r=rn(ks[16], (E,), 0.02), ffn_Wk=rn(ks[17], (E, E), 0.02), ffn_Wr=rn(ks[18], (E, E), 0.02), ffn_Wv=rn(ks[19], (E, E), 0.02), i=0)
    _L1_xattn_all = _L1_xattn_setup()
    _L1_xattn_in = {k: v for k, v in _L1_xattn_all.items() if k in ('ln1_w', 'ln1_b', 'ln2_w', 'ln2_b', 'maa_x', 'maa_w1', 'maa_w2', 'maa_stack', 'time_decay', 'decay_w1', 'decay_w2', 'faaaa', 'Wr', 'Wk', 'Wv', 'Wg', 'Wo', 'gn_w', 'gn_b', 'ffn_maa_k', 'ffn_maa_r', 'ffn_Wk', 'ffn_Wr', 'ffn_Wv')}
    del _L1_xattn_all
    return {'x': x, 'ctx_2048': ctx_2048, 'L0_xattn_Wq': _L0_xattn_in['Wq'], 'L0_xattn_bq': _L0_xattn_in['bq'], 'L0_xattn_Wk': _L0_xattn_in['Wk'], 'L0_xattn_bk': _L0_xattn_in['bk'], 'L0_xattn_Wv': _L0_xattn_in['Wv'], 'L0_xattn_bv': _L0_xattn_in['bv'], 'L1_xattn_ln1_w': _L1_xattn_in['ln1_w'], 'L1_xattn_ln1_b': _L1_xattn_in['ln1_b'], 'L1_xattn_ln2_w': _L1_xattn_in['ln2_w'], 'L1_xattn_ln2_b': _L1_xattn_in['ln2_b'], 'L1_xattn_maa_x': _L1_xattn_in['maa_x'], 'L1_xattn_maa_w1': _L1_xattn_in['maa_w1'], 'L1_xattn_maa_w2': _L1_xattn_in['maa_w2'], 'L1_xattn_maa_stack': _L1_xattn_in['maa_stack'], 'L1_xattn_time_decay': _L1_xattn_in['time_decay'], 'L1_xattn_decay_w1': _L1_xattn_in['decay_w1'], 'L1_xattn_decay_w2': _L1_xattn_in['decay_w2'], 'L1_xattn_faaaa': _L1_xattn_in['faaaa'], 'L1_xattn_Wr': _L1_xattn_in['Wr'], 'L1_xattn_Wk': _L1_xattn_in['Wk'], 'L1_xattn_Wv': _L1_xattn_in['Wv'], 'L1_xattn_Wg': _L1_xattn_in['Wg'], 'L1_xattn_Wo': _L1_xattn_in['Wo'], 'L1_xattn_gn_w': _L1_xattn_in['gn_w'], 'L1_xattn_gn_b': _L1_xattn_in['gn_b'], 'L1_xattn_ffn_maa_k': _L1_xattn_in['ffn_maa_k'], 'L1_xattn_ffn_maa_r': _L1_xattn_in['ffn_maa_r'], 'L1_xattn_ffn_Wk': _L1_xattn_in['ffn_Wk'], 'L1_xattn_ffn_Wr': _L1_xattn_in['ffn_Wr'], 'L1_xattn_ffn_Wv': _L1_xattn_in['ffn_Wv']}

def reference(x, ctx_2048, L0_xattn_Wq, L0_xattn_bq, L0_xattn_Wk, L0_xattn_bk, L0_xattn_Wv, L0_xattn_bv, L1_xattn_ln1_w, L1_xattn_ln1_b, L1_xattn_ln2_w, L1_xattn_ln2_b, L1_xattn_maa_x, L1_xattn_maa_w1, L1_xattn_maa_w2, L1_xattn_maa_stack, L1_xattn_time_decay, L1_xattn_decay_w1, L1_xattn_decay_w2, L1_xattn_faaaa, L1_xattn_Wr, L1_xattn_Wk, L1_xattn_Wv, L1_xattn_Wg, L1_xattn_Wo, L1_xattn_gn_w, L1_xattn_gn_b, L1_xattn_ffn_maa_k, L1_xattn_ffn_maa_r, L1_xattn_ffn_Wk, L1_xattn_ffn_Wr, L1_xattn_ffn_Wv):
    import jax
    import jax.numpy as jnp

    def _L0_xattn_ref(x1, x2, Wq, bq, Wk, bk, Wv, bv):
        import jax, jax.numpy as jnp
        import numpy as np
        B, C1, C2, N = (8, 128, 128, 256)
        D = C2 // 8
        q = jnp.einsum('bcn,dc->bnd', x1, Wq) + bq
        k = jnp.einsum('bcn,dc->bdn', x2, Wk) + bk[:, None]
        v = jnp.einsum('bcn,dc->bdn', x2, Wv) + bv[:, None]
        attn = jax.nn.softmax(jnp.einsum('bnd,bdm->bnm', q, k), axis=2)
        attn_out = jnp.einsum('bcm,bnm->bcn', v, attn)
        return attn_out + x1

    def _L1_xattn_ref(x, state, ln1_w, ln1_b, ln2_w, ln2_b, maa_x, maa_w1, maa_w2, maa_stack, time_decay, decay_w1, decay_w2, faaaa, Wr, Wk, Wv, Wg, Wo, gn_w, gn_b, ffn_maa_k, ffn_maa_r, ffn_Wk, ffn_Wr, ffn_Wv, i):
        import jax, jax.numpy as jnp
        import numpy as np
        B, L, E, H = (4, 64, 256, 32)
        S = E // H
        EXTRA_MAA, EXTRA_DECAY = (32, 64)
        EPS = 1e-05

        def _ln(x, w, b):
            m = jnp.mean(x, axis=-1, keepdims=True)
            v = jnp.mean((x - m) ** 2, axis=-1, keepdims=True)
            return (x - m) * jax.lax.rsqrt(v + EPS) * w + b

        def _token_shift(xn, prev_row):
            first = (prev_row - xn[:, 0])[:, None]
            rest = xn[:, :-1] - xn[:, 1:]
            return jnp.concatenate([first, rest], axis=1)
        b, l = (x.shape[0], x.shape[1])
        i0 = (2 + S) * i + 0
        i1 = (2 + S) * i + 1
        xn = _ln(x, ln1_w, ln1_b)
        sx = _token_shift(xn, state[:, i1])
        xxx = jnp.tanh((xn + sx * maa_x) @ maa_w1).reshape(b, l, 5, 1, EXTRA_MAA)
        xxx = jnp.matmul(xxx, maa_w2).reshape(b, l, 5, E)
        x5 = xn[:, :, None] + sx[:, :, None] * (maa_stack + xxx)
        w = jnp.exp(-jnp.exp(time_decay + jnp.tanh(x5[:, :, 1] @ decay_w1) @ decay_w2))
        w = w.reshape(b, l, H, S)
        r = (x5[:, :, 3] @ Wr.T).reshape(b, l, H, S)
        k = (x5[:, :, 0] @ Wk.T).reshape(b, l, H, S)
        v = (x5[:, :, 2] @ Wv.T).reshape(b, l, H, S)
        g = jax.nn.silu(x5[:, :, 4] @ Wg.T)
        s0 = state[:, (2 + S) * i + 2:(2 + S) * (i + 1)].reshape(b, H, S, S)
        u = faaaa[None, :, :, None]

        def step(s, rkvw):
            r_t, k_t, v_t, w_t = rkvw
            a = k_t[:, :, :, None] * v_t[:, :, None, :]
            out = jnp.einsum('bhk,bhkd->bhd', r_t, u * a + s)
            return (a + w_t[:, :, :, None] * s, out)
        xs = tuple((jnp.moveaxis(t, 1, 0) for t in (r, k, v, w)))
        _, outs = jax.lax.scan(step, s0, xs)
        att = jnp.moveaxis(outs, 0, 1).reshape(b, l, E)
        a4 = att.reshape(b, l, H, S)
        m = jnp.mean(a4, axis=-1, keepdims=True)
        var = jnp.mean((a4 - m) ** 2, axis=-1, keepdims=True)
        att = ((a4 - m) * jax.lax.rsqrt(var + EPS)).reshape(b, l, E) * gn_w + gn_b
        x = x + att * g @ Wo.T
        xn2 = _ln(x, ln2_w, ln2_b)
        sx2 = _token_shift(xn2, state[:, i0])
        xk = xn2 + sx2 * ffn_maa_k
        xr = xn2 + sx2 * ffn_maa_r
        rr = jax.nn.sigmoid(xr @ ffn_Wr.T)
        kk = jnp.square(jax.nn.relu(xk @ ffn_Wk.T))
        x = x + rr * (kk @ ffn_Wv.T)
        return x
    x = _L0_xattn_ref(x, ctx_2048, L0_xattn_Wq, L0_xattn_bq, L0_xattn_Wk, L0_xattn_bk, L0_xattn_Wv, L0_xattn_bv)
    x = _L1_xattn_ref(x, ctx_2048, L1_xattn_ln1_w, L1_xattn_ln1_b, L1_xattn_ln2_w, L1_xattn_ln2_b, L1_xattn_maa_x, L1_xattn_maa_w1, L1_xattn_maa_w2, L1_xattn_maa_stack, L1_xattn_time_decay, L1_xattn_decay_w1, L1_xattn_decay_w2, L1_xattn_faaaa, L1_xattn_Wr, L1_xattn_Wk, L1_xattn_Wv, L1_xattn_Wg, L1_xattn_Wo, L1_xattn_gn_w, L1_xattn_gn_b, L1_xattn_ffn_maa_k, L1_xattn_ffn_maa_r, L1_xattn_ffn_Wk, L1_xattn_ffn_Wr, L1_xattn_ffn_Wv, 0)
    return x

_drawn_inputs = setup_inputs


def setup_inputs(seed=0):
    import zlib

    import numpy as np

    out = dict(_drawn_inputs(seed))
    spreads = {'L1_xattn_ln1_w': (1.0, 0.6),
     'L1_xattn_ln1_b': (0.0, 0.567),
     'L1_xattn_ln2_w': (1.0, 0.6),
     'L1_xattn_ln2_b': (0.0, 0.8),
     'L1_xattn_gn_w': (1.0, 0.6),
     'L1_xattn_gn_b': (0.0, 0.8)}
    factors = {'L0_xattn_bk': 64.0,
     'L1_xattn_maa_x': 8.0,
     'L1_xattn_maa_w1': 7.702,
     'L1_xattn_maa_w2': 7.769,
     'L1_xattn_maa_stack': 8.0,
     'L1_xattn_time_decay': 2.913,
     'L1_xattn_decay_w1': 8.0,
     'L1_xattn_decay_w2': 8.0,
     'L1_xattn_faaaa': 5.963,
     'L1_xattn_ffn_maa_k': 8.0,
     'L1_xattn_ffn_maa_r': 8.0,
     'L1_xattn_ffn_Wk': 2.935,
     'L1_xattn_ffn_Wr': 8.0,
     'L1_xattn_ffn_Wv': 2.703,
     'L0_xattn_bq': 3.5}
    for name, (base, spread) in spreads.items():
        noise = np.random.default_rng([zlib.crc32(name.encode()), seed]).standard_normal(out[name].shape)
        drawn = base * np.exp(spread * noise) if base else spread * noise
        out[name] = jnp.asarray(drawn.astype(out[name].dtype))
    for name, factor in factors.items():
        out[name] = (out[name] * factor).astype(out[name].dtype)
    return out
```

```python
import concourse.bass as bass
from concourse import mybir
from contextlib import ExitStack


def xattn_rwkv(nc: bass.Bass, x, ctx_2048, Wq, bq, Wk, bk, Wv, bv, ln1_w, ln1_b, ln2_w, ln2_b, maa_x, maa_w1,
               maa_w2, maa_stack, time_decay, decay_w1, decay_w2, faaaa, Wr, Wkey, Wval, Wg, Wo, gn_w, gn_b,
               ffn_maa_k, ffn_maa_r, ffn_Wk, ffn_Wr, ffn_Wv, out):
    f32, i32 = mybir.dt.float32, mybir.dt.int32
    ALU = mybir.AluOpType
    ACT = mybir.ActivationFunctionType
    X_AXIS = mybir.AxisListType.X

    B, L, E = x.shape
    D = Wq.shape[0]
    H, S = faaaa.shape
    HALVES = E // 128
    HH = H // HALVES
    PAIR = 2
    G = B // PAIR
    T = PAIR * L
    MIXES, LORA, _ = maa_w2.shape
    MIX_K, MIX_W, MIX_V, MIX_R, MIX_G = range(MIXES)
    DECAY = decay_w1.shape[1]
    UNITS = HALVES * S // 2
    EPS = 1e-5
    RSQRT_MAGIC = 0x5F3759DF

    ctx = ExitStack()
    with ctx:
        def sb(name, shape, dt=f32):
            return ctx.enter_context(nc.sbuf_tensor(name, shape, dt))

        def sem(name):
            return ctx.enter_context(nc.semaphore(name))

        ident = sb("ident", [128, 128])
        w_nat = sb("w_nat", [128, 8, 2, E])
        wT = sb("wT", [128, 8, 2, E])
        WR, WK, WV, WG, WO, FK, FR, FV = range(8)
        attn_nat = sb("attn_nat", [D, 2, L])
        attn_T = sb("attn_T", [L, 2, D])
        v0_nat = sb("v0_nat", [L, L])
        v0_T = sb("v0_T", [L, L])
        bqk = sb("bqk", [D, 2])
        bv_col = sb("bv_col", [L, 1])
        mw1 = sb("mw1", [128, 2, MIXES * LORA])
        mw2 = sb("mw2", [4 * LORA, E])
        mw2_last = sb("mw2_last", [LORA, E])
        dw1 = sb("dw1", [128, 2, DECAY])
        dw2 = sb("dw2", [DECAY, E])
        ROWS = 11 + MIXES
        rows = sb("rows", [ROWS, E])
        cols = sb("cols", [128, 2, ROWS])
        (R_LN1W, R_LN1B, R_LN2W, R_LN2B, R_MAAX, R_DECAY, R_U, R_GNW, R_GNB, R_FK, R_FR) = range(11)
        R_STACK = 11
        gn_half = sb("gn_half", [128, 2, 2])

        xin = sb("xin", [L, PAIR, E])
        cin = sb("cin", [L, PAIR, E])
        state_rows = sb("state_rows", [2 * PAIR, E])
        s0 = sb("s0", [128, 2, PAIR, S])
        qk = sb("qk", [D, 2, PAIR * E])
        vT = sb("vT", [128, PAIR, 2, L])
        neg_max = sb("neg_max", [128, PAIR, 2])
        prob = sb("prob", [128, PAIR, 2, E])
        prob_sum = sb("prob_sum", [128, PAIR, 2])
        prob_rcp = sb("prob_rcp", [128, PAIR, 2])
        probT = sb("probT", [128, PAIR, 2, E])
        x2 = sb("x2", [L, PAIR, E])
        st1 = sb("st1", [128, PAIR, 6])
        mv1 = sb("mv1", [128, PAIR, 2])
        wait_carrier = sb("wait_carrier", [128, 1])
        nwt1 = sb("nwt1", [128, 4, PAIR])
        xh = sb("xh", [L, PAIR, E])
        xn = sb("xn", [128, 2, PAIR, L + 1])
        sx = sb("sx", [128, 2, PAIR, L])
        xmix = sb("xmix", [128, 2, T])
        lora = sb("lora", [4 * LORA, T])
        lora_last = sb("lora_last", [LORA, T])
        mixed = sb("mixed", [128, MIXES, 2, T])
        x5 = sb("x5", [128, MIXES, 2, T])
        wt = sb("wt", [DECAY, T])
        e1 = sb("e1", [128, 2, PAIR, L])
        gate_th = sb("gate_th", [128, 2, T])

        kf = sb("kf", [128, 2, PAIR, L])
        rf = sb("rf", [128, 2, PAIR, L])
        w_prev = sb("w_prev", [128, 2, 2, PAIR, L])
        v_tok = sb("v_tok", [L, PAIR, E])
        v_exp = sb("v_exp", [L, PAIR, 2, S, 128])
        gate = sb("gate", [128, 2, T])
        last_row0 = sb("last_row0", [128, 2, PAIR])

        xres = sb("xres", [L, PAIR, E])
        kv = sb("kv", [128, 2, S, PAIR, L])
        state = sb("state", [128, 2, 2, PAIR, L])
        rs = sb("rs", [128, 2, 2, PAIR, L])
        ru = sb("ru", [128, 2, T])
        ruk = sb("ruk", [128, 2, T])
        bonus = sb("bonus", [L, PAIR, H])
        att = sb("att", [L, PAIR, H, S])
        cv = sb("cv", [L, PAIR, H, S])
        att1 = sb("att1", [L, PAIR, H, S])
        head_sum = sb("head_sum", [L, PAIR * H])
        att_c = sb("att_c", [L, PAIR, H, S])
        sq = sb("sq", [L, PAIR, H, S])
        head_var = sb("head_var", [L, PAIR * H])
        nwt2 = sb("nwt2", [L, 4, PAIR * H])
        att_n = sb("att_n", [L, PAIR, H, S])
        att_f = sb("att_f", [128, 2, T])
        ag = sb("ag", [128, 2, T])
        x3 = sb("x3", [L, PAIR, E])
        st2 = sb("st2", [128, PAIR, 6])
        mv2 = sb("mv2", [128, PAIR, 2])
        nwt3 = sb("nwt3", [128, 4, PAIR])
        xh2 = sb("xh2", [L, PAIR, E])
        xn2 = sb("xn2", [128, 2, PAIR, L + 1])
        sx2 = sb("sx2", [128, 2, PAIR, L])
        xk = sb("xk", [128, 2, T])
        xr = sb("xr", [128, 2, T])
        relu = sb("relu", [128, 2, T])
        kk = sb("kk", [128, 2, T])
        th2 = sb("th2", [L, PAIR, E])
        ffn = sb("ffn", [L, PAIR, E])
        x4 = sb("x4", [L, PAIR, E])

        FB = [ctx.enter_context(nc.psum_tensor(f"front_bank{i}", [128, 512], f32)) for i in range(4)]
        BB = [ctx.enter_context(nc.psum_tensor(f"back_bank{i}", [128, 512], f32)) for i in range(4)]

        def quarters(bank):
            return bank[:, :].rearrange("p (a b n) -> p a b n", a=2, b=2)

        def halves(bank):
            return bank[:, :].rearrange("p (a n) -> p a n", a=2)

        w_loaded = [sem(f"w{n}_loaded") for n in range(8)]
        attn_w_loaded, v0_loaded, rows_loaded = sem("attn_w_loaded"), sem("v0_loaded"), sem("rows_loaded")
        lora_loaded = sem("lora_loaded")
        biases_loaded = sem("biases_loaded")
        ident_ready, ident_zero = sem("ident_ready"), sem("ident_zero")
        w_turned, w_ready = sem("w_turned"), sem("w_ready")
        gn_half_ready = sem("gn_half_ready")
        w_prev_zero = sem("w_prev_zero")
        x_loaded, ctx_loaded, rows01_loaded, s0_loaded = (sem("x_loaded"), sem("ctx_loaded"), sem("rows01_loaded"),
                                                          sem("s0_loaded"))
        q_done, k_done, v_done = sem("q_done"), sem("k_done"), sem("v_done")
        qk_ready, vT_ready = sem("qk_ready"), sem("vT_ready")
        scores_done = sem("scores_done")
        max_ready = sem("max_ready")
        exp_ready = sem("exp_ready")
        rcp_ready = sem("rcp_ready")
        prob_ready = sem("prob_ready")
        prob_turned = sem("prob_turned")
        probT_ready = sem("probT_ready")
        attn_done = sem("attn_done")
        x2_ready = sem("x2_ready")
        ln1_steps = sem("ln1_steps")
        xh_ready = sem("xh_ready")
        xh_turned, rows01_turned = sem("xh_turned"), sem("rows01_turned")
        xn_ready, prev_ready = sem("xn_ready"), sem("prev_ready")
        sx_ready, xmix_ready = sem("sx_ready"), sem("xmix_ready")
        lora_done, lora_ready = sem("lora_done"), sem("lora_ready")
        mix_done = [sem(f"mix{j}_done") for j in range(MIXES)]
        mixed_ready = [sem(f"mixed{j}_ready") for j in range(MIXES)]
        x5_ready = [sem(f"x5_{j}_ready") for j in range(MIXES)]
        dlora_done, wt_ready = sem("dlora_done"), sem("wt_ready")
        decay_done, e1_ready, w_ready_s = sem("decay_done"), sem("e1_ready"), sem("decay_ready")
        kp_done, kf_ready = sem("kp_done"), sem("kf_ready")
        rp_done, rf_ready = sem("rp_done"), sem("rf_ready")
        vp_done, v_exp_ready, v_tok_ready = sem("vp_done"), sem("v_exp_ready"), sem("v_tok_ready")
        gp_done, gate_th_ready, gate_ready = sem("gp_done"), sem("gate_th_ready"), sem("gate_ready")
        xres_ready, s0_placed = sem("xres_ready"), sem("s0_placed")
        v_spread = sem("v_spread")
        kv_ready, state_ready = sem("kv_ready"), sem("state_ready")
        rs_ready = sem("rs_ready")
        ru_ready, ruk_ready = sem("ru_ready"), sem("ruk_ready")
        rs_turned = sem("rs_turned")
        head_out_ready = sem("head_out_ready")
        cv_ready, att1_ready = sem("cv_ready"), sem("att1_ready")
        head_sum_ready, att_c_ready, sq_ready = sem("head_sum_ready"), sem("att_c_ready"), sem("sq_ready")
        gn_sum, gn_steps = sem("gn_sum"), sem("gn_steps")
        att_n_ready = sem("att_n_ready")
        att_turned, att_f_ready, ag_ready = sem("att_turned"), sem("att_f_ready"), sem("ag_ready")
        o_done, x3_ready = sem("o_done"), sem("x3_ready")
        ln2_steps, xh2_ready = sem("ln2_steps"), sem("xh2_ready")
        xh2_turned, xn2_ready, prev2_ready = sem("xh2_turned"), sem("xn2_ready"), sem("prev2_ready")
        sx2_ready, xk_ready, xr_ready = sem("sx2_ready"), sem("xk_ready"), sem("xr_ready")
        fk_done, relu_ready, kk_ready = sem("fk_done"), sem("relu_ready"), sem("kk_ready")
        fr_done, th2_ready = sem("fr_done"), sem("th2_ready")
        fv_done, ffn_ready, x4_ready = sem("fv_done"), sem("ffn_ready"), sem("x4_ready")
        stored = sem("stored")
        NEWTON = 3
        RS = 4 + 3 * NEWTON
        LN_STEPS = 2 * PAIR + RS

        block = ctx.enter_context(nc.Block())

        @block.sync
        def _(sp):
            sp.dma_start(xin[:, :, :], x[0:PAIR, :, :].rearrange("b c n -> c b n")).then_inc(x_loaded, 16)
            sp.dma_start(cin[:, :, :], ctx_2048[0:PAIR, :, :].rearrange("b c n -> c b n")).then_inc(ctx_loaded, 16)
            sp.dma_start(attn_nat[:, 0, :], Wq).then_inc(attn_w_loaded, 16)
            sp.dma_start(attn_nat[:, 1, :], Wk).then_inc(attn_w_loaded, 16)
            sp.dma_start(v0_nat[:, :], Wv).then_inc(v0_loaded, 16)
            sp.dma_start(bqk[:, 0:1], bq.rearrange("(d a) -> d a", a=1)).then_inc(biases_loaded, 16)
            sp.dma_start(bqk[:, 1:2], bk.rearrange("(d a) -> d a", a=1)).then_inc(biases_loaded, 16)
            sp.dma_start(bv_col[:, :], bv.rearrange("(d a) -> d a", a=1)).then_inc(biases_loaded, 16)
            for r, vec in ((R_LN1W, ln1_w), (R_LN1B, ln1_b), (R_LN2W, ln2_w), (R_LN2B, ln2_b), (R_MAAX, maa_x),
                           (R_DECAY, time_decay), (R_GNW, gn_w), (R_GNB, gn_b), (R_FK, ffn_maa_k),
                           (R_FR, ffn_maa_r)):
                sp.dma_start(rows[r:r + 1, :], vec.rearrange("(a e) -> a e", a=1)).then_inc(rows_loaded, 16)
            sp.dma_start(rows[R_U:R_U + 1, :], faaaa.rearrange("h s -> (h s)").rearrange("(a e) -> a e", a=1)
                         ).then_inc(rows_loaded, 16)
            sp.dma_start(rows[R_STACK:ROWS, :], maa_stack).then_inc(rows_loaded, 16)
            sp.dma_start(mw1[:, :, :], maa_w1.rearrange("(h p) n -> p h n", p=128)).then_inc(lora_loaded, 16)
            sp.dma_start(mw2[:, :], maa_w2[0:4, :, :].rearrange("j i e -> (j i) e")).then_inc(lora_loaded, 16)
            sp.dma_start(mw2_last[:, :], maa_w2[4, :, :]).then_inc(lora_loaded, 16)
            sp.dma_start(dw1[:, :, :], decay_w1.rearrange("(h p) n -> p h n", p=128)).then_inc(lora_loaded, 16)
            sp.dma_start(dw2[:, :], decay_w2).then_inc(lora_loaded, 16)

            def load_state(g):
                for b in range(PAIR):
                    if not isinstance(g, int) and b == 0:
                        sp.wait_ge(rows01_turned, g)
                    sp.dma_start(state_rows[2 * b:2 * b + 2, :],
                                 ctx_2048[bass.ds(PAIR * g + b, 1), 0:2, :].rearrange("b r e -> (b r) e")
                                 ).then_inc(rows01_loaded, 16)
                for b in range(PAIR):
                    if not isinstance(g, int) and b == 0:
                        sp.wait_ge(s0_placed, g)
                    sp.dma_start(s0[:, :, b, :],
                                 ctx_2048[bass.ds(PAIR * g + b, 1), 2:2 + S, :].rearrange(
                                     "b (h r) (p s) -> (r p) (b h) s", h=2, s=S)).then_inc(s0_loaded, 16)

            load_state(0)
            with sp.Fori(1, G) as g:
                sp.wait_ge(x2_ready, g)
                sp.dma_start(xin[:, :, :], x[bass.ds(PAIR * g, PAIR), :, :].rearrange("b c n -> c b n")
                             ).then_inc(x_loaded, 16)
                sp.wait_ge(v_done, g)
                sp.dma_start(cin[:, :, :], ctx_2048[bass.ds(PAIR * g, PAIR), :, :].rearrange("b c n -> c b n")
                             ).then_inc(ctx_loaded, 16)
                load_state(g)

        @block.gpsimd
        def _(pool):
            pool.memset(ident[:, :], 0.0).then_inc(ident_zero, 1)
            pool.wait_ge(ident_zero, 1)
            pool.affine_select(out=ident[:, :], in_=ident[:, :], compare_op=ALU.not_equal, fill=1.0, base=0,
                               pattern=[[-1, 128]], channel_multiplier=1).then_inc(ident_ready, 1)
            pool.memset(w_prev[:, :, :, :, 0], 0.0).then_inc(w_prev_zero, 1)

            def normalise(g, b):
                pool.wait_ge(rcp_ready, 2 * g + b + 1)
                pool.tensor_tensor(prob[:, b, :, :], prob[:, b, :, :],
                                   prob_rcp[:, b, :].unsqueeze(2).broadcast_to([128, 2, E]), ALU.mult
                                   ).then_inc(prob_ready, 1)

            def add_xn(g, j):
                pool.wait_ge(mixed_ready[j], 2 * g + 2)
                pool.wait_ge(xn_ready, 2 * g + 2)
                if not isinstance(g, int):
                    pool.wait_ge([kp_done, dlora_done, vp_done, rp_done, gp_done][j], g)
                pool.tensor_tensor(x5[:, j, :, :].rearrange("p h (b t) -> p h b t", b=PAIR),
                                   mixed[:, j, :, :].rearrange("p h (b t) -> p h b t", b=PAIR),
                                   xn[:, :, :, 1:], ALU.add).then_inc(x5_ready[j], 1)

            def scan_start(g):
                pool.wait_ge(rf_ready, g + 1)
                if not (isinstance(g, int) and g == 0):
                    pool.wait_ge(ruk_ready, g)
                pool.wait_ge(w_ready, 3)
                pool.tensor_tensor(ru[:, :, :], rf[:, :, :, :].rearrange("p h b t -> p h (b t)"),
                                   cols[:, :, R_U:R_U + 1].broadcast_to([128, 2, T]), ALU.mult).then_inc(ru_ready, 1)
                pool.wait_ge(ru_ready, g + 1)
                pool.wait_ge(kf_ready, g + 1)
                if not (isinstance(g, int) and g == 0):
                    pool.wait_ge(rs_turned, 9 * g)
                pool.tensor_tensor(ruk[:, :, :], ru[:, :, :], kf[:, :, :, :].rearrange("p h b t -> p h (b t)"),
                                   ALU.mult).then_inc(ruk_ready, 1)

            def scan(g, u):
                h = u // 4
                pool.wait_ge(state_ready, UNITS * g + u + 1)
                if u >= 2:
                    pool.wait_ge(rs_turned, 9 * g + u)
                elif not (isinstance(g, int) and g == 0):
                    pool.wait_ge(rs_turned, 9 * g)
                pool.tensor_tensor(rs[:, u % 2, :, :, :].rearrange("p d b t -> p d (b t)"),
                                   state[:, u % 2, :, :, :].rearrange("p d b t -> p d (b t)"),
                                   rf[:, h, :, :].rearrange("p b t -> p (b t)").unsqueeze(1).broadcast_to([128, 2, T]),
                                   ALU.mult).then_inc(rs_ready, 1)

            def group_norm(g):
                def again(s):
                    if not (isinstance(g, int) and g == 0):
                        pool.wait_ge(s, g)
                pool.wait_ge(head_out_ready, 9 * g + 1)
                pool.wait_ge(v_tok_ready, g + 1)
                again(att1_ready)
                pool.tensor_tensor(cv[:, :, :, :], v_tok[:, :, :].rearrange("p b (h s) -> p b h s", s=S),
                                   bonus[:, :, :].unsqueeze(3).broadcast_to([L, PAIR, H, S]), ALU.mult
                                   ).then_inc(cv_ready, 1)
                pool.wait_ge(cv_ready, g + 1)
                pool.wait_ge(head_out_ready, 9 * g + 9)
                again(att_c_ready)
                pool.tensor_tensor(att1[:, :, :, :], att[:, :, :, :], cv[:, :, :, :], ALU.add).then_inc(att1_ready, 1)
                pool.wait_ge(att1_ready, g + 1)
                pool.wait_ge(head_sum_ready, g + 1)
                again(att_n_ready)
                pool.tensor_tensor(att_c[:, :, :, :].rearrange("p b h s -> p (b h) s"),
                                   att1[:, :, :, :].rearrange("p b h s -> p (b h) s"),
                                   head_sum[:, :].unsqueeze(2).broadcast_to([L, PAIR * H, S]), ALU.add
                                   ).then_inc(att_c_ready, 1)
                pool.wait_ge(gn_steps, (RS + 1) * (g + 1))
                again(att_turned)
                pool.tensor_tensor(att_n[:, :, :, :].rearrange("p b h s -> p (b h) s"),
                                   att_c[:, :, :, :].rearrange("p b h s -> p (b h) s"),
                                   nwt2[:, 3, :].unsqueeze(2).broadcast_to([L, PAIR * H, S]), ALU.mult
                                   ).then_inc(att_n_ready, 1)

            def gated(g):
                pool.wait_ge(att_f_ready, 2 * g + 2)
                pool.wait_ge(gate_ready, g + 1)
                if not (isinstance(g, int) and g == 0):
                    pool.wait_ge(o_done, g)
                pool.tensor_tensor(ag[:, :, :], att_f[:, :, :], gate[:, :, :], ALU.mult).then_inc(ag_ready, 1)

            def body(f, b):
                if f is not None:
                    normalise(f, 0)
                    normalise(f, 1)
                if b is not None:
                    scan_start(b)
                    for u in range(UNITS):
                        scan(b, u)
                    group_norm(b)
                    gated(b)
                if f is not None:
                    for j in (MIX_W, MIX_K, MIX_R, MIX_V, MIX_G):
                        add_xn(f, j)

            body(0, None)
            body(1, 0)
            with pool.Fori(2, G) as i:
                body(i, i - 1)
            body(None, G - 1)

        @block.scalar
        def _(act):
            for n, w in enumerate((Wr, Wkey, Wval, Wg, Wo, ffn_Wk, ffn_Wr, ffn_Wv)):
                act.dma_start(w_nat[:, n, :, :], w.rearrange("(h p) e -> p h e", p=128)).then_inc(w_loaded[n], 16)

            act.wait_ge(w_turned, 1)
            act.activation(attn_T[:, :, :], FB[0][:, 0:2 * D].rearrange("p (a d) -> p a d", a=2), ACT.Copy
                           ).then_inc(w_ready, 1)
            act.wait_ge(w_turned, 2)
            act.activation(v0_T[:, :], FB[1][:, 0:L], ACT.Copy).then_inc(w_ready, 1)
            act.wait_ge(w_turned, 3)
            act.activation(cols[:, :, :], FB[2][:, 0:2 * ROWS].rearrange("p (a r) -> p a r", a=2), ACT.Copy
                           ).then_inc(w_ready, 1)
            act.wait_ge(w_ready, 3)
            act.activation(gn_half[:, :, :], cols[:, :, R_GNW:R_GNB + 1], ACT.Copy, scale=0.5).then_inc(gn_half_ready, 1)
            for n in range(8):
                act.wait_ge(w_turned, 4 + n)
                act.activation(wT[:, n, :, :], halves(BB[n % 4]), ACT.Copy).then_inc(w_ready, 1)

            def first(g):
                return isinstance(g, int) and g == 0

            def attn_in(g):
                act.wait_ge(biases_loaded, 48)
                act.wait_ge(q_done, g + 1)
                if not first(g):
                    act.wait_ge(scores_done, 2 * g)
                act.activation(qk[:, 0, :], FB[0][0:D, :], ACT.Identity, bias=bqk[:, 0:1]).then_inc(qk_ready, 1)
                act.wait_ge(k_done, g + 1)
                act.activation(qk[:, 1, :], FB[1][0:D, :], ACT.Identity, bias=bqk[:, 1:2]).then_inc(qk_ready, 1)
                act.wait_ge(v_done, g + 1)
                if not first(g):
                    act.wait_ge(attn_done, g)
                act.activation(vT[:, :, :, :], quarters(FB[2]), ACT.Copy).then_inc(vT_ready, 1)

            def softmax(g, b):
                act.wait_ge(max_ready, 2 * g + b + 1)
                if not first(g):
                    act.wait_ge(prob_turned, 2 * g)
                bank = (FB[3], FB[0])[b]
                for nt in range(2):
                    act.activation(prob[:, b, nt, :], halves(bank)[:, nt, :], ACT.Exp, bias=neg_max[:, b, nt:nt + 1],
                                   accum_out=prob_sum[:, b, nt:nt + 1]).then_inc(exp_ready, 1)

            def prob_evacuate(g, b):
                act.wait_ge(prob_turned, 2 * g + b + 1)
                if not first(g):
                    act.wait_ge(attn_done, g)
                act.activation(probT[:, b, :, :], halves(FB[1 + b]), ACT.Copy).then_inc(probT_ready, 1)

            def norm_evacuate(g):
                act.wait_ge(w_ready, 3)
                act.wait_ge(xh_turned, g + 1)
                if not first(g):
                    for j in range(MIXES):
                        act.wait_ge(x5_ready[j], g)
                for h in range(2):
                    act.activation(xn[:, h, :, 1:], quarters(FB[0])[:, h, :, :], ACT.Identity,
                                   bias=cols[:, h, R_LN1B:R_LN1B + 1], scale=cols[:, h, R_LN1W:R_LN1W + 1]
                                   ).then_inc(xn_ready, 1)
                act.wait_ge(rows01_turned, g + 1)
                turned = FB[1][:, 0:4 * PAIR].rearrange("p (h b r) -> p h b r", h=2, b=PAIR)
                act.activation(xn[:, :, :, 0], turned[:, :, :, 1], ACT.Copy).then_inc(prev_ready, 1)
                if not first(g):
                    act.wait_ge(prev2_ready, g)
                act.activation(last_row0[:, :, :], turned[:, :, :, 0], ACT.Copy).then_inc(prev_ready, 1)

            def lora_tanh(g):
                act.wait_ge(lora_done, g + 1)
                if not first(g):
                    for j in range(MIXES):
                        act.wait_ge(mix_done[j], g)
                act.activation(lora[:, :], FB[2][:, 0:T], ACT.Tanh).then_inc(lora_ready, 1)
                act.activation(lora_last[:, :], FB[2][0:LORA, T:2 * T], ACT.Tanh).then_inc(lora_ready, 1)

            def decay_tanh(g):
                act.wait_ge(dlora_done, g + 1)
                if not first(g):
                    act.wait_ge(decay_done, g)
                act.activation(wt[:, :], FB[0][0:DECAY, 0:T], ACT.Tanh).then_inc(wt_ready, 1)

            def decay(g):
                act.wait_ge(decay_done, g + 1)
                if not first(g):
                    act.wait_ge(w_ready_s, 2 * g)
                for h in range(2):
                    act.activation(e1[:, h, :, :].rearrange("p b t -> p (b t)"), halves(FB[0])[:, h, :], ACT.Exp,
                                   bias=cols[:, h, R_DECAY:R_DECAY + 1]).then_inc(e1_ready, 1)
                act.wait_ge(e1_ready, 2 * g + 2)
                act.wait_ge(w_prev_zero, 1)
                if not first(g):
                    act.wait_ge(state_ready, UNITS * g)
                for d in range(2):
                    act.activation(w_prev[:, :, d, :, 1:], e1[:, :, :, 0:L - 1], ACT.Exp, scale=-1.0
                                   ).then_inc(w_ready_s, 1)

            def evacuate_k(g):
                act.wait_ge(kp_done, g + 1)
                if not first(g):
                    act.wait_ge(kv_ready, UNITS * g)
                    act.wait_ge(ruk_ready, g)
                act.activation(kf[:, :, :, :], quarters(FB[3]), ACT.Copy).then_inc(kf_ready, 1)

            def evacuate_r(g):
                act.wait_ge(rp_done, g + 1)
                if not first(g):
                    act.wait_ge(rs_ready, UNITS * g)
                act.activation(rf[:, :, :, :], quarters(FB[1]), ACT.Copy).then_inc(rf_ready, 1)

            def evacuate_v(g):
                act.wait_ge(vp_done, g + 1)
                if not first(g):
                    act.wait_ge(v_spread, UNITS * g)
                for b in range(PAIR):
                    for h in range(2):
                        src = halves(FB[2])[:, b, 128 * h:128 * h + 128].rearrange("p (n d) -> p d n", d=S)
                        act.activation(v_exp[:, b, h, :, :].rearrange("p d (n k) -> p d n k", k=S),
                                       src.unsqueeze(3).broadcast_to([L, S, HH, S]), ACT.Copy
                                       ).then_inc(v_exp_ready, 1)
                if not first(g):
                    act.wait_ge(cv_ready, g)
                act.activation(v_tok[:, :, :], halves(FB[2]), ACT.Copy).then_inc(v_tok_ready, 1)

            def gate_tanh(g):
                act.wait_ge(gp_done, g + 1)
                if not first(g):
                    act.wait_ge(gate_ready, g)
                act.activation(gate_th[:, :, :], halves(FB[0]), ACT.Tanh, scale=0.5).then_inc(gate_th_ready, 1)

            def square_heads(g):
                act.wait_ge(att_c_ready, g + 1)
                if not first(g):
                    act.wait_ge(gn_steps, (RS + 1) * g)
                act.activation(sq[:, :, :, :], att_c[:, :, :, :], ACT.Square).then_inc(sq_ready, 1)

            def att_evacuate(g):
                act.wait_ge(gn_half_ready, 1)
                act.wait_ge(att_turned, g + 1)
                if not first(g):
                    act.wait_ge(ag_ready, g)
                for h in range(2):
                    act.activation(att_f[:, h, :], halves(BB[0])[:, h, :], ACT.Identity,
                                   bias=gn_half[:, h, 1:2], scale=gn_half[:, h, 0:1]).then_inc(att_f_ready, 1)

            def norm2_evacuate(g):
                act.wait_ge(xh2_turned, g + 1)
                if not first(g):
                    act.wait_ge(xk_ready, 2 * g)
                    act.wait_ge(xr_ready, 2 * g)
                for h in range(2):
                    act.activation(xn2[:, h, :, 1:], quarters(BB[2])[:, h, :, :], ACT.Identity,
                                   bias=cols[:, h, R_LN2B:R_LN2B + 1], scale=cols[:, h, R_LN2W:R_LN2W + 1]
                                   ).then_inc(xn2_ready, 1)

            def prev2(g):
                act.wait_ge(prev_ready, 2 * g + 2)
                if not first(g):
                    act.wait_ge(sx2_ready, g)
                act.activation(xn2[:, :, :, 0], last_row0[:, :, :], ACT.Copy).then_inc(prev2_ready, 1)

            def ffn_act(g):
                act.wait_ge(fk_done, g + 1)
                if not first(g):
                    act.wait_ge(kk_ready, g)
                act.activation(relu[:, :, :], halves(BB[3]), ACT.Relu).then_inc(relu_ready, 1)
                act.wait_ge(relu_ready, g + 1)
                if not first(g):
                    act.wait_ge(fv_done, g)
                act.activation(kk[:, :, :], relu[:, :, :], ACT.Square).then_inc(kk_ready, 1)
                act.wait_ge(fr_done, g + 1)
                if not first(g):
                    act.wait_ge(ffn_ready, g)
                act.activation(th2[:, :, :], halves(BB[0]), ACT.Tanh, scale=0.5).then_inc(th2_ready, 1)

            def store(g):
                act.wait_ge(x4_ready, g + 1)
                act.dma_start(out[bass.ds(PAIR * g, PAIR), :, :].rearrange("b c n -> c b n"), x4[:, :, :]
                              ).then_inc(stored, 16)

            def body(f, b):
                if b is not None:
                    prev2(b)
                if f is not None:
                    attn_in(f)
                    softmax(f, 0)
                    softmax(f, 1)
                    prob_evacuate(f, 0)
                    prob_evacuate(f, 1)
                    norm_evacuate(f)
                    lora_tanh(f)
                if b is not None:
                    square_heads(b)
                    att_evacuate(b)
                if f is not None:
                    decay_tanh(f)
                    evacuate_k(f)
                    decay(f)
                    evacuate_r(f)
                    evacuate_v(f)
                    gate_tanh(f)
                if b is not None:
                    norm2_evacuate(b)
                    ffn_act(b)
                    store(b)

            body(0, None)
            body(1, 0)
            with act.Fori(2, G) as i:
                body(i, i - 1)
            body(None, G - 1)
            act.wait_ge(stored, 16 * G)

        @block.tensor
        def _(pe):
            def first(g):
                return isinstance(g, int) and g == 0

            def turn(out_, in_, k=128):
                return pe.transpose(out_, in_, ident[0:k, 0:k])

            pe.wait_ge(ident_ready, 1)
            pe.wait_ge(attn_w_loaded, 32)
            for n in range(2):
                i = turn(FB[0][:, n * D:(n + 1) * D], attn_nat[:, n, :], D)
            i.then_inc(w_turned, 1)
            pe.wait_ge(v0_loaded, 16)
            turn(FB[1][:, 0:L], v0_nat[:, :]).then_inc(w_turned, 1)
            pe.wait_ge(rows_loaded, 16 * 12)
            for h in range(2):
                i = turn(FB[2][:, h * ROWS:(h + 1) * ROWS], rows[:, 128 * h:128 * h + 128], ROWS)
            i.then_inc(w_turned, 1)
            for n in range(8):
                pe.wait_ge(w_loaded[n], 16)
                if n >= 4:
                    pe.wait_ge(w_ready, 3 + n - 3)
                for h_in in range(2):
                    for h_out in range(2):
                        i = turn(quarters(BB[n % 4])[:, h_in, h_out, :],
                                 w_nat[:, n, h_out, 128 * h_in:128 * h_in + 128])
                i.then_inc(w_turned, 1)

            def attn_in(g):
                pe.wait_ge(x_loaded, 16 * (g + 1))
                if first(g):
                    pe.wait_ge(w_ready, 3)
                else:
                    pe.wait_ge(gate_ready, g)
                pe.matmul(FB[0][0:D, :], attn_T[:, 0, :], xin[:, :, :].rearrange("p b n -> p (b n)"),
                          start=True, stop=True).then_inc(q_done, 1)
                pe.wait_ge(ctx_loaded, 16 * (g + 1))
                if not first(g):
                    pe.wait_ge(rf_ready, g)
                pe.matmul(FB[1][0:D, :], attn_T[:, 1, :], cin[:, :, :].rearrange("p b n -> p (b n)"),
                          start=True, stop=True).then_inc(k_done, 1)
                if not first(g):
                    pe.wait_ge(v_tok_ready, g)
                for b in range(PAIR):
                    for mt in range(2):
                        i = pe.matmul(quarters(FB[2])[:, b, mt, :], cin[:, b, 128 * mt:128 * mt + 128], v0_T[:, :],
                                      start=True, stop=True)
                i.then_inc(v_done, 1)

            def scores(g):
                pe.wait_ge(qk_ready, 2 * g + 2)
                if not first(g):
                    pe.wait_ge(mixed_ready[MIX_G], 2 * g)
                for b in range(PAIR):
                    bank = (FB[3], FB[0])[b]
                    for nt in range(2):
                        i = pe.matmul(halves(bank)[:, nt, :], qk[:, 0, b * E + 128 * nt:b * E + 128 * nt + 128],
                                      qk[:, 1, b * E:(b + 1) * E], start=True, stop=True)
                    i.then_inc(scores_done, 1)

            def prob_turn(g, b):
                pe.wait_ge(prob_ready, 2 * g + b + 1)
                if b == 1:
                    pe.wait_ge(vT_ready, g + 1)
                for mt in range(2):
                    for nt in range(2):
                        i = turn(quarters(FB[1 + b])[:, mt, nt, :], prob[:, b, nt, 128 * mt:128 * mt + 128])
                i.then_inc(prob_turned, 1)

            def attn_out(g):
                pe.wait_ge(vT_ready, g + 1)
                for b in range(PAIR):
                    pe.wait_ge(probT_ready, 2 * g + b + 1)
                    for mt in range(2):
                        i = pe.matmul(halves(FB[3])[:, b, :], vT[:, b, mt, :], probT[:, b, mt, :],
                                      start=(mt == 0), stop=(mt == 1))
                i.then_inc(attn_done, 1)

            def norm_turn(g):
                pe.wait_ge(rows01_loaded, 16 * PAIR * (g + 1))
                pe.wait_ge(probT_ready, 2 * g + 1)
                for h in range(2):
                    i = pe.matmul(FB[1][:, 2 * PAIR * h:2 * PAIR * (h + 1)], state_rows[:, 128 * h:128 * h + 128],
                                  ident[0:2 * PAIR, 0:2 * PAIR], start=True, stop=True)
                i.then_inc(rows01_turned, 1)
                for b in range(PAIR):
                    pe.wait_ge(xh_ready, 2 * g + b + 1)
                    for h in range(2):
                        i = turn(quarters(FB[0])[:, h, b, :], xh[:, b, 128 * h:128 * h + 128])
                i.then_inc(xh_turned, 1)

            def lora_in(g):
                pe.wait_ge(lora_loaded, 80)
                pe.wait_ge(xmix_ready, 2 * g + 2)
                pe.wait_ge(probT_ready, 2 * g + 2)
                for h in range(2):
                    pe.matmul(FB[2][:, 0:T], mw1[:, h, 0:4 * LORA], xmix[:, h, :], start=(h == 0), stop=(h == 1))
                for h in range(2):
                    i = pe.matmul(FB[2][0:LORA, T:2 * T], mw1[:, h, 4 * LORA:], xmix[:, h, :],
                                  start=(h == 0), stop=(h == 1))
                i.then_inc(lora_done, 1)

            def mix(g, j, bank):
                for h in range(2):
                    if j < 4:
                        w2, lo = mw2[LORA * j:LORA * (j + 1), :], lora[LORA * j:LORA * (j + 1), :]
                    else:
                        w2, lo = mw2_last[:, :], lora_last[:, :]
                    i = pe.matmul(halves(bank)[:, h, :], w2[:, 128 * h:128 * h + 128], lo, start=True, stop=True)
                i.then_inc(mix_done[j], 1)

            def to_features(bank, w, src, done):
                for h_out in range(2):
                    for h_in in range(2):
                        i = pe.matmul(halves(bank)[:, h_out, :], wT[:, w, h_in, 128 * h_out:128 * h_out + 128],
                                      src[:, h_in, :], start=(h_in == 0), stop=(h_in == 1))
                i.then_inc(done, 1)

            def to_tokens(bank, w, src, done):
                for b in range(PAIR):
                    for h_in in range(2):
                        i = pe.matmul(halves(bank)[:, b, :], src[:, h_in, L * b:L * (b + 1)], wT[:, w, h_in, :],
                                      start=(h_in == 0), stop=(h_in == 1))
                i.then_inc(done, 1)

            def mixes(g):
                pe.wait_ge(w_ready, 3 + 8)
                pe.wait_ge(lora_ready, 2 * g + 2)
                pe.wait_ge(x2_ready, g + 1)
                mix(g, MIX_W, FB[3])
                mix(g, MIX_K, FB[2])
                pe.wait_ge(x5_ready[MIX_W], g + 1)
                pe.wait_ge(xn_ready, 2 * g + 2)
                for h in range(2):
                    i = pe.matmul(FB[0][0:DECAY, 0:T], dw1[:, h, :], x5[:, MIX_W, h, :], start=(h == 0), stop=(h == 1))
                i.then_inc(dlora_done, 1)
                pe.wait_ge(prev_ready, 2 * g + 2)
                mix(g, MIX_R, FB[1])
                pe.wait_ge(mixed_ready[MIX_W], 2 * g + 2)
                pe.wait_ge(x5_ready[MIX_K], g + 1)
                to_features(FB[3], WK, x5[:, MIX_K, :, :], kp_done)
                pe.wait_ge(wt_ready, g + 1)
                for h in range(2):
                    i = pe.matmul(halves(FB[0])[:, h, :], dw2[:, 128 * h:128 * h + 128], wt[:, :], start=True, stop=True)
                i.then_inc(decay_done, 1)
                pe.wait_ge(mixed_ready[MIX_K], 2 * g + 2)
                mix(g, MIX_V, FB[2])
                pe.wait_ge(mixed_ready[MIX_R], 2 * g + 2)
                pe.wait_ge(x5_ready[MIX_R], g + 1)
                to_features(FB[1], WR, x5[:, MIX_R, :, :], rp_done)
                pe.wait_ge(kf_ready, g + 1)
                mix(g, MIX_G, FB[3])
                pe.wait_ge(mixed_ready[MIX_V], 2 * g + 2)
                pe.wait_ge(x5_ready[MIX_V], g + 1)
                to_tokens(FB[2], WV, x5[:, MIX_V, :, :], vp_done)
                pe.wait_ge(e1_ready, 2 * g + 2)
                pe.wait_ge(x5_ready[MIX_G], g + 1)
                to_features(FB[0], WG, x5[:, MIX_G, :, :], gp_done)

            def spread(g, u):
                if u == 0:
                    pe.wait_ge(v_exp_ready, 2 * PAIR * (g + 1))
                if u >= 2:
                    pe.wait_ge(kv_ready, UNITS * g + u - 1)
                elif not first(g):
                    pe.wait_ge((th2_ready, ffn_ready)[u], g)
                h, d0 = u // 4, 2 * (u % 4)
                for d in range(2):
                    for b in range(PAIR):
                        i = turn(quarters(BB[u % 2])[:, d, b, :], v_exp[:, b, h, d0 + d, :])
                i.then_inc(v_spread, 1)

            def turn_bonus(g):
                pe.wait_ge(ruk_ready, g + 1)
                if not first(g):
                    pe.wait_ge(xn2_ready, 2 * g)
                for b in range(PAIR):
                    for h in range(2):
                        i = turn(quarters(BB[2])[:, b, h, :], ruk[:, h, L * b:L * (b + 1)])
                i.then_inc(rs_turned, 1)

            def turn_rs(g, u):
                pe.wait_ge(rs_ready, UNITS * g + u + 1)
                if u >= 1:
                    pe.wait_ge(head_out_ready, 9 * g + u)
                elif not first(g):
                    pe.wait_ge(relu_ready, g)
                for b in range(PAIR):
                    for d in range(2):
                        i = turn(quarters(BB[2 + (u + 1) % 2])[:, b, d, :], rs[:, u % 2, d, b, :])
                i.then_inc(rs_turned, 1)

            def units(g, lo, hi):
                for u in range(lo, hi):
                    if u + 2 < UNITS:
                        spread(g, u + 2)
                    turn_rs(g, u)

            def att_turn(g):
                pe.wait_ge(att_n_ready, g + 1)
                flat = att_n[:, :, :, :].rearrange("p b h s -> p b (h s)")
                for h in range(2):
                    for b in range(PAIR):
                        i = turn(quarters(BB[0])[:, h, b, :], flat[:, b, 128 * h:128 * h + 128])
                i.then_inc(att_turned, 1)

            def att_project(g):
                pe.wait_ge(ag_ready, g + 1)
                to_tokens(BB[1], WO, ag, o_done)

            def norm2_turn(g):
                for b in range(PAIR):
                    pe.wait_ge(xh2_ready, 2 * g + b + 1)
                    for h in range(2):
                        i = turn(quarters(BB[2])[:, h, b, :], xh2[:, b, 128 * h:128 * h + 128])
                i.then_inc(xh2_turned, 1)

            def ffn_in(g):
                pe.wait_ge(xk_ready, 2 * g + 2)
                to_features(BB[3], FK, xk, fk_done)
                pe.wait_ge(xr_ready, 2 * g + 2)
                pe.wait_ge(att_f_ready, 2 * g + 2)
                to_tokens(BB[0], FR, xr, fr_done)

            def ffn_out(g):
                pe.wait_ge(kk_ready, g + 1)
                pe.wait_ge(x3_ready, g + 1)
                to_tokens(BB[1], FV, kk, fv_done)

            def body(f, b):
                if f is not None:
                    attn_in(f)
                    scores(f)
                if b is not None:
                    spread(b, 0)
                    turn_bonus(b)
                    spread(b, 1)
                if f is not None:
                    prob_turn(f, 0)
                    prob_turn(f, 1)
                    attn_out(f)
                if b is not None:
                    units(b, 0, 1)
                if f is not None:
                    norm_turn(f)
                if b is not None:
                    units(b, 1, 2)
                if f is not None:
                    lora_in(f)
                if b is not None:
                    units(b, 2, UNITS)
                    att_turn(b)
                    att_project(b)
                if f is not None:
                    mixes(f)
                if b is not None:
                    norm2_turn(b)
                    ffn_in(b)
                    ffn_out(b)

            body(0, None)
            body(1, 0)
            with pe.Fori(2, G) as i:
                body(i, i - 1)
            body(None, G - 1)

        @block.vector
        def _(dve):
            def first(g):
                return isinstance(g, int) and g == 0

            def root(steps, at, var, scale, buf):
                t, v, y, r = (buf[:, n, :] for n in range(4))
                k = at

                def link(ins):
                    nonlocal k
                    ins.then_inc(steps, 1)
                    k = k + 1
                    dve.wait_ge(steps, k)

                link(dve.tensor_scalar(v, var, scale, EPS, ALU.mult, ALU.add))
                link(dve.tensor_scalar(t.bitcast(i32), v.bitcast(i32), 1, None, ALU.arith_shift_right))
                link(dve.tensor_scalar(y.bitcast(i32), t.bitcast(i32), -1.0, float(RSQRT_MAGIC), ALU.mult, ALU.add))
                link(dve.tensor_scalar(v, v, -0.5, None, ALU.mult))
                for n in range(NEWTON):
                    link(dve.tensor_tensor(t, v, y, ALU.mult))
                    link(dve.tensor_tensor(t, t, y, ALU.mult))
                    dst = r if n == NEWTON - 1 else y
                    link(dve.scalar_tensor_tensor(dst, t, 1.5, y, ALU.add, ALU.mult))

            def layer_norm(g, src, stats, mv, buf, dst, steps, ready):
                at = LN_STEPS * g
                for b in range(PAIR):
                    dve.bn_stats(stats[:, b, :], src[:, b, :]).then_inc(steps, 1)
                dve.wait_ge(steps, at + PAIR)
                dve.memset(wait_carrier[:, :], 0.0)
                for b in range(PAIR):
                    dve.bn_aggr(mv[:, b, :], stats[:, b, :]).then_inc(steps, 1)
                dve.wait_ge(steps, at + 2 * PAIR)
                root(steps, at + 2 * PAIR, mv[:, :, 1], 1.0, buf)
                for b in range(PAIR):
                    dve.tensor_scalar(dst[:, b, :], src[:, b, :], mv[:, b, 0:1], buf[:, 3, b:b + 1],
                                      ALU.subtract, ALU.mult).then_inc(ready, 1)

            def row_max(g, b):
                dve.wait_ge(scores_done, 2 * g + b + 1)
                if not first(g):
                    dve.wait_ge(exp_ready, 4 * g)
                dve.tensor_reduce(neg_max[:, b, :], halves((FB[3], FB[0])[b]), X_AXIS, ALU.max, negate=True
                                  ).then_inc(max_ready, 1)

            def row_rcp(g, b):
                dve.wait_ge(exp_ready, 4 * g + 2 * b + 2)
                if not first(g):
                    dve.wait_ge(prob_ready, 2 * g)
                dve.reciprocal(prob_rcp[:, b, :], prob_sum[:, b, :]).then_inc(rcp_ready, 1)

            def attn_residual(g):
                dve.wait_ge(biases_loaded, 48)
                dve.wait_ge(attn_done, g + 1)
                if not first(g):
                    dve.wait_ge(xres_ready, g)
                    dve.wait_ge(xh_ready, 2 * g)
                dve.scalar_tensor_tensor(x2[:, :, :], halves(FB[3]), bv_col[:, 0:1], xin[:, :, :], ALU.add, ALU.add
                                         ).then_inc(x2_ready, 1)
                dve.wait_ge(x2_ready, g + 1)
                if not first(g):
                    dve.wait_ge(xh_turned, g)
                layer_norm(g, x2, st1, mv1, nwt1, xh, ln1_steps, xh_ready)

            def shift(g):
                dve.wait_ge(xn_ready, 2 * g + 2)
                dve.wait_ge(prev_ready, 2 * g + 2)
                if not first(g):
                    dve.wait_ge(mixed_ready[MIX_G], 2 * g)
                    dve.wait_ge(lora_done, g)
                dve.tensor_tensor(sx[:, :, :, :], xn[:, :, :, 0:L], xn[:, :, :, 1:], ALU.subtract
                                  ).then_inc(sx_ready, 1)
                dve.wait_ge(sx_ready, g + 1)
                for h in range(2):
                    dve.scalar_tensor_tensor(xmix[:, h, :].rearrange("p (b t) -> p b t", b=PAIR), sx[:, h, :, :],
                                             cols[:, h, R_MAAX:R_MAAX + 1], xn[:, h, :, 1:], ALU.mult, ALU.add
                                             ).then_inc(xmix_ready, 1)

            def mixed_(g, j, bank):
                dve.wait_ge(mix_done[j], g + 1)
                if not first(g):
                    dve.wait_ge(x5_ready[j], g)
                for h in range(2):
                    dve.scalar_tensor_tensor(mixed[:, j, h, :], halves(bank)[:, h, :],
                                             cols[:, h, R_STACK + j:R_STACK + j + 1],
                                             sx[:, h, :, :].rearrange("p b t -> p (b t)"), ALU.add, ALU.mult
                                             ).then_inc(mixed_ready[j], 1)

            def gate_(g):
                dve.wait_ge(gate_th_ready, g + 1)
                if not first(g):
                    dve.wait_ge(ag_ready, g)
                dve.scalar_tensor_tensor(gate[:, :, :], gate_th[:, :, :], 1.0, halves(FB[0]), ALU.add, ALU.mult
                                         ).then_inc(gate_ready, 1)

            def scan_start(g):
                dve.wait_ge(x2_ready, g + 1)
                if not first(g):
                    dve.wait_ge(x3_ready, g)
                dve.tensor_copy(xres[:, :, :], x2[:, :, :]).then_inc(xres_ready, 1)
                dve.wait_ge(s0_loaded, 16 * PAIR * (g + 1))
                if not first(g):
                    dve.wait_ge(state_ready, UNITS * g)
                for h in range(2):
                    i = dve.tensor_copy(kv[:, h, :, :, 0], s0[:, h, :, :].rearrange("p b d -> p d b"))
                i.then_inc(s0_placed, 1)

            def scan_kv(g, u):
                h, d0 = u // 4, 2 * (u % 4)
                dve.wait_ge(v_spread, UNITS * g + u + 1)
                if u == 0:
                    dve.wait_ge(kf_ready, g + 1)
                    dve.wait_ge(s0_placed, g + 1)
                    dve.wait_ge(w_ready_s, 2 * g + 2)
                    if not first(g):
                        dve.wait_ge(state_ready, UNITS * g)
                dve.tensor_tensor(kv[:, h, d0:d0 + 2, :, 1:], quarters(BB[u % 2])[:, :, :, 0:L - 1],
                                  kf[:, h, :, 0:L - 1].unsqueeze(1).broadcast_to([128, 2, PAIR, L - 1]), ALU.mult
                                  ).then_inc(kv_ready, 1)

            def scan_state(g, u):
                h, d0 = u // 4, 2 * (u % 4)
                dve.wait_ge(kv_ready, UNITS * g + u + 1)
                if u >= 2:
                    dve.wait_ge(rs_ready, UNITS * g + u - 1)
                elif not first(g):
                    dve.wait_ge(rs_ready, UNITS * g)
                dve.tensor_tensor_scan(state[:, u % 2, :, :, :].rearrange("p d b t -> p (d b t)"),
                                       w_prev[:, h, :, :, :].rearrange("p d b t -> p (d b t)"),
                                       kv[:, h, d0:d0 + 2, :, :].rearrange("p d b t -> p (d b t)"),
                                       0.0, ALU.mult, ALU.add).then_inc(state_ready, 1)

            def scan_out(g, u):
                h, d0 = u // 4, 2 * (u % 4)
                dve.wait_ge(rs_turned, 9 * g + u + 2)
                if u == 0 and not first(g):
                    dve.wait_ge(att1_ready, g)
                    dve.wait_ge(head_sum_ready, g)
                dve.tensor_reduce(att[:, :, HH * h:HH * (h + 1), d0:d0 + 2].rearrange("p b h d -> p b d h"),
                                  quarters(BB[2 + (u + 1) % 2]).rearrange("p b d (h k) -> p b d h k", k=S),
                                  X_AXIS, ALU.add).then_inc(head_out_ready, 1)

            def bonus_out(g):
                dve.wait_ge(rs_turned, 9 * g + 1)
                if not first(g):
                    dve.wait_ge(cv_ready, g)
                dve.tensor_reduce(bonus[:, :, :].rearrange("p b (a h) -> p b a h", a=2),
                                  quarters(BB[2]).rearrange("p b a (h k) -> p b a h k", k=S),
                                  X_AXIS, ALU.add).then_inc(head_out_ready, 1)

            def group_norm(g):
                dve.wait_ge(att1_ready, g + 1)
                if not first(g):
                    dve.wait_ge(att_c_ready, g)
                dve.tensor_reduce(head_sum[:, :], att1[:, :, :, :].rearrange("p b h s -> p (b h) s"), X_AXIS,
                                  ALU.add).then_inc(gn_sum, 1)
                dve.wait_ge(gn_sum, g + 1)
                dve.tensor_scalar(head_sum[:, :], head_sum[:, :], -1.0 / S, None, ALU.mult).then_inc(head_sum_ready, 1)
                dve.wait_ge(sq_ready, g + 1)
                if not first(g):
                    dve.wait_ge(att_n_ready, g)
                dve.tensor_reduce(head_var[:, :], sq[:, :, :, :].rearrange("p b h s -> p (b h) s"), X_AXIS,
                                  ALU.add).then_inc(gn_steps, 1)
                at = (RS + 1) * g + 1
                dve.wait_ge(gn_steps, at)
                root(gn_steps, at, head_var[:, :], 1.0 / S, nwt2)

            def residual(g):
                dve.wait_ge(o_done, g + 1)
                dve.wait_ge(xres_ready, g + 1)
                if not first(g):
                    dve.wait_ge(x4_ready, g)
                dve.tensor_tensor(x3[:, :, :], halves(BB[1]), xres[:, :, :], ALU.add).then_inc(x3_ready, 1)
                dve.wait_ge(x3_ready, g + 1)
                if not first(g):
                    dve.wait_ge(xh2_turned, g)
                layer_norm(g, x3, st2, mv2, nwt3, xh2, ln2_steps, xh2_ready)

            def shift2(g):
                dve.wait_ge(xn2_ready, 2 * g + 2)
                dve.wait_ge(prev2_ready, g + 1)
                if not first(g):
                    dve.wait_ge(xk_ready, 2 * g)
                    dve.wait_ge(xr_ready, 2 * g)
                    dve.wait_ge(fk_done, g)
                    dve.wait_ge(fr_done, g)
                dve.tensor_tensor(sx2[:, :, :, :], xn2[:, :, :, 0:L], xn2[:, :, :, 1:], ALU.subtract
                                  ).then_inc(sx2_ready, 1)
                dve.wait_ge(sx2_ready, g + 1)
                for row, dst, ready in ((R_FK, xk, xk_ready), (R_FR, xr, xr_ready)):
                    for h in range(2):
                        dve.scalar_tensor_tensor(dst[:, h, :].rearrange("p (b t) -> p b t", b=PAIR), sx2[:, h, :, :],
                                                 cols[:, h, row:row + 1], xn2[:, h, :, 1:], ALU.mult, ALU.add
                                                 ).then_inc(ready, 1)

            def ffn_out(g):
                dve.wait_ge(fv_done, g + 1)
                dve.wait_ge(th2_ready, g + 1)
                if not first(g):
                    dve.wait_ge(x4_ready, g)
                dve.scalar_tensor_tensor(ffn[:, :, :], th2[:, :, :], 1.0, halves(BB[1]), ALU.add, ALU.mult
                                         ).then_inc(ffn_ready, 1)
                dve.wait_ge(ffn_ready, g + 1)
                if not first(g):
                    dve.wait_ge(stored, 16 * g)
                dve.scalar_tensor_tensor(x4[:, :, :], ffn[:, :, :], 0.5, x3[:, :, :], ALU.mult, ALU.add
                                         ).then_inc(x4_ready, 1)

            def scan(g, lo, hi):
                for u in range(lo, hi):
                    if u < UNITS:
                        scan_kv(g, u)
                        scan_state(g, u)
                    if u == 0:
                        bonus_out(g)
                    if u >= 2:
                        scan_out(g, u - 2)

            def body(f, b):
                if f is not None:
                    row_max(f, 0)
                    row_max(f, 1)
                    row_rcp(f, 0)
                    row_rcp(f, 1)
                if b is not None:
                    scan_start(b)
                    scan(b, 0, 2)
                if f is not None:
                    attn_residual(f)
                if b is not None:
                    scan(b, 2, 4)
                if f is not None:
                    shift(f)
                if b is not None:
                    scan(b, 4, UNITS + 2)
                    group_norm(b)
                if f is not None:
                    mixed_(f, MIX_W, FB[3])
                    mixed_(f, MIX_K, FB[2])
                    mixed_(f, MIX_R, FB[1])
                    mixed_(f, MIX_V, FB[2])
                    mixed_(f, MIX_G, FB[3])
                if b is not None:
                    residual(b)
                if f is not None:
                    gate_(f)
                if b is not None:
                    shift2(b)
                    ffn_out(b)

            body(0, None)
            body(1, 0)
            with dve.Fori(2, G) as i:
                body(i, i - 1)
            body(None, G - 1)


_INS = ["x", "ctx_2048", "L0_xattn_Wq", "L0_xattn_bq", "L0_xattn_Wk", "L0_xattn_bk", "L0_xattn_Wv", "L0_xattn_bv",
        "L1_xattn_ln1_w", "L1_xattn_ln1_b", "L1_xattn_ln2_w", "L1_xattn_ln2_b", "L1_xattn_maa_x",
        "L1_xattn_maa_w1", "L1_xattn_maa_w2", "L1_xattn_maa_stack", "L1_xattn_time_decay", "L1_xattn_decay_w1",
        "L1_xattn_decay_w2", "L1_xattn_faaaa", "L1_xattn_Wr", "L1_xattn_Wk", "L1_xattn_Wv", "L1_xattn_Wg",
        "L1_xattn_Wo", "L1_xattn_gn_w", "L1_xattn_gn_b", "L1_xattn_ffn_maa_k", "L1_xattn_ffn_maa_r",
        "L1_xattn_ffn_Wk", "L1_xattn_ffn_Wr", "L1_xattn_ffn_Wv"]


def kernel(**inputs):
    import numpy as _np
    import concourse.bacc as _bacc
    from concourse import mybir as _mybir
    from concourse.bass_utils import run_bass_kernel_spmd as _run

    nc = _bacc.Bacc("TRN2", target_bir_lowering=False, num_devices=1)
    arrays, args = {}, []
    for name in _INS:
        a = _np.ascontiguousarray(inputs[name])
        arrays[f"in_{name}"] = a
        args.append(nc.dram_tensor(f"in_{name}", a.shape, _mybir.dt.from_np(a.dtype), kind="ExternalInput").ap())
    args.append(nc.dram_tensor("out_0", inputs["x"].shape, _mybir.dt.float32, kind="ExternalOutput").ap())
    xattn_rwkv(nc, *args)
    r = _run(nc, [arrays], core_ids=[0])
    return r.results[0]["out_0"]
```

```python
import concourse.bass as bass
from concourse import mybir
from contextlib import ExitStack


def xattn_rwkv(nc: bass.Bass, x, ctx_2048, Wq, bq, Wk, bk, Wv, bv, ln1_w, ln1_b, ln2_w, ln2_b, maa_x, maa_w1,
               maa_w2, maa_stack, time_decay, decay_w1, decay_w2, faaaa, Wr, Wkey, Wval, Wg, Wo, gn_w, gn_b,
               ffn_maa_k, ffn_maa_r, ffn_Wk, ffn_Wr, ffn_Wv, out):
    f32, i32 = mybir.dt.float32, mybir.dt.int32
    ALU = mybir.AluOpType
    ACT = mybir.ActivationFunctionType
    X_AXIS = mybir.AxisListType.X

    B, L, E = x.shape
    D = Wq.shape[0]
    H, S = faaaa.shape
    HALVES = E // 128
    HH = H // HALVES
    PAIR = 2
    G = B // PAIR
    T = PAIR * L
    MIXES, LORA, _ = maa_w2.shape
    MIX_K, MIX_W, MIX_V, MIX_R, MIX_G = range(MIXES)
    DECAY = decay_w1.shape[1]
    UNITS = HALVES * S // 2
    EPS = 1e-5
    RSQRT_MAGIC = 0x5F3759DF

    ctx = ExitStack()
    with ctx:
        def sb(name, shape, dt=f32):
            return ctx.enter_context(nc.sbuf_tensor(name, shape, dt))

        def sem(name):
            return ctx.enter_context(nc.semaphore(name))

        ident = sb("ident", [128, 128])
        w_nat = sb("w_nat", [128, 8, 2, E])
        wT = sb("wT", [128, 8, 2, E])
        WR, WK, WV, WG, WO, FK, FR, FV = range(8)
        attn_nat = sb("attn_nat", [D, 2, L])
        attn_T = sb("attn_T", [L, 2, D])
        v0_nat = sb("v0_nat", [L, L])
        v0_T = sb("v0_T", [L, L])
        bqk = sb("bqk", [D, 2])
        bv_col = sb("bv_col", [L, 1])
        mw1 = sb("mw1", [128, 2, MIXES * LORA])
        mw2 = sb("mw2", [4 * LORA, E])
        mw2_last = sb("mw2_last", [LORA, E])
        dw1 = sb("dw1", [128, 2, DECAY])
        dw2 = sb("dw2", [DECAY, E])
        ROWS = 11 + MIXES
        rows = sb("rows", [ROWS, E])
        cols = sb("cols", [128, 2, ROWS])
        (R_LN1W, R_LN1B, R_LN2W, R_LN2B, R_MAAX, R_DECAY, R_U, R_GNW, R_GNB, R_FK, R_FR) = range(11)
        R_STACK = 11
        gn_half = sb("gn_half", [128, 2, 2])

        state_rows = sb("state_rows", [2 * B, E])
        prev_cols = sb("prev_cols", [128, 2, 2, B])
        s0 = sb("s0", [128, 2, B, S])
        x2_all = sb("x2_all", [L, B, E])

        xin = sb("xin", [L, PAIR, E])
        cin = sb("cin", [L, PAIR, E])
        qk = sb("qk", [D, 2, PAIR * E])
        vT = sb("vT", [128, PAIR, 2, L])
        neg_max = sb("neg_max", [128, PAIR, 2])
        prob = sb("prob", [128, PAIR, 2, E])
        prob_sum = sb("prob_sum", [128, PAIR, 2])
        prob_rcp = sb("prob_rcp", [128, PAIR, 2])
        probT = sb("probT", [128, PAIR, 2, E])
        x2 = sb("x2", [L, PAIR, E])
        st1 = sb("st1", [128, PAIR, 6])
        mv1 = sb("mv1", [128, PAIR, 2])
        wait_carrier = sb("wait_carrier", [128, 1])
        minus_half = sb("minus_half", [128, PAIR])
        ve1 = sb("ve1", [128, PAIR])
        rstd1 = sb("rstd1", [128, PAIR])
        xh = sb("xh", [L, PAIR, E])
        xn = sb("xn", [128, 2, PAIR, L + 1])
        sx = sb("sx", [128, 2, PAIR, L])
        xmix = sb("xmix", [128, 2, T])
        lora = sb("lora", [4 * LORA, T])
        lora_last = sb("lora_last", [LORA, T])
        mixed = sb("mixed", [128, MIXES, 2, T])
        x5 = sb("x5", [128, MIXES, 2, T])
        wt = sb("wt", [DECAY, T])
        e1 = sb("e1", [128, 2, PAIR, L])
        gate_th = sb("gate_th", [128, 2, T])

        kf = sb("kf", [128, 2, PAIR, L])
        rf = sb("rf", [128, 2, PAIR, L])
        w_prev = sb("w_prev", [128, 2, 2, PAIR, L])
        v_tok = sb("v_tok", [L, PAIR, E])
        v_exp = sb("v_exp", [L, PAIR, 2, S, 128])
        gate = sb("gate", [128, 2, T])

        kv = sb("kv", [128, 2, S, PAIR, L])
        state = sb("state", [128, 2, 2, PAIR, L])
        rs = sb("rs", [128, 2, 2, PAIR, L])
        ru = sb("ru", [128, 2, T])
        ruk = sb("ruk", [128, 2, T])
        bonus = sb("bonus", [L, PAIR, H])
        att = sb("att", [L, PAIR, H, S])
        cv = sb("cv", [L, PAIR, H, S])
        att1 = sb("att1", [L, PAIR, H, S])
        head_sum = sb("head_sum", [L, PAIR * H])
        att_c = sb("att_c", [L, PAIR, H, S])
        sq = sb("sq", [L, PAIR, H, S])
        head_var = sb("head_var", [L, PAIR * H])
        nwt2 = sb("nwt2", [L, 4, PAIR * H])
        att_n = sb("att_n", [L, PAIR, H, S])
        att_f = sb("att_f", [128, 2, T])
        ag = sb("ag", [128, 2, T])
        x3 = sb("x3", [L, PAIR, E])
        st2 = sb("st2", [128, PAIR, 6])
        mv2 = sb("mv2", [128, PAIR, 2])
        ve2 = sb("ve2", [128, PAIR])
        rstd2 = sb("rstd2", [128, PAIR])
        xh2 = sb("xh2", [L, PAIR, E])
        xn2 = sb("xn2", [128, 2, PAIR, L + 1])
        sx2 = sb("sx2", [128, 2, PAIR, L])
        xk = sb("xk", [128, 2, T])
        xr = sb("xr", [128, 2, T])
        relu = sb("relu", [128, 2, T])
        kk = sb("kk", [128, 2, T])
        th2 = sb("th2", [L, PAIR, E])
        ffn = sb("ffn", [L, PAIR, E])
        x4 = sb("x4", [L, PAIR, E])

        FB = [ctx.enter_context(nc.psum_tensor(f"front_bank{i}", [128, 512], f32)) for i in range(4)]
        BB = [ctx.enter_context(nc.psum_tensor(f"back_bank{i}", [128, 512], f32)) for i in range(4)]

        def quarters(bank):
            return bank[:, :].rearrange("p (a b n) -> p a b n", a=2, b=2)

        def halves(bank):
            return bank[:, :].rearrange("p (a n) -> p a n", a=2)

        w_loaded = [sem(f"w{n}_loaded") for n in range(8)]
        attn_w_loaded, v0_loaded, rows_loaded = sem("attn_w_loaded"), sem("v0_loaded"), sem("rows_loaded")
        lora_loaded, more_rows_loaded = sem("lora_loaded"), sem("more_rows_loaded")
        biases_loaded = sem("biases_loaded")
        ident_ready, ident_zero = sem("ident_ready"), sem("ident_zero")
        w_turned, w_ready = sem("w_turned"), sem("w_ready")
        gn_half_ready, prev_cols_ready = sem("gn_half_ready"), sem("prev_cols_ready")
        w_prev_zero = sem("w_prev_zero")
        x_loaded, ctx_loaded = sem("x_loaded"), sem("ctx_loaded")
        state_rows_loaded, s0_loaded = sem("state_rows_loaded"), sem("s0_loaded")
        q_done, k_done, v_done = sem("q_done"), sem("k_done"), sem("v_done")
        qk_ready, vT_ready = sem("qk_ready"), sem("vT_ready")
        scores_done = sem("scores_done")
        max_ready = sem("max_ready")
        exp_ready = sem("exp_ready")
        rcp_ready = sem("rcp_ready")
        prob_ready = sem("prob_ready")
        prob_turned = sem("prob_turned")
        probT_ready = sem("probT_ready")
        rstd1_ready, rstd2_ready = sem("rstd1_ready"), sem("rstd2_ready")
        minus_half_ready = sem("minus_half_ready")
        attn_done = sem("attn_done")
        x2_ready = sem("x2_ready")
        ln1_steps = sem("ln1_steps")
        xh_ready = sem("xh_ready")
        xh_turned = sem("xh_turned")
        xn_ready, prev_ready = sem("xn_ready"), sem("prev_ready")
        sx_ready, xmix_ready = sem("sx_ready"), sem("xmix_ready")
        lora_done, lora_ready = sem("lora_done"), sem("lora_ready")
        mix_done = [sem(f"mix{j}_done") for j in range(MIXES)]
        mixed_ready = [sem(f"mixed{j}_ready") for j in range(MIXES)]
        x5_ready = [sem(f"x5_{j}_ready") for j in range(MIXES)]
        dlora_done, wt_ready = sem("dlora_done"), sem("wt_ready")
        decay_done, e1_ready, w_ready_s = sem("decay_done"), sem("e1_ready"), sem("decay_ready")
        kp_done, kf_ready = sem("kp_done"), sem("kf_ready")
        rp_done, rf_ready = sem("rp_done"), sem("rf_ready")
        vp_done, v_exp_ready, v_tok_ready = sem("vp_done"), sem("v_exp_ready"), sem("v_tok_ready")
        gp_done, gate_th_ready, gate_ready = sem("gp_done"), sem("gate_th_ready"), sem("gate_ready")
        x2_kept, s0_placed = sem("x2_kept"), sem("s0_placed")
        v_spread = sem("v_spread")
        kv_ready, state_ready = sem("kv_ready"), sem("state_ready")
        rs_ready = sem("rs_ready")
        ru_ready, ruk_ready = sem("ru_ready"), sem("ruk_ready")
        rs_turned = sem("rs_turned")
        head_out_ready = sem("head_out_ready")
        cv_ready, att1_ready = sem("cv_ready"), sem("att1_ready")
        head_sum_ready, att_c_ready, sq_ready = sem("head_sum_ready"), sem("att_c_ready"), sem("sq_ready")
        gn_sum, gn_steps = sem("gn_sum"), sem("gn_steps")
        att_n_ready = sem("att_n_ready")
        att_turned, att_f_ready, ag_ready = sem("att_turned"), sem("att_f_ready"), sem("ag_ready")
        o_done, x3_ready = sem("o_done"), sem("x3_ready")
        ln2_steps, xh2_ready = sem("ln2_steps"), sem("xh2_ready")
        xh2_turned, xn2_ready, prev2_ready = sem("xh2_turned"), sem("xn2_ready"), sem("prev2_ready")
        sx2_ready, xk_ready, xr_ready = sem("sx2_ready"), sem("xk_ready"), sem("xr_ready")
        fk_done, relu_ready, kk_ready = sem("fk_done"), sem("relu_ready"), sem("kk_ready")
        fr_done, th2_ready = sem("fr_done"), sem("th2_ready")
        fv_done, ffn_ready, x4_ready = sem("fv_done"), sem("ffn_ready"), sem("x4_ready")
        stored = sem("stored")
        RS = 11
        SPREAD = 0.375 ** -4
        LN_STEPS = 2 * PAIR + 1

        BACK_STEPS = (
            (UNITS, (v_spread, kv_ready, state_ready, rs_ready)),
            (1, (rstd2_ready, ru_ready, ruk_ready, cv_ready, att1_ready, head_sum_ready, att_c_ready,
                sq_ready, gn_sum, att_n_ready, att_turned, ag_ready, o_done, x3_ready,
                xh2_turned, prev2_ready, sx2_ready, fk_done, relu_ready, kk_ready, fr_done,
                th2_ready, fv_done, ffn_ready, x4_ready, s0_placed)),
            (UNITS + 1, (rs_turned, head_out_ready)),
            (RS + 1, (gn_steps,)),
            (2, (att_f_ready, xh2_ready, xn2_ready, xk_ready, xr_ready)),
            (LN_STEPS, (ln2_steps,)),
        )

        block = ctx.enter_context(nc.Block())

        @block.sync
        def _(sp):
            sp.dma_start(attn_nat[:, 0, :], Wq).then_inc(attn_w_loaded, 16)
            sp.dma_start(attn_nat[:, 1, :], Wk).then_inc(attn_w_loaded, 16)
            sp.dma_start(xin[:, :, :], x[0:PAIR, :, :].rearrange("b c n -> c b n")).then_inc(x_loaded, 16)
            sp.dma_start(cin[:, :, :], ctx_2048[0:PAIR, :, :].rearrange("b c n -> c b n")).then_inc(ctx_loaded, 16)
            sp.dma_start(v0_nat[:, :], Wv).then_inc(v0_loaded, 16)
            for n, w in enumerate((Wr, Wkey, Wval, Wg, Wo, ffn_Wk, ffn_Wr, ffn_Wv)):
                if n == 4:
                    for r, vec in ((R_MAAX, maa_x), (R_DECAY, time_decay), (R_GNW, gn_w), (R_GNB, gn_b),
                                   (R_FK, ffn_maa_k), (R_FR, ffn_maa_r)):
                        sp.dma_start(rows[r:r + 1, :], vec.rearrange("(a e) -> a e", a=1)
                                     ).then_inc(more_rows_loaded, 16)
                sp.dma_start(w_nat[:, n, :, :], w.rearrange("(h p) e -> p h e", p=128)).then_inc(w_loaded[n], 16)
            sp.dma_start(mw1[:, :, :], maa_w1.rearrange("(h p) n -> p h n", p=128)).then_inc(lora_loaded, 16)
            sp.dma_start(mw2[:, :], maa_w2[0:4, :, :].rearrange("j i e -> (j i) e")).then_inc(lora_loaded, 16)
            sp.dma_start(mw2_last[:, :], maa_w2[4, :, :]).then_inc(lora_loaded, 16)
            sp.dma_start(dw1[:, :, :], decay_w1.rearrange("(h p) n -> p h n", p=128)).then_inc(lora_loaded, 16)
            sp.dma_start(dw2[:, :], decay_w2).then_inc(lora_loaded, 16)
            sp.dma_start(state_rows[:, :], ctx_2048[:, 0:2, :]).then_inc(state_rows_loaded, 16)
            for b in range(B):
                sp.dma_start(s0[:, :, b, :], ctx_2048[b, 2:2 + S, :].rearrange("(h r) (p s) -> (r p) h s", h=2, s=S)
                             ).then_inc(s0_loaded, 16)

            with sp.Fori(1, G) as g:
                sp.wait_ge(x2_ready, g)
                sp.dma_start(xin[:, :, :], x[bass.ds(PAIR * g, PAIR), :, :].rearrange("b c n -> c b n")
                             ).then_inc(x_loaded, 16)
                sp.wait_ge(v_done, g)
                sp.dma_start(cin[:, :, :], ctx_2048[bass.ds(PAIR * g, PAIR), :, :].rearrange("b c n -> c b n")
                             ).then_inc(ctx_loaded, 16)

        @block.gpsimd
        def _(pool):
            pool.memset(ident[:, :], 0.0).then_inc(ident_zero, 1)
            pool.dma_start(bqk[:, 0:1], bq.rearrange("(d a) -> d a", a=1)).then_inc(biases_loaded, 16)
            pool.dma_start(bqk[:, 1:2], bk.rearrange("(d a) -> d a", a=1)).then_inc(biases_loaded, 16)
            pool.dma_start(bv_col[:, :], bv.rearrange("(d a) -> d a", a=1)).then_inc(biases_loaded, 16)
            pool.wait_ge(ident_zero, 1)
            pool.affine_select(out=ident[:, :], in_=ident[:, :], compare_op=ALU.not_equal, fill=1.0, base=0,
                               pattern=[[-1, 128]], channel_multiplier=1).then_inc(ident_ready, 1)
            pool.memset(w_prev[:, :, :, :, 0], 0.0).then_inc(w_prev_zero, 1)
            for r, vec in ((R_LN1W, ln1_w), (R_LN1B, ln1_b), (R_LN2W, ln2_w), (R_LN2B, ln2_b)):
                pool.dma_start(rows[r:r + 1, :], vec.rearrange("(a e) -> a e", a=1)).then_inc(rows_loaded, 16)
            pool.dma_start(rows[R_U:R_U + 1, :], faaaa.rearrange("h s -> (h s)").rearrange("(a e) -> a e", a=1)
                         ).then_inc(rows_loaded, 16)
            pool.dma_start(rows[R_STACK:ROWS, :], maa_stack).then_inc(rows_loaded, 16)
            pool.memset(minus_half[:, :], -0.5).then_inc(minus_half_ready, 1)
            for per_group, steps in BACK_STEPS:
                for step in steps:
                    pool.nop().then_inc(step, per_group)

            def first(g):
                return isinstance(g, int) and g == 0

            def normalise(g, b):
                pool.wait_ge(rcp_ready, 2 * g + b + 1)
                pool.tensor_tensor(prob[:, b, :, :], prob[:, b, :, :],
                                   prob_rcp[:, b, :].unsqueeze(2).broadcast_to([128, 2, E]), ALU.mult
                                   ).then_inc(prob_ready, 1)

            def root(ve, count, rstd, ready):
                pool.wait_ge(minus_half_ready, 1)
                pool.wait_ge(*count)
                pool.tensor_tensor(rstd[:, :], ve[:, :], minus_half[:, :], ALU.pow).then_inc(ready, 1)

            def root1(g):
                if not first(g):
                    pool.wait_ge(xh_ready, PAIR * g)
                root(ve1, (ln1_steps, LN_STEPS * (g + 1)), rstd1, rstd1_ready)

            def root2(g):
                pool.wait_ge(xh2_ready, PAIR * (g + 1))
                root(ve2, (ln2_steps, LN_STEPS * (g + 2)), rstd2, rstd2_ready)

            def add_xn(g, j):
                pool.wait_ge(mixed_ready[j], 2 * g + 2)
                pool.wait_ge(xn_ready, 2 * g + 2)
                if not first(g):
                    pool.wait_ge([kp_done, dlora_done, vp_done, rp_done, gp_done][j], g)
                pool.tensor_tensor(x5[:, j, :, :].rearrange("p h (b t) -> p h b t", b=PAIR),
                                   mixed[:, j, :, :].rearrange("p h (b t) -> p h b t", b=PAIR),
                                   xn[:, :, :, 1:], ALU.add).then_inc(x5_ready[j], 1)

            def scan_start(g):
                pool.wait_ge(rf_ready, g + 1)
                if not first(g):
                    pool.wait_ge(ruk_ready, g + 1)
                pool.wait_ge(w_ready, 3)
                pool.tensor_tensor(ru[:, :, :], rf[:, :, :, :].rearrange("p h b t -> p h (b t)"),
                                   cols[:, :, R_U:R_U + 1].broadcast_to([128, 2, T]), ALU.mult).then_inc(ru_ready, 1)
                pool.wait_ge(ru_ready, g + 2)
                pool.wait_ge(kf_ready, g + 1)
                if not first(g):
                    pool.wait_ge(rs_turned, 9 * (g + 1))
                pool.tensor_tensor(ruk[:, :, :], ru[:, :, :], kf[:, :, :, :].rearrange("p h b t -> p h (b t)"),
                                   ALU.mult).then_inc(ruk_ready, 1)

            def scan(g, u):
                h = u // 4
                pool.wait_ge(state_ready, UNITS * (g + 1) + u + 1)
                if u >= 2:
                    pool.wait_ge(rs_turned, 9 * (g + 1) + u)
                elif not first(g):
                    pool.wait_ge(rs_turned, 9 * (g + 1))
                pool.tensor_tensor(rs[:, u % 2, :, :, :].rearrange("p d b t -> p d (b t)"),
                                   state[:, u % 2, :, :, :].rearrange("p d b t -> p d (b t)"),
                                   rf[:, h, :, :].rearrange("p b t -> p (b t)").unsqueeze(1).broadcast_to([128, 2, T]),
                                   ALU.mult).then_inc(rs_ready, 1)

            def present_v(g):
                pool.wait_ge(head_out_ready, 9 * (g + 1) + 1)
                pool.wait_ge(v_tok_ready, g + 1)
                pool.wait_ge(att1_ready, g + 1)
                pool.tensor_tensor(cv[:, :, :, :], v_tok[:, :, :].rearrange("p b (h s) -> p b h s", s=S),
                                   bonus[:, :, :].unsqueeze(3).broadcast_to([L, PAIR, H, S]), ALU.mult
                                   ).then_inc(cv_ready, 1)

            def body(m, s, a):
                if s is not None:
                    scan(s, 3)
                    scan(s, 4)
                if m is not None:
                    add_xn(m, MIX_W)
                if s is not None:
                    present_v(s)
                if m is not None:
                    add_xn(m, MIX_K)
                if s is not None:
                    scan(s, 5)
                if m is not None:
                    add_xn(m, MIX_R)
                if s is not None:
                    scan(s, 6)
                    scan(s, 7)
                if a is not None:
                    normalise(a, 0)
                if m is not None:
                    add_xn(m, MIX_V)
                if a is not None:
                    normalise(a, 1)
                if m is not None:
                    add_xn(m, MIX_G)
                    scan_start(m)
                if a is not None:
                    root1(a)
                if m is not None:
                    scan(m, 0)
                    scan(m, 1)
                if s is not None:
                    root2(s)
                if m is not None:
                    scan(m, 2)

            normalise(0, 0)
            normalise(0, 1)
            root1(0)
            add_xn(0, MIX_W)
            add_xn(0, MIX_K)
            add_xn(0, MIX_R)
            normalise(1, 0)
            normalise(1, 1)
            add_xn(0, MIX_V)
            add_xn(0, MIX_G)
            scan_start(0)
            root1(1)
            scan(0, 0)
            scan(0, 1)
            scan(0, 2)
            with pool.Fori(1, G - 1) as i:
                body(i, i - 1, i + 1)
            body(G - 1, G - 2, None)
            body(None, G - 1, None)

        @block.scalar
        def _(act):
            def ready_attn_weights():
                act.wait_ge(w_turned, 1)
                act.activation(attn_T[:, :, :], FB[0][:, 0:2 * D].rearrange("p (a d) -> p a d", a=2), ACT.Copy
                               ).then_inc(w_ready, 1)
                act.wait_ge(w_turned, 2)
                act.activation(v0_T[:, :], FB[3][:, 0:L], ACT.Copy).then_inc(w_ready, 1)

            def ready_rows():
                act.wait_ge(w_turned, 3)
                act.activation(cols[:, :, :], FB[2][:, 0:2 * ROWS].rearrange("p (a r) -> p a r", a=2), ACT.Copy
                               ).then_inc(w_ready, 1)
                act.activation(prev_cols[:, :, :, :],
                               FB[2][:, 128:128 + 4 * B].rearrange("p (h b r) -> p r h b", h=2, r=2), ACT.Copy
                               ).then_inc(prev_cols_ready, 1)
                act.wait_ge(w_ready, 3)
                act.activation(gn_half[:, :, :], cols[:, :, R_GNW:R_GNB + 1], ACT.Copy, scale=0.5
                               ).then_inc(gn_half_ready, 1)

            def ready_weights(lo, hi):
                for n in range(lo, hi):
                    act.wait_ge(w_turned, 4 + n)
                    act.activation(wT[:, n, :, :], halves(BB[n % 4]), ACT.Copy).then_inc(w_ready, 1)

            def first(g):
                return isinstance(g, int) and g == 0

            def attn_in(g):
                act.wait_ge(biases_loaded, 48)
                act.wait_ge(q_done, g + 1)
                if not first(g):
                    act.wait_ge(scores_done, 2 * g)
                act.activation(qk[:, 0, :], FB[0][0:D, :], ACT.Identity, bias=bqk[:, 0:1]).then_inc(qk_ready, 1)
                act.wait_ge(k_done, g + 1)
                act.activation(qk[:, 1, :], FB[1][0:D, :], ACT.Identity, bias=bqk[:, 1:2]).then_inc(qk_ready, 1)
                act.wait_ge(v_done, g + 1)
                if not first(g):
                    act.wait_ge(attn_done, g)
                act.activation(vT[:, :, :, :], quarters(FB[0]), ACT.Copy).then_inc(vT_ready, 1)

            def softmax(g, b):
                act.wait_ge(max_ready, 2 * g + b + 1)
                if not first(g):
                    act.wait_ge(prob_turned, 2 * g)
                bank = FB[1 - b]
                for nt in range(2):
                    act.activation(prob[:, b, nt, :], halves(bank)[:, nt, :], ACT.Exp, bias=neg_max[:, b, nt:nt + 1],
                                   accum_out=prob_sum[:, b, nt:nt + 1]).then_inc(exp_ready, 1)

            def prob_evacuate(g, b):
                act.wait_ge(prob_turned, 2 * g + b + 1)
                if not first(g):
                    act.wait_ge(attn_done, g)
                act.activation(probT[:, b, :, :], halves(FB[1 - b]), ACT.Copy).then_inc(probT_ready, 1)

            def norm_evacuate(g):
                act.wait_ge(w_ready, 3)
                act.wait_ge(xh_turned, g + 1)
                if not first(g):
                    for j in range(MIXES):
                        act.wait_ge(x5_ready[j], g)
                for h in range(2):
                    act.activation(xn[:, h, :, 1:], quarters(FB[0])[:, h, :, :], ACT.Identity,
                                   bias=cols[:, h, R_LN1B:R_LN1B + 1], scale=cols[:, h, R_LN1W:R_LN1W + 1]
                                   ).then_inc(xn_ready, 1)

            def lora_tanh(g):
                act.wait_ge(lora_done, g + 1)
                if not first(g):
                    for j in range(MIXES):
                        act.wait_ge(mix_done[j], g)
                act.activation(lora[:, :], FB[1][:, 0:T], ACT.Tanh).then_inc(lora_ready, 1)
                act.activation(lora_last[:, :], FB[1][0:LORA, T:2 * T], ACT.Tanh).then_inc(lora_ready, 1)

            def decay_tanh(g):
                act.wait_ge(dlora_done, g + 1)
                if not first(g):
                    act.wait_ge(decay_done, g)
                act.activation(wt[:, :], FB[3][0:DECAY, 0:T], ACT.Tanh).then_inc(wt_ready, 1)

            def decay(g):
                act.wait_ge(decay_done, g + 1)
                if not first(g):
                    act.wait_ge(w_ready_s, 2 * g)
                for h in range(2):
                    act.activation(e1[:, h, :, :].rearrange("p b t -> p (b t)"), halves(FB[3])[:, h, :], ACT.Exp,
                                   bias=cols[:, h, R_DECAY:R_DECAY + 1]).then_inc(e1_ready, 1)

            def decay_outer(g):
                act.wait_ge(e1_ready, 2 * g + 2)
                act.wait_ge(w_prev_zero, 1)
                if not first(g):
                    act.wait_ge(state_ready, UNITS * (g + 1))
                for d in range(2):
                    act.activation(w_prev[:, :, d, :, 1:], e1[:, :, :, 0:L - 1], ACT.Exp, scale=-1.0
                                   ).then_inc(w_ready_s, 1)

            def evacuate_k(g):
                act.wait_ge(kp_done, g + 1)
                if not first(g):
                    act.wait_ge(kv_ready, UNITS * (g + 1))
                    act.wait_ge(ruk_ready, g + 1)
                act.activation(kf[:, :, :, :], quarters(FB[2]), ACT.Copy).then_inc(kf_ready, 1)

            def evacuate_r(g):
                act.wait_ge(rp_done, g + 1)
                if not first(g):
                    act.wait_ge(rs_ready, UNITS * (g + 1))
                act.activation(rf[:, :, :, :], quarters(FB[3]), ACT.Copy).then_inc(rf_ready, 1)

            def evacuate_v(g):
                act.wait_ge(vp_done, g + 1)
                if not first(g):
                    act.wait_ge(v_spread, UNITS * (g + 1))
                for b in range(PAIR):
                    for h in range(2):
                        src = halves(FB[2])[:, b, 128 * h:128 * h + 128].rearrange("p (n d) -> p d n", d=S)
                        act.activation(v_exp[:, b, h, :, :].rearrange("p d (n k) -> p d n k", k=S),
                                       src.unsqueeze(3).broadcast_to([L, S, HH, S]), ACT.Copy
                                       ).then_inc(v_exp_ready, 1)
                if not first(g):
                    act.wait_ge(cv_ready, g + 1)
                act.activation(v_tok[:, :, :], halves(FB[2]), ACT.Copy).then_inc(v_tok_ready, 1)

            def gate_tanh(g):
                act.wait_ge(gp_done, g + 1)
                if not first(g):
                    act.wait_ge(gate_ready, g)
                act.activation(gate_th[:, :, :], halves(FB[3]), ACT.Tanh, scale=0.5).then_inc(gate_th_ready, 1)

            def square_heads(g):
                act.wait_ge(att_c_ready, g + 2)
                if not first(g):
                    act.wait_ge(gn_steps, (RS + 1) * (g + 1))
                act.activation(sq[:, :, :, :], att_c[:, :, :, :], ACT.Square).then_inc(sq_ready, 1)

            def att_evacuate(g):
                act.wait_ge(gn_half_ready, 1)
                act.wait_ge(att_turned, g + 2)
                if not first(g):
                    act.wait_ge(ag_ready, g + 1)
                for h in range(2):
                    act.activation(att_f[:, h, :], halves(FB[2])[:, h, :], ACT.Identity,
                                   bias=gn_half[:, h, 1:2], scale=gn_half[:, h, 0:1]).then_inc(att_f_ready, 1)

            def norm2_evacuate(g):
                act.wait_ge(xh2_turned, g + 2)
                if not first(g):
                    act.wait_ge(xk_ready, 2 * (g + 1))
                    act.wait_ge(xr_ready, 2 * (g + 1))
                for h in range(2):
                    act.activation(xn2[:, h, :, 1:], quarters(FB[3])[:, h, :, :], ACT.Identity,
                                   bias=cols[:, h, R_LN2B:R_LN2B + 1], scale=cols[:, h, R_LN2W:R_LN2W + 1]
                                   ).then_inc(xn2_ready, 1)

            def ffn_act(g):
                act.wait_ge(fk_done, g + 2)
                if not first(g):
                    act.wait_ge(kk_ready, g + 1)
                act.activation(relu[:, :, :], halves(FB[2]), ACT.Relu).then_inc(relu_ready, 1)
                act.wait_ge(relu_ready, g + 2)
                if not first(g):
                    act.wait_ge(fv_done, g + 1)
                act.activation(kk[:, :, :], relu[:, :, :], ACT.Square).then_inc(kk_ready, 1)
                act.wait_ge(fr_done, g + 2)
                if not first(g):
                    act.wait_ge(ffn_ready, g + 1)
                act.activation(th2[:, :, :], halves(FB[3]), ACT.Tanh, scale=0.5).then_inc(th2_ready, 1)

            def store(g):
                act.wait_ge(x4_ready, g + 2)
                act.dma_start(out[bass.ds(PAIR * g, PAIR), :, :].rearrange("b c n -> c b n"), x4[:, :, :]
                              ).then_inc(stored, 16)

            def body(m, s, a):
                if a is not None:
                    attn_in(a)
                    softmax(a, 0)
                if m is not None:
                    decay_tanh(m)
                if a is not None:
                    softmax(a, 1)
                if m is not None:
                    decay(m)
                    decay_outer(m)
                    evacuate_k(m)
                    evacuate_r(m)
                if s is not None:
                    square_heads(s)
                if a is not None:
                    prob_evacuate(a, 0)
                    prob_evacuate(a, 1)
                if m is not None:
                    evacuate_v(m)
                    gate_tanh(m)
                if s is not None:
                    att_evacuate(s)
                if a is not None:
                    norm_evacuate(a)
                if s is not None:
                    norm2_evacuate(s)
                    ffn_act(s)
                if a is not None:
                    lora_tanh(a)
                if s is not None:
                    store(s)

            ready_attn_weights()
            attn_in(0)
            softmax(0, 0)
            softmax(0, 1)
            prob_evacuate(0, 0)
            ready_rows()
            prob_evacuate(0, 1)
            ready_weights(0, 4)
            norm_evacuate(0)
            ready_weights(4, 8)
            lora_tanh(0)
            attn_in(1)
            softmax(1, 0)
            decay_tanh(0)
            softmax(1, 1)
            evacuate_k(0)
            decay(0)
            prob_evacuate(1, 0)
            decay_outer(0)
            prob_evacuate(1, 1)
            evacuate_r(0)
            evacuate_v(0)
            norm_evacuate(1)
            gate_tanh(0)
            lora_tanh(1)
            with act.Fori(1, G - 1) as i:
                body(i, i - 1, i + 1)
            body(G - 1, G - 2, None)
            body(None, G - 1, None)
            act.wait_ge(stored, 16 * G)

        @block.tensor
        def _(pe):
            def first(g):
                return isinstance(g, int) and g == 0

            def last(g):
                return isinstance(g, int) and g == G - 1

            def turn(out_, in_, k=128):
                return pe.transpose(out_, in_, ident[0:k, 0:k])

            def turn_attn_weights():
                pe.wait_ge(ident_ready, 1)
                pe.wait_ge(attn_w_loaded, 32)
                for n in range(2):
                    i = turn(FB[0][:, n * D:(n + 1) * D], attn_nat[:, n, :], D)
                i.then_inc(w_turned, 1)
                pe.wait_ge(v0_loaded, 16)
                turn(FB[3][:, 0:L], v0_nat[:, :]).then_inc(w_turned, 1)

            def turn_rows():
                pe.wait_ge(rows_loaded, 16 * 6)
                pe.wait_ge(more_rows_loaded, 16 * 6)
                for h in range(2):
                    turn(FB[2][:, h * ROWS:(h + 1) * ROWS], rows[:, 128 * h:128 * h + 128], ROWS)
                pe.wait_ge(state_rows_loaded, 16)
                for h in range(2):
                    i = turn(FB[2][:, 128 + 2 * B * h:128 + 2 * B * (h + 1)], state_rows[:, 128 * h:128 * h + 128],
                             2 * B)
                i.then_inc(w_turned, 1)

            def turn_weights(lo, hi):
                for n in range(lo, hi):
                    pe.wait_ge(w_loaded[n], 16)
                    if n >= 4:
                        pe.wait_ge(w_ready, n)
                    for h_in in range(2):
                        for h_out in range(2):
                            i = turn(quarters(BB[n % 4])[:, h_in, h_out, :],
                                     w_nat[:, n, h_out, 128 * h_in:128 * h_in + 128])
                    i.then_inc(w_turned, 1)

            def attn_qk(g):
                pe.wait_ge(x_loaded, 16 * (g + 1))
                if first(g):
                    pe.wait_ge(w_ready, 2)
                else:
                    pe.wait_ge(xn_ready, 2 * g)
                pe.matmul(FB[0][0:D, :], attn_T[:, 0, :], xin[:, :, :].rearrange("p b n -> p (b n)"),
                          start=True, stop=True).then_inc(q_done, 1)
                pe.wait_ge(ctx_loaded, 16 * (g + 1))
                if not first(g):
                    pe.wait_ge(lora_ready, 2 * g)
                pe.matmul(FB[1][0:D, :], attn_T[:, 1, :], cin[:, :, :].rearrange("p b n -> p (b n)"),
                          start=True, stop=True).then_inc(k_done, 1)

            def attn_v(g):
                pe.wait_ge(qk_ready, 2 * g + 1)
                for b in range(PAIR):
                    for mt in range(2):
                        i = pe.matmul(quarters(FB[0])[:, b, mt, :], cin[:, b, 128 * mt:128 * mt + 128], v0_T[:, :],
                                      start=True, stop=True)
                i.then_inc(v_done, 1)

            def scores(g):
                pe.wait_ge(qk_ready, 2 * g + 2)
                for b in range(PAIR):
                    bank = FB[1 - b]
                    if b == 1:
                        pe.wait_ge(vT_ready, g + 1)
                    for nt in range(2):
                        i = pe.matmul(halves(bank)[:, nt, :], qk[:, 0, b * E + 128 * nt:b * E + 128 * nt + 128],
                                      qk[:, 1, b * E:(b + 1) * E], start=True, stop=True)
                    i.then_inc(scores_done, 1)

            def prob_turn(g, b):
                pe.wait_ge(prob_ready, 2 * g + b + 1)
                for mt in range(2):
                    for nt in range(2):
                        i = turn(quarters(FB[1 - b])[:, mt, nt, :], prob[:, b, nt, 128 * mt:128 * mt + 128])
                i.then_inc(prob_turned, 1)

            def attn_out(g):
                pe.wait_ge(vT_ready, g + 1)
                for b in range(PAIR):
                    pe.wait_ge(probT_ready, 2 * g + b + 1)
                    for mt in range(2):
                        i = pe.matmul(halves(FB[1])[:, b, :], vT[:, b, mt, :], probT[:, b, mt, :],
                                      start=(mt == 0), stop=(mt == 1))
                i.then_inc(attn_done, 1)

            def norm_turn(g):
                pe.wait_ge(probT_ready, 2 * g + 2)
                for b in range(PAIR):
                    pe.wait_ge(xh_ready, 2 * g + b + 1)
                    for h in range(2):
                        i = turn(quarters(FB[0])[:, h, b, :], xh[:, b, 128 * h:128 * h + 128])
                i.then_inc(xh_turned, 1)

            def lora_in(g):
                pe.wait_ge(lora_loaded, 80)
                pe.wait_ge(xmix_ready, 2 * g + 2)
                pe.wait_ge(x2_ready, g + 1)
                for h in range(2):
                    pe.matmul(FB[1][:, 0:T], mw1[:, h, 0:4 * LORA], xmix[:, h, :], start=(h == 0), stop=(h == 1))
                for h in range(2):
                    i = pe.matmul(FB[1][0:LORA, T:2 * T], mw1[:, h, 4 * LORA:], xmix[:, h, :],
                                  start=(h == 0), stop=(h == 1))
                i.then_inc(lora_done, 1)

            def to_features(bank, w, src, done):
                for h_out in range(2):
                    for h_in in range(2):
                        i = pe.matmul(halves(bank)[:, h_out, :], wT[:, w, h_in, 128 * h_out:128 * h_out + 128],
                                      src[:, h_in, :], start=(h_in == 0), stop=(h_in == 1))
                i.then_inc(done, 1)

            def to_tokens(bank, w, src, done):
                for b in range(PAIR):
                    for h_in in range(2):
                        i = pe.matmul(halves(bank)[:, b, :], src[:, h_in, L * b:L * (b + 1)], wT[:, w, h_in, :],
                                      start=(h_in == 0), stop=(h_in == 1))
                i.then_inc(done, 1)

            MIX_BANK = {MIX_W: FB[2], MIX_K: FB[3], MIX_R: FB[2], MIX_V: FB[3], MIX_G: FB[2]}

            def mix(g, j):
                if j in (MIX_W, MIX_K):
                    pe.wait_ge(w_ready, 3 + 8)
                    pe.wait_ge(lora_ready, 2 * g + 2)
                if j == MIX_W:
                    if not first(g):
                        pe.wait_ge(ffn_ready, g)
                elif j == MIX_K:
                    if not first(g):
                        pe.wait_ge(th2_ready, g)
                else:
                    pe.wait_ge(mixed_ready[{MIX_R: MIX_W, MIX_V: MIX_K, MIX_G: MIX_R}[j]], 2 * g + 2)
                for h in range(2):
                    if j < 4:
                        w2, lo = mw2[LORA * j:LORA * (j + 1), :], lora[LORA * j:LORA * (j + 1), :]
                    else:
                        w2, lo = mw2_last[:, :], lora_last[:, :]
                    i = pe.matmul(halves(MIX_BANK[j])[:, h, :], w2[:, 128 * h:128 * h + 128], lo, start=True, stop=True)
                i.then_inc(mix_done[j], 1)

            def decay_rank(g):
                pe.wait_ge(x5_ready[MIX_W], g + 1)
                pe.wait_ge(mixed_ready[MIX_V], 2 * g + 2)
                for h in range(2):
                    i = pe.matmul(FB[3][0:DECAY, 0:T], dw1[:, h, :], x5[:, MIX_W, h, :], start=(h == 0), stop=(h == 1))
                i.then_inc(dlora_done, 1)

            def decay_out(g):
                pe.wait_ge(wt_ready, g + 1)
                for h in range(2):
                    i = pe.matmul(halves(FB[3])[:, h, :], dw2[:, 128 * h:128 * h + 128], wt[:, :], start=True, stop=True)
                i.then_inc(decay_done, 1)

            def project_k(g):
                pe.wait_ge(mixed_ready[MIX_G], 2 * g + 2)
                pe.wait_ge(x5_ready[MIX_K], g + 1)
                to_features(FB[2], WK, x5[:, MIX_K, :, :], kp_done)

            def project_r(g):
                pe.wait_ge(e1_ready, 2 * g + 2)
                pe.wait_ge(x5_ready[MIX_R], g + 1)
                to_features(FB[3], WR, x5[:, MIX_R, :, :], rp_done)

            def project_v(g):
                pe.wait_ge(kf_ready, g + 1)
                pe.wait_ge(x5_ready[MIX_V], g + 1)
                to_tokens(FB[2], WV, x5[:, MIX_V, :, :], vp_done)

            def project_g(g):
                pe.wait_ge(rf_ready, g + 1)
                pe.wait_ge(x5_ready[MIX_G], g + 1)
                to_features(FB[3], WG, x5[:, MIX_G, :, :], gp_done)

            def spread(g, u):
                if u == 0:
                    pe.wait_ge(v_exp_ready, 2 * PAIR * (g + 1))
                if u >= 2 or not first(g):
                    pe.wait_ge(kv_ready, UNITS * (g + 1) + u - 1)
                h, d0 = u // 4, 2 * (u % 4)
                for d in range(2):
                    for b in range(PAIR):
                        i = turn(quarters(BB[u % 2])[:, d, b, :], v_exp[:, b, h, d0 + d, :])
                i.then_inc(v_spread, 1)

            def turn_bonus(g):
                pe.wait_ge(ruk_ready, g + 2)
                if not first(g):
                    pe.wait_ge(head_out_ready, 9 * (g + 1))
                for b in range(PAIR):
                    for h in range(2):
                        i = turn(quarters(BB[2])[:, b, h, :], ruk[:, h, L * b:L * (b + 1)])
                i.then_inc(rs_turned, 1)

            def turn_rs(g, u):
                pe.wait_ge(rs_ready, UNITS * (g + 1) + u + 1)
                if u >= 1 or not first(g):
                    pe.wait_ge(head_out_ready, 9 * (g + 1) + u)
                for b in range(PAIR):
                    for d in range(2):
                        i = turn(quarters(BB[2 + (u + 1) % 2])[:, b, d, :], rs[:, u % 2, d, b, :])
                i.then_inc(rs_turned, 1)

            def units(g, lo, hi):
                for u in range(lo, hi):
                    if u + 2 < UNITS:
                        spread(g, u + 2)
                    turn_rs(g, u)

            def att_turn(g):
                pe.wait_ge(att_n_ready, g + 2)
                if last(g):
                    pe.wait_ge(ffn_ready, g + 1)
                else:
                    pe.wait_ge(v_tok_ready, g + 2)
                flat = att_n[:, :, :, :].rearrange("p b h s -> p b (h s)")
                for h in range(2):
                    for b in range(PAIR):
                        i = turn(quarters(FB[2])[:, h, b, :], flat[:, b, 128 * h:128 * h + 128])
                i.then_inc(att_turned, 1)

            def att_project(g):
                pe.wait_ge(ag_ready, g + 2)
                to_tokens(FB[2], WO, ag, o_done)

            def norm2_turn(g):
                if last(g):
                    pe.wait_ge(th2_ready, g + 1)
                else:
                    pe.wait_ge(gate_ready, g + 2)
                for b in range(PAIR):
                    pe.wait_ge(xh2_ready, 2 * (g + 1) + b + 1)
                    for h in range(2):
                        i = turn(quarters(FB[3])[:, h, b, :], xh2[:, b, 128 * h:128 * h + 128])
                i.then_inc(xh2_turned, 1)

            def ffn_in(g):
                pe.wait_ge(xk_ready, 2 * (g + 1) + 2)
                pe.wait_ge(x3_ready, g + 2)
                to_features(FB[2], FK, xk, fk_done)
                pe.wait_ge(xr_ready, 2 * (g + 1) + 2)
                pe.wait_ge(xn2_ready, 2 * (g + 1) + 2)
                to_tokens(FB[3], FR, xr, fr_done)

            def ffn_out(g):
                pe.wait_ge(kk_ready, g + 2)
                to_tokens(FB[2], FV, kk, fv_done)

            def body(m, s, a):
                if a is not None:
                    attn_qk(a)
                if m is not None:
                    mix(m, MIX_W)
                if s is not None:
                    spread(s, 6)
                if m is not None:
                    mix(m, MIX_K)
                if s is not None:
                    turn_rs(s, 3)
                if a is not None:
                    attn_v(a)
                if m is not None:
                    mix(m, MIX_R)
                    mix(m, MIX_V)
                if s is not None:
                    spread(s, 7)
                    turn_rs(s, 4)
                if m is not None:
                    mix(m, MIX_G)
                if a is not None:
                    scores(a)
                if m is not None:
                    decay_rank(m)
                if s is not None:
                    turn_rs(s, 5)
                if m is not None:
                    decay_out(m)
                    project_k(m)
                if s is not None:
                    turn_rs(s, 6)
                    turn_rs(s, 7)
                if m is not None:
                    project_r(m)
                if a is not None:
                    prob_turn(a, 0)
                if m is not None:
                    project_v(m)
                if a is not None:
                    prob_turn(a, 1)
                    attn_out(a)
                if m is not None:
                    project_g(m)
                    spread(m, 0)
                if s is not None:
                    att_turn(s)
                if m is not None:
                    spread(m, 1)
                if s is not None:
                    att_project(s)
                if a is not None:
                    norm_turn(a)
                if m is not None:
                    spread(m, 2)
                    turn_bonus(m)
                    spread(m, 3)
                    turn_rs(m, 0)
                if s is not None:
                    norm2_turn(s)
                if m is not None:
                    spread(m, 4)
                if a is not None:
                    lora_in(a)
                if m is not None:
                    turn_rs(m, 1)
                if s is not None:
                    ffn_in(s)
                    ffn_out(s)
                if m is not None:
                    turn_rs(m, 2)
                    spread(m, 5)

            turn_attn_weights()
            attn_qk(0)
            attn_v(0)
            scores(0)
            prob_turn(0, 0)
            turn_rows()
            prob_turn(0, 1)
            attn_out(0)
            turn_weights(0, 4)
            norm_turn(0)
            turn_weights(4, 8)
            lora_in(0)
            mix(0, MIX_W)
            mix(0, MIX_K)
            attn_qk(1)
            mix(0, MIX_V)
            attn_v(1)
            scores(1)
            mix(0, MIX_R)
            decay_rank(0)
            mix(0, MIX_G)
            decay_out(0)
            project_k(0)
            prob_turn(1, 0)
            prob_turn(1, 1)
            project_v(0)
            project_r(0)
            attn_out(1)
            spread(0, 0)
            norm_turn(1)
            spread(0, 1)
            spread(0, 2)
            turn_bonus(0)
            project_g(0)
            spread(0, 3)
            turn_rs(0, 0)
            spread(0, 4)
            lora_in(1)
            turn_rs(0, 1)
            spread(0, 5)
            turn_rs(0, 2)
            with pe.Fori(1, G - 1) as i:
                body(i, i - 1, i + 1)
            body(G - 1, G - 2, None)
            body(None, G - 1, None)

        @block.vector
        def _(dve):
            def first(g):
                return isinstance(g, int) and g == 0

            def root(steps, at, var, scale, buf):
                t, v, y, r = (buf[:, n, :] for n in range(4))
                k = at

                def link(ins):
                    nonlocal k
                    ins.then_inc(steps, 1)
                    k = k + 1
                    dve.wait_ge(steps, k)

                link(dve.tensor_scalar(v, var, SPREAD * scale, SPREAD * EPS, ALU.mult, ALU.add))
                link(dve.tensor_scalar(t.bitcast(i32), v.bitcast(i32), 1, None, ALU.arith_shift_right))
                link(dve.tensor_scalar(y.bitcast(i32), t.bitcast(i32), -1.0, float(RSQRT_MAGIC), ALU.mult, ALU.add))
                link(dve.tensor_tensor(t, v, y, ALU.mult))
                link(dve.tensor_tensor(t, t, y, ALU.mult))
                link(dve.scalar_tensor_tensor(t, t, 10.0 / 3.0, t, ALU.subtract, ALU.mult))
                link(dve.scalar_tensor_tensor(y, t, 5.0, y, ALU.add, ALU.mult))
                link(dve.scalar_tensor_tensor(t, y, 0.375 ** 2, v, ALU.mult, ALU.mult))
                link(dve.tensor_tensor(t, t, y, ALU.mult))
                link(dve.scalar_tensor_tensor(t, t, 10.0 / 3.0, t, ALU.subtract, ALU.mult))
                link(dve.scalar_tensor_tensor(r, t, 5.0, y, ALU.add, ALU.mult))

            def layer_stats(g_at, src, stats, mv, ve, steps):
                at = LN_STEPS * g_at
                for b in range(PAIR):
                    dve.bn_stats(stats[:, b, :], src[:, b, :]).then_inc(steps, 1)
                dve.wait_ge(steps, at + PAIR)
                dve.memset(wait_carrier[:, :], 0.0)
                for b in range(PAIR):
                    dve.bn_aggr(mv[:, b, :], stats[:, b, :]).then_inc(steps, 1)
                dve.wait_ge(steps, at + 2 * PAIR)
                dve.tensor_scalar(ve[:, :], mv[:, :, 1], EPS, None, ALU.add).then_inc(steps, 1)

            def layer_apply(src, mv, rstd, dst, ready):
                for b in range(PAIR):
                    dve.tensor_scalar(dst[:, b, :], src[:, b, :], mv[:, b, 0:1], rstd[:, b:b + 1],
                                      ALU.subtract, ALU.mult).then_inc(ready, 1)

            def row_max(g, b):
                dve.wait_ge(scores_done, 2 * g + b + 1)
                if not first(g):
                    dve.wait_ge(exp_ready, 4 * g)
                dve.tensor_reduce(neg_max[:, b, :], halves(FB[1 - b]), X_AXIS, ALU.max, negate=True
                                  ).then_inc(max_ready, 1)

            def row_rcp(g, b):
                dve.wait_ge(exp_ready, 4 * g + 2 * b + 2)
                if not first(g):
                    dve.wait_ge(prob_ready, 2 * g)
                dve.reciprocal(prob_rcp[:, b, :], prob_sum[:, b, :]).then_inc(rcp_ready, 1)

            def attn_residual(g):
                dve.wait_ge(biases_loaded, 48)
                dve.wait_ge(attn_done, g + 1)
                if not first(g):
                    dve.wait_ge(x2_kept, g)
                    dve.wait_ge(xh_ready, 2 * g)
                dve.scalar_tensor_tensor(x2[:, :, :], halves(FB[1]), bv_col[:, 0:1], xin[:, :, :], ALU.add, ALU.add
                                         ).then_inc(x2_ready, 1)
                dve.wait_ge(x2_ready, g + 1)
                if not first(g):
                    dve.wait_ge(xh_turned, g)
                layer_stats(g, x2, st1, mv1, ve1, ln1_steps)
                dve.tensor_scalar(x2_all[:, bass.ds(PAIR * g, PAIR), :], x2[:, :, :], 1.0, None, ALU.mult
                                  ).then_inc(x2_kept, 1)

            def normed(g):
                dve.wait_ge(rstd1_ready, g + 1)
                layer_apply(x2, mv1, rstd1, xh, xh_ready)

            def shift(g):
                dve.wait_ge(prev_cols_ready, 1)
                if not first(g):
                    dve.wait_ge(sx_ready, g)
                dve.tensor_scalar(xn[:, :, :, 0], prev_cols[:, 1, :, bass.ds(PAIR * g, PAIR)], 1.0, None, ALU.mult
                                  ).then_inc(prev_ready, 1)
                dve.wait_ge(xn_ready, 2 * g + 2)
                dve.wait_ge(prev_ready, g + 1)
                if not first(g):
                    dve.wait_ge(mixed_ready[MIX_G], 2 * g)
                    dve.wait_ge(lora_done, g)
                dve.tensor_tensor(sx[:, :, :, :], xn[:, :, :, 0:L], xn[:, :, :, 1:], ALU.subtract
                                  ).then_inc(sx_ready, 1)
                dve.wait_ge(sx_ready, g + 1)
                for h in range(2):
                    dve.scalar_tensor_tensor(xmix[:, h, :].rearrange("p (b t) -> p b t", b=PAIR), sx[:, h, :, :],
                                             cols[:, h, R_MAAX:R_MAAX + 1], xn[:, h, :, 1:], ALU.mult, ALU.add
                                             ).then_inc(xmix_ready, 1)

            def mixed_(g, j, bank):
                dve.wait_ge(mix_done[j], g + 1)
                if not first(g):
                    dve.wait_ge(x5_ready[j], g)
                for h in range(2):
                    dve.scalar_tensor_tensor(mixed[:, j, h, :], halves(bank)[:, h, :],
                                             cols[:, h, R_STACK + j:R_STACK + j + 1],
                                             sx[:, h, :, :].rearrange("p b t -> p (b t)"), ALU.add, ALU.mult
                                             ).then_inc(mixed_ready[j], 1)

            def gate_(g):
                dve.wait_ge(gate_th_ready, g + 1)
                if not first(g):
                    dve.wait_ge(ag_ready, g + 1)
                dve.scalar_tensor_tensor(gate[:, :, :], gate_th[:, :, :], 1.0, halves(FB[3]), ALU.add, ALU.mult
                                         ).then_inc(gate_ready, 1)

            def scan_start(g):
                dve.wait_ge(s0_loaded, 16 * B)
                if not first(g):
                    dve.wait_ge(state_ready, UNITS * (g + 1))
                for h in range(2):
                    i = dve.tensor_scalar(kv[:, h, :, :, 0],
                                          s0[:, h, bass.ds(PAIR * g, PAIR), :].rearrange("p b d -> p d b"),
                                          1.0, None, ALU.mult)
                i.then_inc(s0_placed, 1)

            def scan_kv(g, u):
                h, d0 = u // 4, 2 * (u % 4)
                dve.wait_ge(v_spread, UNITS * (g + 1) + u + 1)
                if u == 0:
                    dve.wait_ge(kf_ready, g + 1)
                    dve.wait_ge(s0_placed, g + 2)
                    dve.wait_ge(w_ready_s, 2 * g + 2)
                    if not first(g):
                        dve.wait_ge(state_ready, UNITS * (g + 1))
                dve.tensor_tensor(kv[:, h, d0:d0 + 2, :, 1:], quarters(BB[u % 2])[:, :, :, 0:L - 1],
                                  kf[:, h, :, 0:L - 1].unsqueeze(1).broadcast_to([128, 2, PAIR, L - 1]), ALU.mult
                                  ).then_inc(kv_ready, 1)

            def scan_state(g, u):
                h, d0 = u // 4, 2 * (u % 4)
                dve.wait_ge(kv_ready, UNITS * (g + 1) + u + 1)
                if u >= 2:
                    dve.wait_ge(rs_ready, UNITS * (g + 1) + u - 1)
                elif not first(g):
                    dve.wait_ge(rs_ready, UNITS * (g + 1))
                dve.tensor_tensor_scan(state[:, u % 2, :, :, :].rearrange("p d b t -> p (d b t)"),
                                       w_prev[:, h, :, :, :].rearrange("p d b t -> p (d b t)"),
                                       kv[:, h, d0:d0 + 2, :, :].rearrange("p d b t -> p (d b t)"),
                                       0.0, ALU.mult, ALU.add).then_inc(state_ready, 1)

            def scan_out(g, u):
                h, d0 = u // 4, 2 * (u % 4)
                dve.wait_ge(rs_turned, 9 * (g + 1) + u + 2)
                if u == 0 and not first(g):
                    dve.wait_ge(att1_ready, g + 1)
                    dve.wait_ge(head_sum_ready, g + 1)
                dve.tensor_reduce(att[:, :, HH * h:HH * (h + 1), d0:d0 + 2].rearrange("p b h d -> p b d h"),
                                  quarters(BB[2 + (u + 1) % 2]).rearrange("p b d (h k) -> p b d h k", k=S),
                                  X_AXIS, ALU.add).then_inc(head_out_ready, 1)

            def bonus_out(g):
                dve.wait_ge(rs_turned, 9 * (g + 1) + 1)
                if not first(g):
                    dve.wait_ge(cv_ready, g + 1)
                dve.tensor_reduce(bonus[:, :, :].rearrange("p b (a h) -> p b a h", a=2),
                                  quarters(BB[2]).rearrange("p b a (h k) -> p b a h k", k=S),
                                  X_AXIS, ALU.add).then_inc(head_out_ready, 1)

            def head_mean(g):
                dve.wait_ge(cv_ready, g + 2)
                dve.wait_ge(head_out_ready, 9 * (g + 2))
                dve.wait_ge(att_c_ready, g + 1)
                dve.tensor_tensor(att1[:, :, :, :], att[:, :, :, :], cv[:, :, :, :], ALU.add).then_inc(att1_ready, 1)
                dve.wait_ge(att1_ready, g + 2)
                dve.tensor_reduce(head_sum[:, :], att1[:, :, :, :].rearrange("p b h s -> p (b h) s"), X_AXIS,
                                  ALU.add).then_inc(gn_sum, 1)
                dve.wait_ge(gn_sum, g + 2)
                dve.tensor_scalar(head_sum[:, :], head_sum[:, :], -1.0 / S, None, ALU.mult).then_inc(head_sum_ready, 1)
                dve.wait_ge(head_sum_ready, g + 2)
                dve.wait_ge(att_n_ready, g + 1)
                dve.tensor_tensor(att_c[:, :, :, :].rearrange("p b h s -> p (b h) s"),
                                  att1[:, :, :, :].rearrange("p b h s -> p (b h) s"),
                                  head_sum[:, :].unsqueeze(2).broadcast_to([L, PAIR * H, S]), ALU.add
                                  ).then_inc(att_c_ready, 1)

            def head_norm(g):
                dve.wait_ge(sq_ready, g + 2)
                dve.tensor_reduce(head_var[:, :], sq[:, :, :, :].rearrange("p b h s -> p (b h) s"), X_AXIS,
                                  ALU.add).then_inc(gn_steps, 1)
                at = (RS + 1) * (g + 1) + 1
                dve.wait_ge(gn_steps, at)
                root(gn_steps, at, head_var[:, :], 1.0 / S, nwt2)
                dve.wait_ge(att_turned, g + 1)
                dve.tensor_tensor(att_n[:, :, :, :].rearrange("p b h s -> p (b h) s"),
                                  att_c[:, :, :, :].rearrange("p b h s -> p (b h) s"),
                                  nwt2[:, 3, :].unsqueeze(2).broadcast_to([L, PAIR * H, S]), ALU.mult
                                  ).then_inc(att_n_ready, 1)

            def gated(g):
                dve.wait_ge(att_f_ready, 2 * (g + 2))
                dve.wait_ge(gate_ready, g + 1)
                dve.wait_ge(o_done, g + 1)
                dve.tensor_tensor(ag[:, :, :], att_f[:, :, :], gate[:, :, :], ALU.mult).then_inc(ag_ready, 1)

            def residual(g):
                dve.wait_ge(o_done, g + 2)
                dve.wait_ge(x2_kept, g + 1)
                if not first(g):
                    dve.wait_ge(x4_ready, g + 1)
                dve.tensor_tensor(x3[:, :, :], halves(FB[2]), x2_all[:, bass.ds(PAIR * g, PAIR), :], ALU.add).then_inc(x3_ready, 1)
                dve.wait_ge(x3_ready, g + 2)
                if not first(g):
                    dve.wait_ge(xh2_turned, g + 1)
                layer_stats(g + 1, x3, st2, mv2, ve2, ln2_steps)

            def normed2(g):
                dve.wait_ge(rstd2_ready, g + 2)
                layer_apply(x3, mv2, rstd2, xh2, xh2_ready)

            def shift2(g):
                if not first(g):
                    dve.wait_ge(sx2_ready, g + 1)
                dve.tensor_scalar(xn2[:, :, :, 0], prev_cols[:, 0, :, bass.ds(PAIR * g, PAIR)], 1.0, None, ALU.mult
                                  ).then_inc(prev2_ready, 1)
                dve.wait_ge(xn2_ready, 2 * (g + 1) + 2)
                dve.wait_ge(prev2_ready, g + 2)
                if not first(g):
                    dve.wait_ge(xk_ready, 2 * (g + 1))
                    dve.wait_ge(xr_ready, 2 * (g + 1))
                    dve.wait_ge(fk_done, g + 1)
                    dve.wait_ge(fr_done, g + 1)
                dve.tensor_tensor(sx2[:, :, :, :], xn2[:, :, :, 0:L], xn2[:, :, :, 1:], ALU.subtract
                                  ).then_inc(sx2_ready, 1)
                dve.wait_ge(sx2_ready, g + 2)
                for row, dst, ready in ((R_FK, xk, xk_ready), (R_FR, xr, xr_ready)):
                    for h in range(2):
                        dve.scalar_tensor_tensor(dst[:, h, :].rearrange("p (b t) -> p b t", b=PAIR), sx2[:, h, :, :],
                                                 cols[:, h, row:row + 1], xn2[:, h, :, 1:], ALU.mult, ALU.add
                                                 ).then_inc(ready, 1)

            def ffn_out(g):
                dve.wait_ge(fv_done, g + 2)
                dve.wait_ge(th2_ready, g + 2)
                if not first(g):
                    dve.wait_ge(x4_ready, g + 1)
                dve.scalar_tensor_tensor(ffn[:, :, :], th2[:, :, :], 1.0, halves(FB[2]), ALU.add, ALU.mult
                                         ).then_inc(ffn_ready, 1)
                dve.wait_ge(ffn_ready, g + 2)
                if not first(g):
                    dve.wait_ge(stored, 16 * g)
                dve.scalar_tensor_tensor(x4[:, :, :], ffn[:, :, :], 0.5, x3[:, :, :], ALU.mult, ALU.add
                                         ).then_inc(x4_ready, 1)

            def scan(g, lo, hi):
                for u in range(lo, hi):
                    if u < UNITS:
                        scan_kv(g, u)
                        scan_state(g, u)
                    if u == 0:
                        bonus_out(g)
                    if u >= 2:
                        scan_out(g, u - 2)

            def body(m, s, a):
                if s is not None:
                    scan_kv(s, 5)
                if m is not None:
                    mixed_(m, MIX_W, FB[2])
                    mixed_(m, MIX_K, FB[3])
                if s is not None:
                    scan_state(s, 5)
                if m is not None:
                    mixed_(m, MIX_R, FB[2])
                    mixed_(m, MIX_V, FB[3])
                if s is not None:
                    scan_kv(s, 6)
                    scan_out(s, 3)
                if m is not None:
                    mixed_(m, MIX_G, FB[2])
                if a is not None:
                    row_max(a, 0)
                if s is not None:
                    scan_state(s, 6)
                if a is not None:
                    row_max(a, 1)
                if s is not None:
                    scan_kv(s, 7)
                    scan_state(s, 7)
                if a is not None:
                    row_rcp(a, 0)
                if s is not None:
                    scan_out(s, 4)
                    scan_out(s, 5)
                    scan_out(s, 6)
                if a is not None:
                    row_rcp(a, 1)
                if s is not None:
                    scan_out(s, 7)
                    head_mean(s)
                if m is not None:
                    scan_start(m)
                if s is not None:
                    head_norm(s)
                if a is not None:
                    attn_residual(a)
                if m is not None:
                    scan_kv(m, 0)
                    scan_state(m, 0)
                if s is not None:
                    gated(s)
                if m is not None:
                    scan_kv(m, 1)
                    gate_(m)
                    scan_state(m, 1)
                if a is not None:
                    normed(a)
                if s is not None:
                    residual(s)
                if m is not None:
                    bonus_out(m)
                if s is not None:
                    normed2(s)
                if m is not None:
                    scan_kv(m, 2)
                if a is not None:
                    shift(a)
                if m is not None:
                    scan_state(m, 2)
                if s is not None:
                    shift2(s)
                if m is not None:
                    scan_kv(m, 3)
                    scan_out(m, 0)
                    scan_out(m, 1)
                    scan_state(m, 3)
                    scan_kv(m, 4)
                    scan_state(m, 4)
                if s is not None:
                    ffn_out(s)
                if m is not None:
                    scan_out(m, 2)

            row_max(0, 0)
            row_max(0, 1)
            row_rcp(0, 0)
            row_rcp(0, 1)
            attn_residual(0)
            normed(0)
            shift(0)
            mixed_(0, MIX_K, FB[3])
            mixed_(0, MIX_W, FB[2])
            row_max(1, 0)
            mixed_(0, MIX_V, FB[3])
            row_max(1, 1)
            row_rcp(1, 0)
            mixed_(0, MIX_R, FB[2])
            scan_start(0)
            mixed_(0, MIX_G, FB[2])
            row_rcp(1, 1)
            attn_residual(1)
            normed(1)
            scan_kv(0, 0)
            scan_state(0, 0)
            scan_kv(0, 1)
            shift(1)
            scan_state(0, 1)
            bonus_out(0)
            scan_kv(0, 2)
            scan_kv(0, 3)
            scan_state(0, 2)
            gate_(0)
            scan_out(0, 0)
            scan_kv(0, 4)
            scan_state(0, 3)
            scan_state(0, 4)
            scan_out(0, 1)
            scan_out(0, 2)
            with dve.Fori(1, G - 1) as i:
                body(i, i - 1, i + 1)
            body(G - 1, G - 2, None)
            body(None, G - 1, None)


_INS = ["x", "ctx_2048", "L0_xattn_Wq", "L0_xattn_bq", "L0_xattn_Wk", "L0_xattn_bk", "L0_xattn_Wv", "L0_xattn_bv",
        "L1_xattn_ln1_w", "L1_xattn_ln1_b", "L1_xattn_ln2_w", "L1_xattn_ln2_b", "L1_xattn_maa_x",
        "L1_xattn_maa_w1", "L1_xattn_maa_w2", "L1_xattn_maa_stack", "L1_xattn_time_decay", "L1_xattn_decay_w1",
        "L1_xattn_decay_w2", "L1_xattn_faaaa", "L1_xattn_Wr", "L1_xattn_Wk", "L1_xattn_Wv", "L1_xattn_Wg",
        "L1_xattn_Wo", "L1_xattn_gn_w", "L1_xattn_gn_b", "L1_xattn_ffn_maa_k", "L1_xattn_ffn_maa_r",
        "L1_xattn_ffn_Wk", "L1_xattn_ffn_Wr", "L1_xattn_ffn_Wv"]


def kernel(**inputs):
    import numpy as _np
    import concourse.bacc as _bacc
    from concourse import mybir as _mybir
    from concourse.bass_utils import run_bass_kernel_spmd as _run

    nc = _bacc.Bacc("TRN2", target_bir_lowering=False, num_devices=1)
    arrays, args = {}, []
    for name in _INS:
        a = _np.ascontiguousarray(inputs[name])
        arrays[f"in_{name}"] = a
        args.append(nc.dram_tensor(f"in_{name}", a.shape, _mybir.dt.from_np(a.dtype), kind="ExternalInput").ap())
    args.append(nc.dram_tensor("out_0", inputs["x"].shape, _mybir.dt.float32, kind="ExternalOutput").ap())
    xattn_rwkv(nc, *args)
    r = _run(nc, [arrays], core_ids=[0])
    return r.results[0]["out_0"]
```

```python
import concourse.bass as bass
from concourse import mybir
from contextlib import ExitStack


def xattn_rwkv(nc: bass.Bass, x, ctx_2048, Wq, bq, Wk, bk, Wv, bv, ln1_w, ln1_b, ln2_w, ln2_b, maa_x, maa_w1,
               maa_w2, maa_stack, time_decay, decay_w1, decay_w2, faaaa, Wr, Wkey, Wval, Wg, Wo, gn_w, gn_b,
               ffn_maa_k, ffn_maa_r, ffn_Wk, ffn_Wr, ffn_Wv, out):
    f32, i32 = mybir.dt.float32, mybir.dt.int32
    ALU = mybir.AluOpType
    ACT = mybir.ActivationFunctionType
    X_AXIS = mybir.AxisListType.X

    B, L, E = x.shape
    D = Wq.shape[0]
    H, S = faaaa.shape
    HALVES = E // 128
    HH = H // HALVES
    PAIR = 2
    G = B // PAIR
    T = PAIR * L
    MIXES, LORA, _ = maa_w2.shape
    MIX_K, MIX_W, MIX_V, MIX_R, MIX_G = range(MIXES)
    DECAY = decay_w1.shape[1]
    UNITS = HALVES * S // 2
    PRODUCTS = UNITS + 1
    EPS = 1e-5
    RSQRT_MAGIC = 0x5F3759DF

    ctx = ExitStack()
    with ctx:
        def sb(name, shape, dt=f32):
            return ctx.enter_context(nc.sbuf_tensor(name, shape, dt))

        def sem(name):
            return ctx.enter_context(nc.semaphore(name))

        ident = sb("ident", [128, 128])
        w_nat = sb("w_nat", [128, 8, 2, E])
        wT = sb("wT", [128, 8, 2, E])
        WR, WK, WV, WG, WO, FK, FR, FV = range(8)
        attn_nat = sb("attn_nat", [D, 2, L])
        attn_T = sb("attn_T", [L, 2, D])
        v0_nat = sb("v0_nat", [L, L])
        v0_T = sb("v0_T", [L, L])
        bqk = sb("bqk", [D, 2])
        bv_col = sb("bv_col", [L, 1])
        mw1 = sb("mw1", [128, 2, MIXES * LORA])
        mw2 = sb("mw2", [4 * LORA, E])
        mw2_last = sb("mw2_last", [LORA, E])
        dw1 = sb("dw1", [128, 2, DECAY])
        dw2 = sb("dw2", [DECAY, E])
        ROWS = 11 + MIXES
        rows = sb("rows", [ROWS, E])
        cols = sb("cols", [128, 2, ROWS])
        (R_LN1W, R_LN1B, R_LN2W, R_LN2B, R_MAAX, R_DECAY, R_U, R_GNW, R_GNB, R_FK, R_FR) = range(11)
        R_STACK = 11
        gn_half = sb("gn_half", [128, 2, 2])

        state_rows = sb("state_rows", [2 * B, E])
        prev_cols = sb("prev_cols", [128, 2, 2, B])
        s0 = sb("s0", [128, 2, B, S])
        x2_all = sb("x2_all", [L, B, E])

        xin = sb("xin", [L, PAIR, E])
        cin = sb("cin", [L, PAIR, E])
        qk = sb("qk", [D, 2, PAIR * E])
        vT = sb("vT", [128, PAIR, 2, L])
        neg_max = sb("neg_max", [128, PAIR, 2])
        prob = sb("prob", [128, PAIR, 2, E])
        prob_sum = sb("prob_sum", [128, PAIR, 2])
        prob_rcp = sb("prob_rcp", [128, PAIR, 2])
        probT = sb("probT", [128, PAIR, 2, E])
        x2 = sb("x2", [L, PAIR, E])
        st1 = sb("st1", [128, PAIR, 6])
        mv1 = sb("mv1", [128, PAIR, 2])
        wait_carrier = sb("wait_carrier", [128, 1])
        minus_half = sb("minus_half", [128, PAIR])
        head_ones = sb("head_ones", [128, HH])
        ve1 = sb("ve1", [128, PAIR])
        rstd1 = sb("rstd1", [128, PAIR])
        xh = sb("xh", [L, PAIR, E])
        xn = sb("xn", [128, 2, PAIR, L + 1])
        sx = sb("sx", [128, 2, PAIR, L])
        xmix = sb("xmix", [128, 2, T])
        lora = sb("lora", [4 * LORA, T])
        lora_last = sb("lora_last", [LORA, T])
        mixed = sb("mixed", [128, MIXES, 2, T])
        x5 = sb("x5", [128, MIXES, 2, T])
        wt = sb("wt", [DECAY, T])
        e1 = sb("e1", [128, 2, PAIR, L])
        gate_th = sb("gate_th", [128, 2, T])
        gate_y = sb("gate_y", [128, 2, T])

        kf = sb("kf", [128, 2, PAIR, L])
        rf = sb("rf", [128, 2, PAIR, L])
        w_prev = sb("w_prev", [128, 2, 2, PAIR, L])
        v_tok = sb("v_tok", [L, PAIR, E])
        v_exp = sb("v_exp", [L, PAIR, 2, S, 128])
        gate = sb("gate", [128, 2, T])

        kv = sb("kv", [128, 2, S, PAIR, L])
        state = sb("state", [128, 2, 2, PAIR, L])
        rs = sb("rs", [128, 2, 2, PAIR, L])
        ru = sb("ru", [128, 2, T])
        ruk = sb("ruk", [128, 2, T])
        bonus = sb("bonus", [L, PAIR, H])
        att = sb("att", [L, PAIR, H, S])
        cv = sb("cv", [L, PAIR, H, S])
        att1 = sb("att1", [L, PAIR, H, S])
        head_sum = sb("head_sum", [L, PAIR * H])
        att_c = sb("att_c", [L, PAIR, H, S])
        sq = sb("sq", [L, PAIR, H, S])
        head_var = sb("head_var", [L, PAIR * H])
        nwt2 = sb("nwt2", [L, 4, PAIR * H])
        att_n = sb("att_n", [L, PAIR, H, S])
        att_f = sb("att_f", [128, 2, T])
        ag = sb("ag", [128, 2, T])
        x3 = sb("x3", [L, PAIR, E])
        st2 = sb("st2", [128, PAIR, 6])
        mv2 = sb("mv2", [128, PAIR, 2])
        ve2 = sb("ve2", [128, PAIR])
        rstd2 = sb("rstd2", [128, PAIR])
        xh2 = sb("xh2", [L, PAIR, E])
        xn2 = sb("xn2", [128, 2, PAIR, L + 1])
        sx2 = sb("sx2", [128, 2, PAIR, L])
        xk = sb("xk", [128, 2, T])
        xr = sb("xr", [128, 2, T])
        relu = sb("relu", [128, 2, T])
        kk = sb("kk", [128, 2, T])
        th2 = sb("th2", [L, PAIR, E])
        ffn = sb("ffn", [L, PAIR, E])
        x4 = sb("x4", [L, PAIR, E])

        FB = [ctx.enter_context(nc.psum_tensor(f"front_bank{i}", [128, 512], f32)) for i in range(4)]
        BB = [ctx.enter_context(nc.psum_tensor(f"back_bank{i}", [128, 512], f32)) for i in range(4)]

        def first(g):
            return isinstance(g, int) and g == 0

        def last(g):
            return isinstance(g, int) and g == G - 1

        def slot(u):
            return u if u < UNITS // 2 else u + 1

        BONUS_SLOT = UNITS // 2

        def quarters(bank):
            return bank[:, :].rearrange("p (a b n) -> p a b n", a=2, b=2)

        def halves(bank):
            return bank[:, :].rearrange("p (a n) -> p a n", a=2)

        ATT_LAST = BB[3][:, :].rearrange("p (b h s) -> p b h s", b=PAIR, h=H)

        w_loaded = [sem(f"w{n}_loaded") for n in range(8)]
        attn_w_loaded, v0_loaded, rows_loaded = sem("attn_w_loaded"), sem("v0_loaded"), sem("rows_loaded")
        lora_loaded, more_rows_loaded = sem("lora_loaded"), sem("more_rows_loaded")
        biases_loaded = sem("biases_loaded")
        ident_ready, ident_zero = sem("ident_ready"), sem("ident_zero")
        w_turned, w_ready = sem("w_turned"), sem("w_ready")
        gn_half_ready, prev_cols_ready = sem("gn_half_ready"), sem("prev_cols_ready")
        w_prev_zero = sem("w_prev_zero")
        x_loaded, ctx_loaded = sem("x_loaded"), sem("ctx_loaded")
        state_rows_loaded, s0_loaded = sem("state_rows_loaded"), sem("s0_loaded")
        q_done, k_done, v_done = sem("q_done"), sem("k_done"), sem("v_done")
        qk_ready, vT_ready = sem("qk_ready"), sem("vT_ready")
        scores_done = sem("scores_done")
        max_ready = sem("max_ready")
        exp_ready = sem("exp_ready")
        rcp_ready = sem("rcp_ready")
        prob_ready = sem("prob_ready")
        prob_turned = sem("prob_turned")
        probT_ready = sem("probT_ready")
        rstd1_ready, rstd2_ready = sem("rstd1_ready"), sem("rstd2_ready")
        minus_half_ready = sem("minus_half_ready")
        attn_done = sem("attn_done")
        x2_ready = sem("x2_ready")
        ln1_steps = sem("ln1_steps")
        xh_ready = sem("xh_ready")
        xh_turned = sem("xh_turned")
        xn_ready, prev_ready = sem("xn_ready"), sem("prev_ready")
        sx_ready, xmix_ready = sem("sx_ready"), sem("xmix_ready")
        lora_done, lora_ready = sem("lora_done"), sem("lora_ready")
        mix_done = [sem(f"mix{j}_done") for j in range(MIXES)]
        mixed_ready = [sem(f"mixed{j}_ready") for j in range(MIXES)]
        x5_ready = [sem(f"x5_{j}_ready") for j in range(MIXES)]
        dlora_done, wt_ready = sem("dlora_done"), sem("wt_ready")
        decay_done = sem("decay_done")
        e1_ready, decay_ready = sem("e1_ready"), sem("decay_ready")
        kp_done, kf_ready = sem("kp_done"), sem("kf_ready")
        rp_done, rf_ready = sem("rp_done"), sem("rf_ready")
        vp_done, v_exp_ready, v_tok_ready = sem("vp_done"), sem("v_exp_ready"), sem("v_tok_ready")
        gp_done, gate_th_ready, gate_ready = sem("gp_done"), sem("gate_th_ready"), sem("gate_ready")
        head_ones_ready = sem("head_ones_ready")
        x2_kept, s0_placed = sem("x2_kept"), sem("s0_placed")
        v_spread = sem("v_spread")
        kv_ready, state_ready = sem("kv_ready"), sem("state_ready")
        rs_ready = sem("rs_ready")
        ru_ready, ruk_ready = sem("ru_ready"), sem("ruk_ready")
        rs_turned = sem("rs_turned")
        head_out_ready = sem("head_out_ready")
        cv_ready, att1_ready = sem("cv_ready"), sem("att1_ready")
        att_c_ready, sq_ready = sem("att_c_ready"), sem("sq_ready")
        gn_sum, gn_steps = sem("gn_sum"), sem("gn_steps")
        att_n_ready = sem("att_n_ready")
        att_turned, att_f_ready, ag_ready = sem("att_turned"), sem("att_f_ready"), sem("ag_ready")
        o_done, x3_ready = sem("o_done"), sem("x3_ready")
        ln2_steps, xh2_ready = sem("ln2_steps"), sem("xh2_ready")
        xh2_turned, xn2_ready = sem("xh2_turned"), sem("xn2_ready")
        prev2_ready = sem("prev2_ready")
        sx2_ready, xk_ready, xr_ready = sem("sx2_ready"), sem("xk_ready"), sem("xr_ready")
        fk_done, relu_ready, kk_ready = sem("fk_done"), sem("relu_ready"), sem("kk_ready")
        fr_done, th2_ready = sem("fr_done"), sem("th2_ready")
        fv_done, ffn_ready, x4_ready = sem("fv_done"), sem("ffn_ready"), sem("x4_ready")
        stored = sem("stored")
        RS = 11
        SPREAD = 0.375 ** -4
        LN_STEPS = 2 * PAIR + 1

        BACK_STEPS = (
            (UNITS, (v_spread, kv_ready, state_ready, rs_ready)),
            (1, (rstd2_ready, ru_ready, ruk_ready, cv_ready, att1_ready, att_c_ready,
                sq_ready, gn_sum, att_n_ready, att_turned, ag_ready, o_done, x3_ready,
                xh2_turned, prev2_ready, sx2_ready, fk_done, relu_ready, kk_ready, fr_done,
                th2_ready, fv_done, ffn_ready, x4_ready)),
            (PRODUCTS, (rs_turned, head_out_ready)),
            (RS + 1, (gn_steps,)),
            (2, (s0_placed, att_f_ready, xh2_ready, xn2_ready, xk_ready, xr_ready)),
            (LN_STEPS, (ln2_steps,)),
        )

        block = ctx.enter_context(nc.Block())

        @block.sync
        def _(sp):
            sp.dma_start(attn_nat[:, 0, :], Wq).then_inc(attn_w_loaded, 16)
            sp.dma_start(attn_nat[:, 1, :], Wk).then_inc(attn_w_loaded, 16)
            sp.dma_start(xin[:, :, :], x[0:PAIR, :, :].rearrange("b c n -> c b n")).then_inc(x_loaded, 16)
            sp.dma_start(cin[:, :, :], ctx_2048[0:PAIR, :, :].rearrange("b c n -> c b n")).then_inc(ctx_loaded, 16)
            sp.dma_start(v0_nat[:, :], Wv).then_inc(v0_loaded, 16)
            for n, w in enumerate((Wr, Wkey, Wval, Wg, Wo, ffn_Wk, ffn_Wr, ffn_Wv)):
                if n == 4:
                    for r, vec in ((R_MAAX, maa_x), (R_DECAY, time_decay), (R_GNW, gn_w), (R_GNB, gn_b),
                                   (R_FK, ffn_maa_k), (R_FR, ffn_maa_r)):
                        sp.dma_start(rows[r:r + 1, :], vec.rearrange("(a e) -> a e", a=1)
                                     ).then_inc(more_rows_loaded, 16)
                sp.dma_start(w_nat[:, n, :, :], w.rearrange("(h p) e -> p h e", p=128)).then_inc(w_loaded[n], 16)
            sp.dma_start(mw1[:, :, :], maa_w1.rearrange("(h p) n -> p h n", p=128)).then_inc(lora_loaded, 16)
            sp.dma_start(mw2[:, :], maa_w2[0:4, :, :].rearrange("j i e -> (j i) e")).then_inc(lora_loaded, 16)
            sp.dma_start(mw2_last[:, :], maa_w2[4, :, :]).then_inc(lora_loaded, 16)
            sp.dma_start(dw1[:, :, :], decay_w1.rearrange("(h p) n -> p h n", p=128)).then_inc(lora_loaded, 16)
            sp.dma_start(dw2[:, :], decay_w2).then_inc(lora_loaded, 16)
            sp.dma_start(state_rows[:, :], ctx_2048[:, 0:2, :]).then_inc(state_rows_loaded, 16)
            for b in range(B):
                sp.dma_start(s0[:, :, b, :], ctx_2048[b, 2:2 + S, :].rearrange("(h r) (p s) -> (r p) h s", h=2, s=S)
                             ).then_inc(s0_loaded, 16)

            with sp.Fori(1, G) as g:
                sp.wait_ge(x2_ready, g)
                sp.dma_start(xin[:, :, :], x[bass.ds(PAIR * g, PAIR), :, :].rearrange("b c n -> c b n")
                             ).then_inc(x_loaded, 16)
                sp.wait_ge(v_done, g)
                sp.dma_start(cin[:, :, :], ctx_2048[bass.ds(PAIR * g, PAIR), :, :].rearrange("b c n -> c b n")
                             ).then_inc(ctx_loaded, 16)

        @block.gpsimd
        def _(pool):
            pool.memset(ident[:, :], 0.0).then_inc(ident_zero, 1)
            pool.dma_start(bqk[:, 0:1], bq.rearrange("(d a) -> d a", a=1)).then_inc(biases_loaded, 16)
            pool.dma_start(bqk[:, 1:2], bk.rearrange("(d a) -> d a", a=1)).then_inc(biases_loaded, 16)
            pool.dma_start(bv_col[:, :], bv.rearrange("(d a) -> d a", a=1)).then_inc(biases_loaded, 16)
            pool.wait_ge(ident_zero, 1)
            pool.affine_select(out=ident[:, :], in_=ident[:, :], compare_op=ALU.not_equal, fill=1.0, base=0,
                               pattern=[[-1, 128]], channel_multiplier=1).then_inc(ident_ready, 1)
            pool.memset(w_prev[:, :, :, :, 0], 0.0).then_inc(w_prev_zero, 1)
            for r, vec in ((R_LN1W, ln1_w), (R_LN1B, ln1_b), (R_LN2W, ln2_w), (R_LN2B, ln2_b)):
                pool.dma_start(rows[r:r + 1, :], vec.rearrange("(a e) -> a e", a=1)).then_inc(rows_loaded, 16)
            pool.dma_start(rows[R_U:R_U + 1, :], faaaa.rearrange("h s -> (h s)").rearrange("(a e) -> a e", a=1)
                         ).then_inc(rows_loaded, 16)
            pool.dma_start(rows[R_STACK:ROWS, :], maa_stack).then_inc(rows_loaded, 16)
            pool.memset(minus_half[:, :], -0.5).then_inc(minus_half_ready, 1)
            for per_group, steps in BACK_STEPS:
                for step in steps:
                    pool.nop().then_inc(step, per_group)

            def normalise(g, b):
                pool.wait_ge(rcp_ready, 2 * g + b + 1)
                pool.tensor_tensor(prob[:, b, :, :], prob[:, b, :, :],
                                   prob_rcp[:, b, :].unsqueeze(2).broadcast_to([128, 2, E]), ALU.mult
                                   ).then_inc(prob_ready, 1)

            def root(ve, count, rstd, ready):
                pool.wait_ge(minus_half_ready, 1)
                pool.wait_ge(*count)
                pool.tensor_tensor(rstd[:, :], ve[:, :], minus_half[:, :], ALU.pow).then_inc(ready, 1)

            def root1(g):
                if not first(g):
                    pool.wait_ge(xh_ready, PAIR * g)
                root(ve1, (ln1_steps, LN_STEPS * (g + 1)), rstd1, rstd1_ready)

            def root2(g):
                pool.wait_ge(xh2_ready, PAIR * (g + 1))
                root(ve2, (ln2_steps, LN_STEPS * (g + 2)), rstd2, rstd2_ready)

            def add_xn(g, j):
                pool.wait_ge(mixed_ready[j], 2 * g + 2)
                pool.wait_ge(xn_ready, 2 * g + 2)
                if not first(g):
                    pool.wait_ge([kp_done, dlora_done, vp_done, rp_done, gp_done][j], g)
                pool.tensor_tensor(x5[:, j, :, :].rearrange("p h (b t) -> p h b t", b=PAIR),
                                   mixed[:, j, :, :].rearrange("p h (b t) -> p h b t", b=PAIR),
                                   xn[:, :, :, 1:], ALU.add).then_inc(x5_ready[j], 1)

            def bonus_weight(g):
                pool.wait_ge(rf_ready, 2 * g + 2)
                if not first(g):
                    pool.wait_ge(ruk_ready, g + 1)
                pool.wait_ge(w_ready, 3)
                pool.tensor_tensor(ru[:, :, :], rf[:, :, :, :].rearrange("p h b t -> p h (b t)"),
                                   cols[:, :, R_U:R_U + 1].broadcast_to([128, 2, T]), ALU.mult).then_inc(ru_ready, 1)
                pool.wait_ge(ru_ready, g + 2)
                pool.wait_ge(kf_ready, 2 * g + 2)
                if not first(g):
                    pool.wait_ge(rs_turned, PRODUCTS * g + BONUS_SLOT + 1)
                pool.tensor_tensor(ruk[:, :, :], ru[:, :, :], kf[:, :, :, :].rearrange("p h b t -> p h (b t)"),
                                   ALU.mult).then_inc(ruk_ready, 1)

            def times_r(g, u):
                h = u // 4
                pool.wait_ge(state_ready, UNITS * (g + 1) + u + 1)
                pool.wait_ge(rf_ready, 2 * g + h + 1)
                if u >= 2:
                    pool.wait_ge(rs_turned, PRODUCTS * (g + 1) + slot(u - 2) + 1)
                elif not first(g):
                    pool.wait_ge(rs_turned, PRODUCTS * g + slot(u + UNITS - 2) + 1)
                pool.tensor_tensor(rs[:, u % 2, :, :, :].rearrange("p d b t -> p d (b t)"),
                                   state[:, u % 2, :, :, :].rearrange("p d b t -> p d (b t)"),
                                   rf[:, h, :, :].rearrange("p b t -> p (b t)").unsqueeze(1).broadcast_to([128, 2, T]),
                                   ALU.mult).then_inc(rs_ready, 1)

            def present_v(g):
                pool.wait_ge(head_out_ready, PRODUCTS * (g + 1) + (0 if last(g) else BONUS_SLOT) + 1)
                pool.wait_ge(v_tok_ready, g + 1)
                pool.wait_ge(att1_ready, g + 1)
                pool.tensor_tensor(cv[:, :, :, :], v_tok[:, :, :].rearrange("p b (h s) -> p b h s", s=S),
                                   bonus[:, :, :].unsqueeze(3).broadcast_to([L, PAIR, H, S]), ALU.mult
                                   ).then_inc(cv_ready, 1)

            def body(m, s, a):
                times_r(s, 5)
                add_xn(m, MIX_W)
                add_xn(m, MIX_K)
                add_xn(m, MIX_R)
                times_r(s, 6)
                add_xn(m, MIX_V)
                present_v(s)
                times_r(s, 7)
                normalise(a, 0)
                normalise(a, 1)
                add_xn(m, MIX_G)
                root1(a)
                times_r(m, 0)
                root2(s)
                times_r(m, 1)
                bonus_weight(m)
                times_r(m, 2)
                times_r(m, 3)
                times_r(m, 4)

            normalise(0, 0)
            normalise(0, 1)
            root1(0)
            add_xn(0, MIX_W)
            add_xn(0, MIX_K)
            add_xn(0, MIX_R)
            add_xn(0, MIX_V)
            add_xn(0, MIX_G)
            normalise(1, 0)
            normalise(1, 1)
            root1(1)
            times_r(0, 0)
            times_r(0, 1)
            bonus_weight(0)
            times_r(0, 2)
            times_r(0, 3)
            times_r(0, 4)
            with pool.Fori(1, G - 1) as i:
                body(i, i - 1, i + 1)

            times_r(G - 2, 5)
            add_xn(G - 1, MIX_W)
            add_xn(G - 1, MIX_K)
            add_xn(G - 1, MIX_R)
            add_xn(G - 1, MIX_V)
            times_r(G - 2, 6)
            present_v(G - 2)
            times_r(G - 2, 7)
            add_xn(G - 1, MIX_G)
            times_r(G - 1, 0)
            bonus_weight(G - 1)
            times_r(G - 1, 1)
            times_r(G - 1, 2)
            root2(G - 2)
            times_r(G - 1, 3)
            times_r(G - 1, 4)
            times_r(G - 1, 5)
            times_r(G - 1, 6)
            times_r(G - 1, 7)
            present_v(G - 1)
            root2(G - 1)

        @block.scalar
        def _(act):
            def ready_attn_weights():
                act.wait_ge(w_turned, 1)
                act.activation(attn_T[:, :, :], FB[0][:, 0:2 * D].rearrange("p (a d) -> p a d", a=2), ACT.Copy
                               ).then_inc(w_ready, 1)
                act.wait_ge(w_turned, 2)
                act.activation(v0_T[:, :], FB[3][:, 0:L], ACT.Copy).then_inc(w_ready, 1)

            def ready_rows():
                act.wait_ge(w_turned, 3)
                act.activation(cols[:, :, :], FB[2][:, 0:2 * ROWS].rearrange("p (a r) -> p a r", a=2), ACT.Copy
                               ).then_inc(w_ready, 1)
                act.activation(prev_cols[:, :, :, :],
                               FB[2][:, 128:128 + 4 * B].rearrange("p (h b r) -> p r h b", h=2, r=2), ACT.Copy
                               ).then_inc(prev_cols_ready, 1)
                act.wait_ge(w_ready, 3)
                act.activation(gn_half[:, :, :], cols[:, :, R_GNW:R_GNB + 1], ACT.Copy, scale=0.5
                               ).then_inc(gn_half_ready, 1)

            def ready_weights(lo, hi):
                for n in range(lo, hi):
                    act.wait_ge(w_turned, 4 + n)
                    act.activation(wT[:, n, :, :], halves(BB[n % 4]), ACT.Copy).then_inc(w_ready, 1)

            def attn_in(g):
                act.wait_ge(biases_loaded, 48)
                act.wait_ge(q_done, g + 1)
                if not first(g):
                    act.wait_ge(scores_done, 2 * g)
                act.activation(qk[:, 0, :], FB[0][0:D, :], ACT.Identity, bias=bqk[:, 0:1]).then_inc(qk_ready, 1)
                act.wait_ge(k_done, g + 1)
                act.activation(qk[:, 1, :], FB[1][0:D, :], ACT.Identity, bias=bqk[:, 1:2]).then_inc(qk_ready, 1)
                act.wait_ge(v_done, g + 1)
                if not first(g):
                    act.wait_ge(attn_done, g)
                act.activation(vT[:, :, :, :], quarters(FB[0]), ACT.Copy).then_inc(vT_ready, 1)

            def softmax(g, b):
                act.wait_ge(max_ready, 2 * g + b + 1)
                if not first(g):
                    act.wait_ge(prob_turned, 2 * g)
                bank = FB[1 - b]
                for nt in range(2):
                    act.activation(prob[:, b, nt, :], halves(bank)[:, nt, :], ACT.Exp, bias=neg_max[:, b, nt:nt + 1],
                                   accum_out=prob_sum[:, b, nt:nt + 1]).then_inc(exp_ready, 1)

            def prob_evacuate(g, b):
                act.wait_ge(prob_turned, 2 * g + b + 1)
                if not first(g):
                    act.wait_ge(attn_done, g)
                act.activation(probT[:, b, :, :], halves(FB[1 - b]), ACT.Copy).then_inc(probT_ready, 1)

            def norm_evacuate(g):
                act.wait_ge(w_ready, 3)
                act.wait_ge(xh_turned, g + 1)
                if not first(g):
                    for j in range(MIXES):
                        act.wait_ge(x5_ready[j], g)
                for h in range(2):
                    act.activation(xn[:, h, :, 1:], quarters(FB[0])[:, h, :, :], ACT.Identity,
                                   bias=cols[:, h, R_LN1B:R_LN1B + 1], scale=cols[:, h, R_LN1W:R_LN1W + 1]
                                   ).then_inc(xn_ready, 1)

            def lora_tanh(g):
                act.wait_ge(lora_done, g + 1)
                if not first(g):
                    for j in range(MIXES):
                        act.wait_ge(mix_done[j], g)
                act.activation(lora[:, :], FB[1][:, 0:T], ACT.Tanh).then_inc(lora_ready, 1)
                act.activation(lora_last[:, :], FB[1][0:LORA, T:2 * T], ACT.Tanh).then_inc(lora_ready, 1)

            def decay_tanh(g):
                act.wait_ge(dlora_done, g + 1)
                if not first(g):
                    act.wait_ge(decay_done, g)
                act.activation(wt[:, :], FB[3][0:DECAY, 0:T], ACT.Tanh).then_inc(wt_ready, 1)

            def decay(g):
                act.wait_ge(decay_done, g + 1)
                if not first(g):
                    act.wait_ge(decay_ready, 2 * g)
                for h in range(2):
                    act.activation(e1[:, h, :, :].rearrange("p b t -> p (b t)"), halves(FB[3])[:, h, :], ACT.Exp,
                                   bias=cols[:, h, R_DECAY:R_DECAY + 1]).then_inc(e1_ready, 1)

            def decay_outer(g, h):
                act.wait_ge(e1_ready, 2 * g + h + 1)
                act.wait_ge(w_prev_zero, 1)
                if not first(g):
                    act.wait_ge(state_ready, UNITS * g + UNITS // 2 * (h + 1))
                act.activation(w_prev[:, h, :, :, 1:], e1[:, h, :, 0:L - 1].unsqueeze(1).broadcast_to(
                    [128, 2, PAIR, L - 1]), ACT.Exp, scale=-1.0).then_inc(decay_ready, 1)

            def evacuate_k(g, h):
                act.wait_ge(kp_done, g + 1)
                if not first(g):
                    act.wait_ge(kv_ready, UNITS * g + UNITS // 2 * (h + 1))
                    act.wait_ge(ruk_ready, g + 1)
                act.activation(kf[:, h, :, :], quarters(FB[2])[:, h, :, :], ACT.Copy).then_inc(kf_ready, 1)

            def evacuate_r(g, h):
                act.wait_ge(rp_done, g + 1)
                if not first(g):
                    act.wait_ge(rs_ready, UNITS * g + UNITS // 2 * (h + 1))
                    act.wait_ge(ru_ready, g + 1)
                act.activation(rf[:, h, :, :], quarters(FB[3])[:, h, :, :], ACT.Copy).then_inc(rf_ready, 1)

            def keep_v(g):
                act.wait_ge(vp_done, g + 1)
                if not first(g):
                    act.wait_ge(cv_ready, g + 1)
                    act.wait_ge(v_exp_ready, 2 * PAIR * g)
                act.activation(v_tok[:, :, :], halves(FB[2]), ACT.Copy).then_inc(v_tok_ready, 1)

            def expand_v(g, h):
                act.wait_ge(v_tok_ready, g + 1)
                if not first(g):
                    act.wait_ge(v_spread, UNITS * g + UNITS // 2 * (h + 1))
                for b in range(PAIR):
                    src = v_tok[:, b, 128 * h:128 * h + 128].rearrange("p (n d) -> p d n", d=S)
                    act.activation(v_exp[:, b, h, :, :].rearrange("p d (n k) -> p d n k", k=S),
                                   src.unsqueeze(3).broadcast_to([L, S, HH, S]), ACT.Copy).then_inc(v_exp_ready, 1)

            def gate_tanh(g):
                act.wait_ge(gp_done, g + 1)
                if not first(g):
                    act.wait_ge(gate_ready, g)
                act.activation(gate_th[:, :, :], halves(FB[3]), ACT.Tanh, scale=0.5).then_inc(gate_th_ready, 1)
                act.activation(gate_y[:, :, :], halves(FB[3]), ACT.Copy).then_inc(gate_th_ready, 1)

            def square_heads(g):
                act.wait_ge(att_c_ready, g + 2)
                if not first(g):
                    act.wait_ge(gn_steps, (RS + 1) * (g + 1))
                act.activation(sq[:, :, :, :], att_c[:, :, :, :], ACT.Square).then_inc(sq_ready, 1)

            def att_evacuate(g):
                act.wait_ge(gn_half_ready, 1)
                act.wait_ge(att_turned, g + 2)
                if not first(g):
                    act.wait_ge(ag_ready, g + 1)
                for h in range(2):
                    act.activation(att_f[:, h, :], halves(FB[2])[:, h, :], ACT.Identity,
                                   bias=gn_half[:, h, 1:2], scale=gn_half[:, h, 0:1]).then_inc(att_f_ready, 1)

            def norm2_evacuate(g):
                act.wait_ge(xh2_turned, g + 2)
                if not first(g):
                    act.wait_ge(xk_ready, 2 * (g + 1))
                    act.wait_ge(xr_ready, 2 * (g + 1))
                for h in range(2):
                    act.activation(xn2[:, h, :, 1:], quarters(FB[3])[:, h, :, :], ACT.Identity,
                                   bias=cols[:, h, R_LN2B:R_LN2B + 1], scale=cols[:, h, R_LN2W:R_LN2W + 1]
                                   ).then_inc(xn2_ready, 1)

            def ffn_act(g):
                act.wait_ge(fk_done, g + 2)
                if not first(g):
                    act.wait_ge(kk_ready, g + 1)
                act.activation(relu[:, :, :], halves(FB[2]), ACT.Relu).then_inc(relu_ready, 1)
                act.wait_ge(relu_ready, g + 2)
                if not first(g):
                    act.wait_ge(fv_done, g + 1)
                act.activation(kk[:, :, :], relu[:, :, :], ACT.Square).then_inc(kk_ready, 1)
                act.wait_ge(fr_done, g + 2)
                if not first(g):
                    act.wait_ge(ffn_ready, g + 1)
                act.activation(th2[:, :, :], halves(FB[3]), ACT.Tanh, scale=0.5).then_inc(th2_ready, 1)

            def store(g):
                act.wait_ge(x4_ready, g + 2)
                act.dma_start(out[bass.ds(PAIR * g, PAIR), :, :].rearrange("b c n -> c b n"), x4[:, :, :]
                              ).then_inc(stored, 16)

            def body(m, s, a):
                attn_in(a)
                softmax(a, 0)
                softmax(a, 1)
                keep_v(m)
                expand_v(m, 0)
                decay_tanh(m)
                evacuate_k(m, 0)
                square_heads(s)
                prob_evacuate(a, 0)
                decay(m)
                prob_evacuate(a, 1)
                evacuate_k(m, 1)
                decay_outer(m, 0)
                decay_outer(m, 1)
                gate_tanh(m)
                att_evacuate(s)
                evacuate_r(m, 0)
                norm_evacuate(a)
                expand_v(m, 1)
                evacuate_r(m, 1)
                norm2_evacuate(s)
                lora_tanh(a)
                ffn_act(s)
                store(s)

            ready_attn_weights()
            attn_in(0)
            softmax(0, 0)
            softmax(0, 1)
            ready_rows()
            prob_evacuate(0, 0)
            prob_evacuate(0, 1)
            ready_weights(0, 4)
            norm_evacuate(0)
            ready_weights(4, 8)
            lora_tanh(0)
            attn_in(1)
            softmax(1, 0)
            softmax(1, 1)
            keep_v(0)
            decay_tanh(0)
            prob_evacuate(1, 0)
            expand_v(0, 0)
            decay(0)
            prob_evacuate(1, 1)
            expand_v(0, 1)
            evacuate_k(0, 0)
            decay_outer(0, 0)
            gate_tanh(0)
            evacuate_r(0, 0)
            evacuate_r(0, 1)
            decay_outer(0, 1)
            evacuate_k(0, 1)
            norm_evacuate(1)
            lora_tanh(1)
            with act.Fori(1, G - 1) as i:
                body(i, i - 1, i + 1)

            keep_v(G - 1)
            decay_tanh(G - 1)
            decay(G - 1)
            expand_v(G - 1, 0)
            decay_outer(G - 1, 0)
            square_heads(G - 2)
            gate_tanh(G - 1)
            evacuate_k(G - 1, 0)
            decay_outer(G - 1, 1)
            expand_v(G - 1, 1)
            evacuate_r(G - 1, 0)
            evacuate_r(G - 1, 1)
            evacuate_k(G - 1, 1)
            att_evacuate(G - 2)
            norm2_evacuate(G - 2)
            ffn_act(G - 2)
            store(G - 2)
            square_heads(G - 1)
            att_evacuate(G - 1)
            norm2_evacuate(G - 1)
            ffn_act(G - 1)
            store(G - 1)
            act.wait_ge(stored, 16 * G)

        @block.tensor
        def _(pe):
            def turn(out_, in_, k=128):
                return pe.transpose(out_, in_, ident[0:k, 0:k])

            def turn_attn_weights():
                pe.wait_ge(ident_ready, 1)
                pe.wait_ge(attn_w_loaded, 32)
                for n in range(2):
                    i = turn(FB[0][:, n * D:(n + 1) * D], attn_nat[:, n, :], D)
                i.then_inc(w_turned, 1)
                pe.wait_ge(v0_loaded, 16)
                turn(FB[3][:, 0:L], v0_nat[:, :]).then_inc(w_turned, 1)

            def turn_rows():
                pe.wait_ge(rows_loaded, 16 * 6)
                pe.wait_ge(more_rows_loaded, 16 * 6)
                for h in range(2):
                    turn(FB[2][:, h * ROWS:(h + 1) * ROWS], rows[:, 128 * h:128 * h + 128], ROWS)
                pe.wait_ge(state_rows_loaded, 16)
                for h in range(2):
                    i = turn(FB[2][:, 128 + 2 * B * h:128 + 2 * B * (h + 1)], state_rows[:, 128 * h:128 * h + 128],
                             2 * B)
                i.then_inc(w_turned, 1)

            def turn_weights(lo, hi):
                for n in range(lo, hi):
                    pe.wait_ge(w_loaded[n], 16)
                    if n >= 4:
                        pe.wait_ge(w_ready, n)
                    for h_in in range(2):
                        for h_out in range(2):
                            i = turn(quarters(BB[n % 4])[:, h_in, h_out, :],
                                     w_nat[:, n, h_out, 128 * h_in:128 * h_in + 128])
                    i.then_inc(w_turned, 1)

            def attn_qk(g):
                pe.wait_ge(x_loaded, 16 * (g + 1))
                if first(g):
                    pe.wait_ge(w_ready, 2)
                else:
                    pe.wait_ge(xn_ready, 2 * g)
                pe.matmul(FB[0][0:D, :], attn_T[:, 0, :], xin[:, :, :].rearrange("p b n -> p (b n)"),
                          start=True, stop=True).then_inc(q_done, 1)
                pe.wait_ge(ctx_loaded, 16 * (g + 1))
                if not first(g):
                    pe.wait_ge(lora_ready, 2 * g)
                pe.matmul(FB[1][0:D, :], attn_T[:, 1, :], cin[:, :, :].rearrange("p b n -> p (b n)"),
                          start=True, stop=True).then_inc(k_done, 1)

            def attn_v(g):
                pe.wait_ge(qk_ready, 2 * g + 1)
                for b in range(PAIR):
                    for mt in range(2):
                        i = pe.matmul(quarters(FB[0])[:, b, mt, :], cin[:, b, 128 * mt:128 * mt + 128], v0_T[:, :],
                                      start=True, stop=True)
                i.then_inc(v_done, 1)

            def scores(g):
                pe.wait_ge(qk_ready, 2 * g + 2)
                for b in range(PAIR):
                    bank = FB[1 - b]
                    if b == 1:
                        pe.wait_ge(vT_ready, g + 1)
                    for nt in range(2):
                        i = pe.matmul(halves(bank)[:, nt, :], qk[:, 0, b * E + 128 * nt:b * E + 128 * nt + 128],
                                      qk[:, 1, b * E:(b + 1) * E], start=True, stop=True)
                    i.then_inc(scores_done, 1)

            def prob_turn(g, b):
                pe.wait_ge(prob_ready, 2 * g + b + 1)
                for mt in range(2):
                    for nt in range(2):
                        i = turn(quarters(FB[1 - b])[:, mt, nt, :], prob[:, b, nt, 128 * mt:128 * mt + 128])
                i.then_inc(prob_turned, 1)

            def attn_out(g):
                pe.wait_ge(vT_ready, g + 1)
                for b in range(PAIR):
                    pe.wait_ge(probT_ready, 2 * g + b + 1)
                    for mt in range(2):
                        i = pe.matmul(halves(FB[1])[:, b, :], vT[:, b, mt, :], probT[:, b, mt, :],
                                      start=(mt == 0), stop=(mt == 1))
                i.then_inc(attn_done, 1)

            def norm_turn(g):
                pe.wait_ge(probT_ready, 2 * g + 2)
                for b in range(PAIR):
                    pe.wait_ge(xh_ready, 2 * g + b + 1)
                    for h in range(2):
                        i = turn(quarters(FB[0])[:, h, b, :], xh[:, b, 128 * h:128 * h + 128])
                i.then_inc(xh_turned, 1)

            def lora_in(g):
                pe.wait_ge(lora_loaded, 80)
                pe.wait_ge(xmix_ready, 2 * g + 2)
                pe.wait_ge(x2_ready, g + 1)
                for h in range(2):
                    pe.matmul(FB[1][:, 0:T], mw1[:, h, 0:4 * LORA], xmix[:, h, :], start=(h == 0), stop=(h == 1))
                for h in range(2):
                    i = pe.matmul(FB[1][0:LORA, T:2 * T], mw1[:, h, 4 * LORA:], xmix[:, h, :],
                                  start=(h == 0), stop=(h == 1))
                i.then_inc(lora_done, 1)

            def to_features(bank, w, src, done):
                for h_out in range(2):
                    for h_in in range(2):
                        i = pe.matmul(halves(bank)[:, h_out, :], wT[:, w, h_in, 128 * h_out:128 * h_out + 128],
                                      src[:, h_in, :], start=(h_in == 0), stop=(h_in == 1))
                i.then_inc(done, 1)

            def to_tokens(bank, w, src, done):
                for b in range(PAIR):
                    for h_in in range(2):
                        i = pe.matmul(halves(bank)[:, b, :], src[:, h_in, L * b:L * (b + 1)], wT[:, w, h_in, :],
                                      start=(h_in == 0), stop=(h_in == 1))
                i.then_inc(done, 1)

            MIX_BANK = {MIX_W: FB[2], MIX_K: FB[3], MIX_R: FB[2], MIX_V: FB[3], MIX_G: FB[2]}

            def mix(g, j):
                if j in (MIX_W, MIX_K):
                    pe.wait_ge(w_ready, 3 + 8)
                    pe.wait_ge(lora_ready, 2 * g + 2)
                if j == MIX_W:
                    if not first(g):
                        pe.wait_ge(kf_ready, 2 * g)
                        pe.wait_ge(ffn_ready, g)
                elif j == MIX_K:
                    if not first(g):
                        pe.wait_ge(rf_ready, 2 * g)
                        pe.wait_ge(th2_ready, g)
                else:
                    pe.wait_ge(mixed_ready[{MIX_R: MIX_W, MIX_V: MIX_K, MIX_G: MIX_R}[j]], 2 * g + 2)
                for h in range(2):
                    if j < 4:
                        w2, lo = mw2[LORA * j:LORA * (j + 1), :], lora[LORA * j:LORA * (j + 1), :]
                    else:
                        w2, lo = mw2_last[:, :], lora_last[:, :]
                    i = pe.matmul(halves(MIX_BANK[j])[:, h, :], w2[:, 128 * h:128 * h + 128], lo, start=True, stop=True)
                i.then_inc(mix_done[j], 1)

            def decay_rank(g):
                pe.wait_ge(x5_ready[MIX_W], g + 1)
                pe.wait_ge(mixed_ready[MIX_V], 2 * g + 2)
                for h in range(2):
                    i = pe.matmul(FB[3][0:DECAY, 0:T], dw1[:, h, :], x5[:, MIX_W, h, :], start=(h == 0), stop=(h == 1))
                i.then_inc(dlora_done, 1)

            def decay_out(g):
                pe.wait_ge(wt_ready, g + 1)
                for h in range(2):
                    i = pe.matmul(halves(FB[3])[:, h, :], dw2[:, 128 * h:128 * h + 128], wt[:, :],
                                  start=True, stop=True)
                i.then_inc(decay_done, 1)

            def project_v(g):
                pe.wait_ge(mixed_ready[MIX_G], 2 * g + 2)
                pe.wait_ge(x5_ready[MIX_V], g + 1)
                to_tokens(FB[2], WV, x5[:, MIX_V, :, :], vp_done)

            def project_k(g):
                pe.wait_ge(v_tok_ready, g + 1)
                pe.wait_ge(x5_ready[MIX_K], g + 1)
                to_features(FB[2], WK, x5[:, MIX_K, :, :], kp_done)

            def project_g(g):
                pe.wait_ge(e1_ready, 2 * g + 2)
                pe.wait_ge(x5_ready[MIX_G], g + 1)
                to_features(FB[3], WG, x5[:, MIX_G, :, :], gp_done)

            def project_r(g):
                pe.wait_ge(gate_th_ready, 2 * g + 2)
                pe.wait_ge(x5_ready[MIX_R], g + 1)
                to_features(FB[3], WR, x5[:, MIX_R, :, :], rp_done)

            def spread(g, u):
                if u % (UNITS // 2) == 0:
                    pe.wait_ge(v_exp_ready, 2 * PAIR * g + (PAIR if u == 0 else 2 * PAIR))
                if u >= 2 or not first(g):
                    pe.wait_ge(kv_ready, UNITS * (g + 1) + u - 1)
                h, d0 = u // 4, 2 * (u % 4)
                for d in range(2):
                    for b in range(PAIR):
                        i = turn(quarters(BB[u % 2])[:, d, b, :], v_exp[:, b, h, d0 + d, :])
                i.then_inc(v_spread, 1)

            def turn_bonus(g):
                pe.wait_ge(ruk_ready, g + 2)
                pe.wait_ge(head_out_ready, PRODUCTS * (g + 1) + (0 if last(g) else BONUS_SLOT - 1))
                for b in range(PAIR):
                    for h in range(2):
                        i = turn(quarters(BB[2])[:, b, h, :], ruk[:, h, L * b:L * (b + 1)])
                i.then_inc(rs_turned, 1)

            def turn_rs(g, u):
                pe.wait_ge(rs_ready, UNITS * (g + 1) + u + 1)
                if last(g):
                    if u == 0:
                        pe.wait_ge(head_out_ready, PRODUCTS * (g + 1))
                    h, d0 = u // 4, 2 * (u % 4)
                    for b in range(PAIR):
                        for d in range(2):
                            i = pe.matmul(ATT_LAST[:, b, HH * h:HH * (h + 1), d0 + d], rs[:, u % 2, d, b, :],
                                          head_ones[:, :], start=True, stop=True)
                    i.then_inc(rs_turned, 1)
                    return
                n = slot(u)
                if n >= 2 or not first(g):
                    pe.wait_ge(head_out_ready, PRODUCTS * (g + 1) + n - 1)
                for b in range(PAIR):
                    for d in range(2):
                        i = turn(quarters(BB[2 + n % 2])[:, b, d, :], rs[:, u % 2, d, b, :])
                i.then_inc(rs_turned, 1)

            def att_turn(g):
                pe.wait_ge(att_n_ready, g + 2)
                if last(g):
                    pe.wait_ge(ffn_ready, g + 1)
                else:
                    pe.wait_ge(kf_ready, 2 * (g + 2))
                flat = att_n[:, :, :, :].rearrange("p b h s -> p b (h s)")
                for h in range(2):
                    for b in range(PAIR):
                        i = turn(quarters(FB[2])[:, h, b, :], flat[:, b, 128 * h:128 * h + 128])
                i.then_inc(att_turned, 1)

            def att_project(g):
                pe.wait_ge(ag_ready, g + 2)
                to_tokens(FB[2], WO, ag, o_done)

            def norm2_turn(g):
                if last(g):
                    pe.wait_ge(th2_ready, g + 1)
                else:
                    pe.wait_ge(rf_ready, 2 * (g + 2))
                for b in range(PAIR):
                    pe.wait_ge(xh2_ready, 2 * (g + 1) + b + 1)
                    for h in range(2):
                        i = turn(quarters(FB[3])[:, h, b, :], xh2[:, b, 128 * h:128 * h + 128])
                i.then_inc(xh2_turned, 1)

            def ffn_in(g):
                pe.wait_ge(xk_ready, 2 * (g + 1) + 2)
                pe.wait_ge(x3_ready, g + 2)
                to_features(FB[2], FK, xk, fk_done)
                pe.wait_ge(xr_ready, 2 * (g + 1) + 2)
                pe.wait_ge(xn2_ready, 2 * (g + 1) + 2)
                to_tokens(FB[3], FR, xr, fr_done)

            def ffn_out(g):
                pe.wait_ge(kk_ready, g + 2)
                to_tokens(FB[2], FV, kk, fv_done)

            def body(m, s, a):
                mix(m, MIX_K)
                turn_rs(s, 3)
                mix(m, MIX_W)
                attn_qk(a)
                mix(m, MIX_R)
                mix(m, MIX_V)
                turn_bonus(s)
                mix(m, MIX_G)
                turn_rs(s, 4)
                attn_v(a)
                turn_rs(s, 5)
                scores(a)
                turn_rs(s, 6)
                project_v(m)
                turn_rs(s, 7)
                decay_rank(m)
                project_k(m)
                spread(m, 0)
                prob_turn(a, 0)
                prob_turn(a, 1)
                decay_out(m)
                spread(m, 1)
                attn_out(a)
                project_g(m)
                spread(m, 2)
                att_turn(s)
                spread(m, 3)
                project_r(m)
                norm_turn(a)
                att_project(s)
                lora_in(a)
                norm2_turn(s)
                spread(m, 4)
                spread(m, 5)
                turn_rs(m, 0)
                spread(m, 6)
                turn_rs(m, 1)
                ffn_in(s)
                ffn_out(s)
                turn_rs(m, 2)
                spread(m, 7)

            pe.wait_ge(head_ones_ready, 1)
            turn_attn_weights()
            attn_qk(0)
            attn_v(0)
            scores(0)
            turn_rows()
            prob_turn(0, 0)
            prob_turn(0, 1)
            attn_out(0)
            turn_weights(0, 4)
            norm_turn(0)
            turn_weights(4, 8)
            lora_in(0)
            mix(0, MIX_K)
            mix(0, MIX_W)
            attn_qk(1)
            mix(0, MIX_V)
            mix(0, MIX_R)
            attn_v(1)
            decay_rank(0)
            mix(0, MIX_G)
            scores(1)
            project_v(0)
            prob_turn(1, 0)
            project_k(0)
            decay_out(0)
            spread(0, 0)
            prob_turn(1, 1)
            spread(0, 1)
            attn_out(1)
            project_g(0)
            project_r(0)
            spread(0, 2)
            norm_turn(1)
            spread(0, 3)
            turn_rs(0, 0)
            spread(0, 4)
            turn_rs(0, 1)
            spread(0, 5)
            lora_in(1)
            spread(0, 6)
            spread(0, 7)
            turn_rs(0, 2)
            with pe.Fori(1, G - 1) as i:
                body(i, i - 1, i + 1)

            turn_rs(G - 2, 3)
            mix(G - 1, MIX_W)
            turn_bonus(G - 2)
            mix(G - 1, MIX_K)
            turn_rs(G - 2, 4)
            mix(G - 1, MIX_R)
            mix(G - 1, MIX_V)
            mix(G - 1, MIX_G)
            decay_rank(G - 1)
            project_v(G - 1)
            turn_rs(G - 2, 5)
            decay_out(G - 1)
            turn_rs(G - 2, 6)
            turn_rs(G - 2, 7)
            project_k(G - 1)
            spread(G - 1, 0)
            project_g(G - 1)
            spread(G - 1, 1)
            project_r(G - 1)
            att_turn(G - 2)
            spread(G - 1, 2)
            spread(G - 1, 3)
            att_project(G - 2)
            turn_rs(G - 1, 0)
            spread(G - 1, 4)
            turn_rs(G - 1, 1)
            spread(G - 1, 5)
            spread(G - 1, 6)
            turn_rs(G - 1, 2)
            norm2_turn(G - 2)
            turn_rs(G - 1, 3)
            turn_bonus(G - 1)
            spread(G - 1, 7)
            turn_rs(G - 1, 4)
            ffn_in(G - 2)
            turn_rs(G - 1, 5)
            ffn_out(G - 2)
            turn_rs(G - 1, 6)
            turn_rs(G - 1, 7)
            att_turn(G - 1)
            att_project(G - 1)
            norm2_turn(G - 1)
            ffn_in(G - 1)
            ffn_out(G - 1)

        @block.vector
        def _(dve):
            def root(steps, at, var, scale, buf):
                t, v, y, r = (buf[:, n, :] for n in range(4))
                k = at

                def link(ins):
                    nonlocal k
                    ins.then_inc(steps, 1)
                    k = k + 1
                    dve.wait_ge(steps, k)

                link(dve.tensor_scalar(v, var, SPREAD * scale, SPREAD * EPS, ALU.mult, ALU.add))
                link(dve.tensor_scalar(t.bitcast(i32), v.bitcast(i32), 1, None, ALU.arith_shift_right))
                link(dve.tensor_scalar(y.bitcast(i32), t.bitcast(i32), -1.0, float(RSQRT_MAGIC), ALU.mult, ALU.add))
                link(dve.tensor_tensor(t, v, y, ALU.mult))
                link(dve.tensor_tensor(t, t, y, ALU.mult))
                link(dve.scalar_tensor_tensor(t, t, 10.0 / 3.0, t, ALU.subtract, ALU.mult))
                link(dve.scalar_tensor_tensor(y, t, 5.0, y, ALU.add, ALU.mult))
                link(dve.scalar_tensor_tensor(t, y, 0.375 ** 2, v, ALU.mult, ALU.mult))
                link(dve.tensor_tensor(t, t, y, ALU.mult))
                link(dve.scalar_tensor_tensor(t, t, 10.0 / 3.0, t, ALU.subtract, ALU.mult))
                link(dve.scalar_tensor_tensor(r, t, 5.0, y, ALU.add, ALU.mult))

            def layer_stats(g_at, src, stats, mv, ve, steps):
                at = LN_STEPS * g_at
                for b in range(PAIR):
                    dve.bn_stats(stats[:, b, :], src[:, b, :]).then_inc(steps, 1)
                dve.wait_ge(steps, at + PAIR)
                dve.memset(wait_carrier[:, :], 0.0)
                for b in range(PAIR):
                    dve.bn_aggr(mv[:, b, :], stats[:, b, :]).then_inc(steps, 1)
                dve.wait_ge(steps, at + 2 * PAIR)
                dve.tensor_scalar(ve[:, :], mv[:, :, 1], EPS, None, ALU.add).then_inc(steps, 1)

            def layer_apply(src, mv, rstd, dst, ready):
                for b in range(PAIR):
                    dve.tensor_scalar(dst[:, b, :], src[:, b, :], mv[:, b, 0:1], rstd[:, b:b + 1],
                                      ALU.subtract, ALU.mult).then_inc(ready, 1)

            def row_max(g, b):
                dve.wait_ge(scores_done, 2 * g + b + 1)
                if not first(g):
                    dve.wait_ge(exp_ready, 4 * g)
                dve.tensor_reduce(neg_max[:, b, :], halves(FB[1 - b]), X_AXIS, ALU.max, negate=True
                                  ).then_inc(max_ready, 1)

            def row_rcp(g, b):
                dve.wait_ge(exp_ready, 4 * g + 2 * b + 2)
                if not first(g):
                    dve.wait_ge(prob_ready, 2 * g)
                dve.reciprocal(prob_rcp[:, b, :], prob_sum[:, b, :]).then_inc(rcp_ready, 1)

            def attn_residual(g):
                dve.wait_ge(biases_loaded, 48)
                dve.wait_ge(attn_done, g + 1)
                if not first(g):
                    dve.wait_ge(x2_kept, g)
                    dve.wait_ge(xh_ready, 2 * g)
                dve.scalar_tensor_tensor(x2[:, :, :], halves(FB[1]), bv_col[:, 0:1], xin[:, :, :], ALU.add, ALU.add
                                         ).then_inc(x2_ready, 1)
                dve.wait_ge(x2_ready, g + 1)
                if not first(g):
                    dve.wait_ge(xh_turned, g)
                layer_stats(g, x2, st1, mv1, ve1, ln1_steps)
                dve.tensor_scalar(x2_all[:, bass.ds(PAIR * g, PAIR), :], x2[:, :, :], 1.0, None, ALU.mult
                                  ).then_inc(x2_kept, 1)

            def normed(g):
                dve.wait_ge(rstd1_ready, g + 1)
                layer_apply(x2, mv1, rstd1, xh, xh_ready)

            def shift(g):
                dve.wait_ge(prev_cols_ready, 1)
                if not first(g):
                    dve.wait_ge(sx_ready, g)
                dve.tensor_scalar(xn[:, :, :, 0], prev_cols[:, 1, :, bass.ds(PAIR * g, PAIR)], 1.0, None, ALU.mult
                                  ).then_inc(prev_ready, 1)
                dve.wait_ge(xn_ready, 2 * g + 2)
                dve.wait_ge(prev_ready, g + 1)
                if not first(g):
                    dve.wait_ge(mixed_ready[MIX_G], 2 * g)
                    dve.wait_ge(lora_done, g)
                dve.tensor_tensor(sx[:, :, :, :], xn[:, :, :, 0:L], xn[:, :, :, 1:], ALU.subtract
                                  ).then_inc(sx_ready, 1)
                dve.wait_ge(sx_ready, g + 1)
                for h in range(2):
                    dve.scalar_tensor_tensor(xmix[:, h, :].rearrange("p (b t) -> p b t", b=PAIR), sx[:, h, :, :],
                                             cols[:, h, R_MAAX:R_MAAX + 1], xn[:, h, :, 1:], ALU.mult, ALU.add
                                             ).then_inc(xmix_ready, 1)

            def mixed_(g, j, bank):
                dve.wait_ge(mix_done[j], g + 1)
                if not first(g):
                    dve.wait_ge(x5_ready[j], g)
                for h in range(2):
                    dve.scalar_tensor_tensor(mixed[:, j, h, :], halves(bank)[:, h, :],
                                             cols[:, h, R_STACK + j:R_STACK + j + 1],
                                             sx[:, h, :, :].rearrange("p b t -> p (b t)"), ALU.add, ALU.mult
                                             ).then_inc(mixed_ready[j], 1)

            def gate_(g):
                dve.wait_ge(gate_th_ready, 2 * g + 2)
                if not first(g):
                    dve.wait_ge(ag_ready, g + 1)
                dve.scalar_tensor_tensor(gate[:, :, :], gate_th[:, :, :], 1.0, gate_y[:, :, :], ALU.add, ALU.mult
                                         ).then_inc(gate_ready, 1)

            def scan_start(g, h):
                dve.wait_ge(s0_loaded, 16 * B)
                if not first(g):
                    dve.wait_ge(state_ready, UNITS * g + UNITS // 2 * (h + 1))
                dve.tensor_scalar(kv[:, h, :, :, 0], s0[:, h, bass.ds(PAIR * g, PAIR), :].rearrange("p b d -> p d b"),
                                  1.0, None, ALU.mult).then_inc(s0_placed, 1)

            def scan_kv(g, u):
                h, d0 = u // 4, 2 * (u % 4)
                dve.wait_ge(v_spread, UNITS * (g + 1) + u + 1)
                if d0 == 0:
                    dve.wait_ge(kf_ready, 2 * g + h + 1)
                    dve.wait_ge(s0_placed, 2 * (g + 1) + h + 1)
                dve.tensor_tensor(kv[:, h, d0:d0 + 2, :, 1:], quarters(BB[u % 2])[:, :, :, 0:L - 1],
                                  kf[:, h, :, 0:L - 1].unsqueeze(1).broadcast_to([128, 2, PAIR, L - 1]), ALU.mult
                                  ).then_inc(kv_ready, 1)

            def scan_state(g, u):
                h, d0 = u // 4, 2 * (u % 4)
                dve.wait_ge(kv_ready, UNITS * (g + 1) + u + 1)
                if d0 == 0:
                    dve.wait_ge(decay_ready, 2 * g + h + 1)
                if u >= 2:
                    dve.wait_ge(rs_ready, UNITS * (g + 1) + u - 1)
                elif not first(g):
                    dve.wait_ge(rs_ready, UNITS * (g + 1) + u - 1)
                dve.tensor_tensor_scan(state[:, u % 2, :, :, :].rearrange("p d b t -> p (d b t)"),
                                       w_prev[:, h, :, :, :].rearrange("p d b t -> p (d b t)"),
                                       kv[:, h, d0:d0 + 2, :, :].rearrange("p d b t -> p (d b t)"),
                                       0.0, ALU.mult, ALU.add).then_inc(state_ready, 1)

            def scan_out(g, u):
                if last(g):
                    return
                h, d0 = u // 4, 2 * (u % 4)
                dve.wait_ge(rs_turned, PRODUCTS * (g + 1) + slot(u) + 1)
                if u == 0 and not first(g):
                    dve.wait_ge(att1_ready, g + 1)
                    dve.wait_ge(gn_sum, g + 1)
                dve.tensor_reduce(att[:, :, HH * h:HH * (h + 1), d0:d0 + 2].rearrange("p b h d -> p b d h"),
                                  quarters(BB[2 + slot(u) % 2]).rearrange("p b d (h k) -> p b d h k", k=S),
                                  X_AXIS, ALU.add).then_inc(head_out_ready, 1)

            def bonus_out(g):
                dve.wait_ge(rs_turned, PRODUCTS * (g + 1) + BONUS_SLOT + 1)
                if not first(g):
                    dve.wait_ge(cv_ready, g + 1)
                dve.tensor_reduce(bonus[:, :, :].rearrange("p b (a h) -> p b a h", a=2),
                                  quarters(BB[2]).rearrange("p b a (h k) -> p b a h k", k=S),
                                  X_AXIS, ALU.add).then_inc(head_out_ready, 1)

            def head_mean(g):
                dve.wait_ge(cv_ready, g + 2)
                if last(g):
                    dve.wait_ge(rs_turned, PRODUCTS * (g + 2))
                else:
                    dve.wait_ge(head_out_ready, PRODUCTS * (g + 2))
                dve.wait_ge(att_c_ready, g + 1)
                dve.tensor_tensor(att1[:, :, :, :], ATT_LAST if last(g) else att[:, :, :, :], cv[:, :, :, :], ALU.add
                                  ).then_inc(att1_ready, 1)
                dve.wait_ge(att1_ready, g + 2)
                dve.tensor_reduce(head_sum[:, :], att1[:, :, :, :].rearrange("p b h s -> p (b h) s"), X_AXIS,
                                  ALU.add).then_inc(gn_sum, 1)
                dve.wait_ge(gn_sum, g + 2)
                dve.wait_ge(att_n_ready, g + 1)
                dve.scalar_tensor_tensor(att_c[:, :, :, :].rearrange("p b h s -> p (b h) s"),
                                  head_sum[:, :].unsqueeze(2).broadcast_to([L, PAIR * H, S]), -1.0 / S,
                                  att1[:, :, :, :].rearrange("p b h s -> p (b h) s"), ALU.mult, ALU.add
                                  ).then_inc(att_c_ready, 1)

            def head_norm(g):
                dve.wait_ge(sq_ready, g + 2)
                dve.tensor_reduce(head_var[:, :], sq[:, :, :, :].rearrange("p b h s -> p (b h) s"), X_AXIS,
                                  ALU.add).then_inc(gn_steps, 1)
                at = (RS + 1) * (g + 1) + 1
                dve.wait_ge(gn_steps, at)
                root(gn_steps, at, head_var[:, :], 1.0 / S, nwt2)
                dve.wait_ge(att_turned, g + 1)
                dve.tensor_tensor(att_n[:, :, :, :].rearrange("p b h s -> p (b h) s"),
                                  att_c[:, :, :, :].rearrange("p b h s -> p (b h) s"),
                                  nwt2[:, 3, :].unsqueeze(2).broadcast_to([L, PAIR * H, S]), ALU.mult
                                  ).then_inc(att_n_ready, 1)

            def gated(g):
                dve.wait_ge(att_f_ready, 2 * (g + 2))
                dve.wait_ge(gate_ready, g + 1)
                dve.wait_ge(o_done, g + 1)
                dve.tensor_tensor(ag[:, :, :], att_f[:, :, :], gate[:, :, :], ALU.mult).then_inc(ag_ready, 1)

            def residual(g):
                dve.wait_ge(o_done, g + 2)
                dve.wait_ge(x2_kept, g + 1)
                if not first(g):
                    dve.wait_ge(x4_ready, g + 1)
                dve.tensor_tensor(x3[:, :, :], halves(FB[2]), x2_all[:, bass.ds(PAIR * g, PAIR), :], ALU.add
                                  ).then_inc(x3_ready, 1)
                dve.wait_ge(x3_ready, g + 2)
                if not first(g):
                    dve.wait_ge(xh2_turned, g + 1)
                layer_stats(g + 1, x3, st2, mv2, ve2, ln2_steps)

            def normed2(g):
                dve.wait_ge(rstd2_ready, g + 2)
                layer_apply(x3, mv2, rstd2, xh2, xh2_ready)

            def shift2(g):
                if not first(g):
                    dve.wait_ge(sx2_ready, g + 1)
                dve.tensor_scalar(xn2[:, :, :, 0], prev_cols[:, 0, :, bass.ds(PAIR * g, PAIR)], 1.0, None, ALU.mult
                                  ).then_inc(prev2_ready, 1)
                dve.wait_ge(xn2_ready, 2 * (g + 1) + 2)
                dve.wait_ge(prev2_ready, g + 2)
                if not first(g):
                    dve.wait_ge(xk_ready, 2 * (g + 1))
                    dve.wait_ge(xr_ready, 2 * (g + 1))
                    dve.wait_ge(fk_done, g + 1)
                    dve.wait_ge(fr_done, g + 1)
                dve.tensor_tensor(sx2[:, :, :, :], xn2[:, :, :, 0:L], xn2[:, :, :, 1:], ALU.subtract
                                  ).then_inc(sx2_ready, 1)
                dve.wait_ge(sx2_ready, g + 2)
                for row, dst, ready in ((R_FK, xk, xk_ready), (R_FR, xr, xr_ready)):
                    for h in range(2):
                        dve.scalar_tensor_tensor(dst[:, h, :].rearrange("p (b t) -> p b t", b=PAIR), sx2[:, h, :, :],
                                                 cols[:, h, row:row + 1], xn2[:, h, :, 1:], ALU.mult, ALU.add
                                                 ).then_inc(ready, 1)

            def ffn_out(g):
                dve.wait_ge(fv_done, g + 2)
                dve.wait_ge(th2_ready, g + 2)
                if not first(g):
                    dve.wait_ge(x4_ready, g + 1)
                dve.scalar_tensor_tensor(ffn[:, :, :], th2[:, :, :], 1.0, halves(FB[2]), ALU.add, ALU.mult
                                         ).then_inc(ffn_ready, 1)
                dve.wait_ge(ffn_ready, g + 2)
                if not first(g):
                    dve.wait_ge(stored, 16 * g)
                dve.scalar_tensor_tensor(x4[:, :, :], ffn[:, :, :], 0.5, x3[:, :, :], ALU.mult, ALU.add
                                         ).then_inc(x4_ready, 1)

            def body(m, s, a):
                scan_out(s, 2)
                scan_out(s, 3)
                mixed_(m, MIX_W, FB[2])
                scan_start(m, 0)
                mixed_(m, MIX_K, FB[3])
                scan_kv(s, 7)
                mixed_(m, MIX_R, FB[2])
                mixed_(m, MIX_V, FB[3])
                scan_state(s, 6)
                bonus_out(s)
                scan_out(s, 4)
                scan_state(s, 7)
                mixed_(m, MIX_G, FB[2])
                row_max(a, 0)
                scan_out(s, 5)
                row_max(a, 1)
                row_rcp(a, 0)
                scan_out(s, 6)
                row_rcp(a, 1)
                scan_out(s, 7)
                scan_start(m, 1)
                head_mean(s)
                scan_kv(m, 0)
                head_norm(s)
                scan_kv(m, 1)
                attn_residual(a)
                scan_state(m, 0)
                normed(a)
                gated(s)
                scan_kv(m, 2)
                shift(a)
                residual(s)
                scan_kv(m, 3)
                normed2(s)
                gate_(m)
                scan_state(m, 1)
                scan_kv(m, 4)
                shift2(s)
                scan_state(m, 2)
                scan_kv(m, 5)
                scan_state(m, 3)
                scan_out(m, 0)
                scan_state(m, 4)
                scan_out(m, 1)
                scan_state(m, 5)
                scan_kv(m, 6)
                ffn_out(s)

            dve.wait_ge(ident_ready, 1)
            dve.tensor_reduce(head_ones[:, :], ident[:, :].rearrange("p (h k) -> p h k", k=S), X_AXIS, ALU.add
                              ).then_inc(head_ones_ready, 1)
            row_max(0, 0)
            row_max(0, 1)
            row_rcp(0, 0)
            row_rcp(0, 1)
            attn_residual(0)
            normed(0)
            scan_start(0, 0)
            shift(0)
            mixed_(0, MIX_K, FB[3])
            mixed_(0, MIX_W, FB[2])
            mixed_(0, MIX_V, FB[3])
            mixed_(0, MIX_R, FB[2])
            mixed_(0, MIX_G, FB[2])
            row_max(1, 0)
            row_max(1, 1)
            row_rcp(1, 0)
            row_rcp(1, 1)
            scan_start(0, 1)
            attn_residual(1)
            scan_kv(0, 0)
            scan_kv(0, 1)
            gate_(0)
            scan_state(0, 0)
            normed(1)
            scan_kv(0, 2)
            scan_state(0, 1)
            scan_state(0, 2)
            scan_kv(0, 3)
            shift(1)
            scan_kv(0, 4)
            scan_out(0, 0)
            scan_kv(0, 5)
            scan_state(0, 3)
            scan_state(0, 4)
            scan_kv(0, 6)
            scan_out(0, 1)
            scan_state(0, 5)
            with dve.Fori(1, G - 1) as i:
                body(i, i - 1, i + 1)

            scan_out(G - 2, 2)
            scan_out(G - 2, 3)
            scan_start(G - 1, 0)
            mixed_(G - 1, MIX_W, FB[2])
            mixed_(G - 1, MIX_K, FB[3])
            scan_state(G - 2, 6)
            mixed_(G - 1, MIX_R, FB[2])
            mixed_(G - 1, MIX_V, FB[3])
            mixed_(G - 1, MIX_G, FB[2])
            bonus_out(G - 2)
            scan_kv(G - 2, 7)
            scan_out(G - 2, 4)
            scan_state(G - 2, 7)
            scan_out(G - 2, 5)
            scan_out(G - 2, 6)
            scan_out(G - 2, 7)
            head_mean(G - 2)
            head_norm(G - 2)
            scan_kv(G - 1, 0)
            scan_state(G - 1, 0)
            scan_kv(G - 1, 1)
            scan_kv(G - 1, 2)
            scan_start(G - 1, 1)
            gated(G - 2)
            scan_out(G - 1, 0)
            scan_state(G - 1, 1)
            scan_state(G - 1, 2)
            scan_out(G - 1, 1)
            scan_kv(G - 1, 3)
            residual(G - 2)
            scan_out(G - 1, 2)
            scan_kv(G - 1, 4)
            scan_state(G - 1, 3)
            normed2(G - 2)
            scan_state(G - 1, 4)
            scan_kv(G - 1, 5)
            shift2(G - 2)
            scan_out(G - 1, 3)
            scan_kv(G - 1, 6)
            scan_state(G - 1, 5)
            scan_state(G - 1, 6)
            bonus_out(G - 1)
            scan_out(G - 1, 4)
            scan_kv(G - 1, 7)
            gate_(G - 1)
            scan_state(G - 1, 7)
            ffn_out(G - 2)
            head_mean(G - 1)
            scan_out(G - 1, 5)
            head_norm(G - 1)
            gated(G - 1)
            residual(G - 1)
            scan_out(G - 1, 6)
            normed2(G - 1)
            shift2(G - 1)
            ffn_out(G - 1)
            scan_out(G - 1, 7)


_INS = ["x", "ctx_2048", "L0_xattn_Wq", "L0_xattn_bq", "L0_xattn_Wk", "L0_xattn_bk", "L0_xattn_Wv", "L0_xattn_bv",
        "L1_xattn_ln1_w", "L1_xattn_ln1_b", "L1_xattn_ln2_w", "L1_xattn_ln2_b", "L1_xattn_maa_x",
        "L1_xattn_maa_w1", "L1_xattn_maa_w2", "L1_xattn_maa_stack", "L1_xattn_time_decay", "L1_xattn_decay_w1",
        "L1_xattn_decay_w2", "L1_xattn_faaaa", "L1_xattn_Wr", "L1_xattn_Wk", "L1_xattn_Wv", "L1_xattn_Wg",
        "L1_xattn_Wo", "L1_xattn_gn_w", "L1_xattn_gn_b", "L1_xattn_ffn_maa_k", "L1_xattn_ffn_maa_r",
        "L1_xattn_ffn_Wk", "L1_xattn_ffn_Wr", "L1_xattn_ffn_Wv"]


def kernel(**inputs):
    import numpy as _np
    import concourse.bacc as _bacc
    from concourse import mybir as _mybir
    from concourse.bass_utils import run_bass_kernel_spmd as _run

    nc = _bacc.Bacc("TRN2", target_bir_lowering=False, num_devices=1)
    arrays, args = {}, []
    for name in _INS:
        a = _np.ascontiguousarray(inputs[name])
        arrays[f"in_{name}"] = a
        args.append(nc.dram_tensor(f"in_{name}", a.shape, _mybir.dt.from_np(a.dtype), kind="ExternalInput").ap())
    args.append(nc.dram_tensor("out_0", inputs["x"].shape, _mybir.dt.float32, kind="ExternalOutput").ap())
    xattn_rwkv(nc, *args)
    r = _run(nc, [arrays], core_ids=[0])
    return r.results[0]["out_0"]
```
